# Optimizing a Trainium2 kernel written in Bass

```python
import numpy as np
import jax
import jax.numpy as jnp

def _softmax(x, axis=-1):
    return jax.nn.softmax(x, axis=axis)

def _gelu(x):
    return jax.nn.gelu(x, approximate=True)

def _silu(x):
    return jax.nn.silu(x)

def _sigmoid(x):
    return jax.nn.sigmoid(x)

def _layernorm(x, axis=-1, eps=1e-05):
    m = jnp.mean(x, axis=axis, keepdims=True)
    v = jnp.var(x, axis=axis, keepdims=True)
    return (x - m) / jnp.sqrt(v + eps)

def _scatter_add(tgt, idx, src, axis=0):
    return tgt.at[idx].add(src)

def _segment_sum(src, seg, n):
    return jax.ops.segment_sum(src, seg, n)
kernel_name = 'mk_adaln_d1_jaxref_r4_588139'

def setup_inputs(seed: int=0):
    np.random.seed(seed)
    _w = jnp.asarray

    def _L0_attn_setup():
        import jax, jax.numpy as jnp
        import numpy as np
        from jax import lax
        B, T, D, H, CS = (4, 1024, 512, 16, 64)
        DK = D // H

        def apply_rope(x):
            t, d = (x.shape[-2], x.shape[-1])
            inv_freq = 1.0 / 10000.0 ** (jnp.arange(0, d, 2, dtype=jnp.float32) / d)
            pos = jnp.arange(t, dtype=jnp.float32)
            sinusoid = pos[:, None] * inv_freq[None, :]
            sin, cos = (jnp.sin(sinusoid), jnp.cos(sinusoid))
            x1, x2 = (x[..., ::2], x[..., 1::2])
            out = jnp.stack([x1 * cos - x2 * sin, x1 * sin + x2 * cos], axis=-1)
            return out.reshape(x.shape)
        key = jax.random.key(seed)
        ks = jax.random.split(key, 6)
        s = 0.02
        return {'x': jax.random.normal(ks[0], (B, T, D), dtype=jnp.float32), 'Wq': jax.random.normal(ks[1], (D, D), dtype=jnp.float32) * s, 'bq': jnp.zeros((D,), jnp.float32), 'Wk': jax.random.normal(ks[2], (D, D), dtype=jnp.float32) * s, 'bk': jnp.zeros((D,), jnp.float32), 'Wv': jax.random.normal(ks[3], (D, D), dtype=jnp.float32) * s, 'bv': jnp.zeros((D,), jnp.float32), 'Wg': jax.random.normal(ks[4], (D, D), dtype=jnp.float32) * s, 'bg': jnp.zeros((D,), jnp.float32), 'Wo': jax.random.normal(ks[5], (D, D), dtype=jnp.float32) * s, 'bo': jnp.zeros((D,), jnp.float32)}
    _L0_attn_in = _L0_attn_setup()

    def _L0_ffn_setup():
        import jax, jax.numpy as jnp
        import numpy as np
        B, S, H = (1, 256, 512)
        E, K = (32, 4)
        F, FS = (352, 1408)
        CAP = 64

        def silu(x):
            return x * jax.nn.sigmoid(x)
        key = jax.random.key(seed)
        ks = jax.random.split(key, 9)
        sc = 0.02
        return {'hidden_states': jax.random.normal(ks[0], (B, S, H), jnp.float32), 'Wr': jax.random.normal(ks[1], (H, E), jnp.float32) * sc, 'Wg': jax.random.normal(ks[2], (E, H, F), jnp.float32) * sc, 'Wu': jax.random.normal(ks[3], (E, H, F), jnp.float32) * sc, 'Wd': jax.random.normal(ks[4], (E, F, H), jnp.float32) * sc, 'Wsg': jax.random.normal(ks[5], (H, FS), jnp.float32) * sc, 'Wsu': jax.random.normal(ks[6], (H, FS), jnp.float32) * sc, 'Wsd': jax.random.normal(ks[7], (FS, H), jnp.float32) * sc, 'Wse': jax.random.normal(ks[8], (H, 1), jnp.float32) * sc}
    _L0_ffn_in = _L0_ffn_setup()
    _L0_c = _w((lambda *s: np.random.randn(*s).astype(np.float32) * 0.05)(2, 512))
    _L0_wmod = _w((lambda *s: np.random.randn(*s).astype(np.float32) * 0.05)(512, 6 * 512) * 512 ** (-0.5))
    _d = {'L0_attn_x': _L0_attn_in['x'], 'L0_attn_Wq': _L0_attn_in['Wq'], 'L0_attn_bq': _L0_attn_in['bq'], 'L0_attn_Wk': _L0_attn_in['Wk'], 'L0_attn_bk': _L0_attn_in['bk'], 'L0_attn_Wv': _L0_attn_in['Wv'], 'L0_attn_bv': _L0_attn_in['bv'], 'L0_attn_Wg': _L0_attn_in['Wg'], 'L0_attn_bg': _L0_attn_in['bg'], 'L0_attn_Wo': _L0_attn_in['Wo'], 'L0_attn_bo': _L0_attn_in['bo'], 'L0_ffn_Wr': _L0_ffn_in['Wr'], 'L0_ffn_Wg': _L0_ffn_in['Wg'], 'L0_ffn_Wu': _L0_ffn_in['Wu'], 'L0_ffn_Wd': _L0_ffn_in['Wd'], 'L0_ffn_Wsg': _L0_ffn_in['Wsg'], 'L0_ffn_Wsu': _L0_ffn_in['Wsu'], 'L0_ffn_Wsd': _L0_ffn_in['Wsd'], 'L0_ffn_Wse': _L0_ffn_in['Wse'], 'L0_c': _L0_c, 'L0_wmod': _L0_wmod}
    _x0 = _d['L0_attn_x']
    _d['L0_attn_x'] = jax.random.normal(jax.random.fold_in(jax.random.key(seed), 1), (2, 1024, 512), dtype=_x0.dtype)
    del _x0
    return _d

def reference(L0_attn_x, L0_attn_Wq, L0_attn_bq, L0_attn_Wk, L0_attn_bk, L0_attn_Wv, L0_attn_bv, L0_attn_Wg, L0_attn_bg, L0_attn_Wo, L0_attn_bo, L0_ffn_Wr, L0_ffn_Wg, L0_ffn_Wu, L0_ffn_Wd, L0_ffn_Wsg, L0_ffn_Wsu, L0_ffn_Wsd, L0_ffn_Wse, L0_c, L0_wmod):

    def _L0_attn_ref(x, Wq, bq, Wk, bk, Wv, bv, Wg, bg, Wo, bo):
        import jax, jax.numpy as jnp
        import numpy as np
        from jax import lax
        B, T, D, H, CS = (4, 1024, 512, 16, 64)
        DK = D // H

        def apply_rope(x):
            t, d = (x.shape[-2], x.shape[-1])
            inv_freq = 1.0 / 10000.0 ** (jnp.arange(0, d, 2, dtype=jnp.float32) / d)
            pos = jnp.arange(t, dtype=jnp.float32)
            sinusoid = pos[:, None] * inv_freq[None, :]
            sin, cos = (jnp.sin(sinusoid), jnp.cos(sinusoid))
            x1, x2 = (x[..., ::2], x[..., 1::2])
            out = jnp.stack([x1 * cos - x2 * sin, x1 * sin + x2 * cos], axis=-1)
            return out.reshape(x.shape)
        b, t, c = x.shape
        h, dk, cs = (H, DK, CS)
        nc = t // cs

        def heads(y):
            return y.reshape(b, t, h, dk).transpose(0, 2, 1, 3)
        q = heads(x @ Wq.T + bq)
        k = heads(x @ Wk.T + bk)
        v = heads(x @ Wv.T + bv)
        g = jax.nn.sigmoid(heads(x @ Wg.T + bg))
        q = jax.nn.elu(apply_rope(q)) + 1.0
        k = jax.nn.elu(apply_rope(k)) + 1.0

        def chunked(y):
            return y.reshape(b, h, nc, cs, dk).transpose(2, 0, 1, 3, 4)
        qc, kc, vc, gc = (chunked(q), chunked(k), chunked(v), chunked(g))
        S0 = jnp.zeros((b, h, dk, dk), x.dtype)
        Z0 = jnp.zeros((b, h, dk), x.dtype)

        def step(carry, inp):
            S, Z = carry
            qi, ki, vi, gi = inp
            S = S + jnp.einsum('bhtd,bhte->bhde', ki, vi)
            Z = Z + ki.sum(axis=2)
            num = jnp.einsum('bhtd,bhde->bhte', qi, S)
            den = jnp.einsum('bhtd,bhd->bht', qi, Z)[..., None] + 1e-06
            return ((S, Z), gi * num / den)
        _, out = lax.scan(step, (S0, Z0), (qc, kc, vc, gc))
        out = out.transpose(1, 2, 0, 3, 4).reshape(b, h, t, dk)
        out = out.transpose(0, 2, 1, 3).reshape(b, t, c)
        return out @ Wo.T + bo

    def _L0_ffn_ref(hidden_states, Wr, Wg, Wu, Wd, Wsg, Wsu, Wsd, Wse):
        import jax, jax.numpy as jnp
        import numpy as np
        B, S, H = (1, 256, 512)
        E, K = (32, 4)
        F, FS = (352, 1408)
        CAP = 64

        def silu(x):
            return x * jax.nn.sigmoid(x)
        b, s_len, h = hidden_states.shape
        x = hidden_states.reshape(-1, h)
        T = x.shape[0]
        probs = jax.nn.softmax(x @ Wr, axis=-1)
        topw, topi = jax.lax.top_k(probs, K)
        topw = topw / jnp.sum(topw, axis=-1, keepdims=True)
        shared = silu(x @ Wsg) * (x @ Wsu) @ Wsd
        shared = shared * jax.nn.sigmoid(x @ Wse)
        sel = topi.reshape(-1)
        w = topw.reshape(-1)
        tok = jnp.repeat(jnp.arange(T), K)
        oh = jax.nn.one_hot(sel, E, dtype=jnp.int32)
        pos = (jnp.cumsum(oh, axis=0) * oh).sum(-1) - 1
        valid = (pos < CAP).astype(x.dtype)
        posc = jnp.clip(pos, 0, CAP - 1)
        xe = jnp.zeros((E, CAP, h), x.dtype).at[sel, posc].add(x[tok] * valid[:, None])
        g = silu(jnp.einsum('ech,ehf->ecf', xe, Wg))
        u = jnp.einsum('ech,ehf->ecf', xe, Wu)
        ye = jnp.einsum('ecf,efh->ech', g * u, Wd)
        y_pair = ye[sel, posc] * (w * valid)[:, None]
        out = shared.at[tok].add(y_pair)
        return out.reshape(b, s_len, h)
    x = L0_attn_x
    mod = (_silu(L0_c) @ L0_wmod).reshape(L0_c.shape[0], 6, 1, -1)
    sa, ca, ga, sb, cb, gb = (mod[:, 0], mod[:, 1], mod[:, 2], mod[:, 3], mod[:, 4], mod[:, 5])
    ga = (2 * (ga >= 0) - 1) * jnp.maximum(jnp.abs(ga), 0.25)
    gb = (2 * (gb >= 0) - 1) * jnp.maximum(jnp.abs(gb), 0.25)
    h = _layernorm(x, axis=-1) * (1 + ca) + sa
    x = x + ga * _L0_attn_ref(h, L0_attn_Wq, L0_attn_bq, L0_attn_Wk, L0_attn_bk, L0_attn_Wv, L0_attn_bv, L0_attn_Wg, L0_attn_bg, L0_attn_Wo, L0_attn_bo)
    h = _layernorm(x, axis=-1) * (1 + cb) + sb
    x = x + gb * _L0_ffn_ref(h, L0_ffn_Wr, L0_ffn_Wg, L0_ffn_Wu, L0_ffn_Wd, L0_ffn_Wsg, L0_ffn_Wsu, L0_ffn_Wsd, L0_ffn_Wse)
    return x

_drawn_inputs = setup_inputs


def setup_inputs(seed=0):
    import zlib

    import numpy as np

    out = dict(_drawn_inputs(seed))
    spreads = {'L0_attn_bq': (0.0, 0.8),
     'L0_attn_bk': (0.0, 0.8),
     'L0_attn_bv': (0.0, 0.8),
     'L0_attn_bg': (0.0, 0.8),
     'L0_attn_bo': (0.0, 0.33)}
    factors = {'L0_attn_Wq': 8.0,
     'L0_attn_Wk': 8.0,
     'L0_attn_Wv': 8.0,
     'L0_attn_Wg': 8.0,
     'L0_attn_Wo': 8.0,
     'L0_ffn_Wr': 8.0,
     'L0_ffn_Wg': 8.0,
     'L0_ffn_Wu': 8.0,
     'L0_ffn_Wd': 8.0,
     'L0_ffn_Wsg': 5.527,
     'L0_ffn_Wsu': 5.409,
     'L0_ffn_Wsd': 5.407,
     'L0_ffn_Wse': 8.0}
    for name, (base, spread) in spreads.items():
        noise = np.random.default_rng([zlib.crc32(name.encode()), seed]).standard_normal(out[name].shape)
        drawn = base * np.exp(spread * noise) if base else spread * noise
        out[name] = jnp.asarray(drawn.astype(out[name].dtype))
    for name, factor in factors.items():
        out[name] = (out[name] * factor).astype(out[name].dtype)
    return out
```

```python
import concourse.bass as bass
from concourse import mybir
from contextlib import ExitStack

F32 = mybir.dt.float32
F32R = mybir.dt.float32r
BF16 = mybir.dt.bfloat16
F16 = mybir.dt.float16
I32 = mybir.dt.int32
U32 = mybir.dt.uint32
ALU = mybir.AluOpType
ACT = mybir.ActivationFunctionType

P = 128
B, T, D = 2, 1024, 512
H, DK = 16, 32
CS = 64
KC = D // P
TPB = T // P
NT = B * TPB
HG = P // DK
NG = H // HG
SW = P + HG
LN_EPS = 1e-5
DEN_EPS = 1e-6
E, TOPK, CAP = 32, 4, 64
RW = E + 2
F, FS = 352, 1408


def raw(ap):
    return ap.bitcast(F32)


def lag(j, b, d):
    return j + (b - d) // 2, (b - d) % 2


def real(j, b, d):
    return not isinstance(j, int) or 0 <= 2 * j + b - d < NT


def done(j, b, d=0, per=1, k=None):
    return per * (2 * j + b - d) + (per if k is None else k)


def wait_tile(eng, sem, j, b, d=0, per=1, k=None):
    if real(j, b, d):
        value = done(j, b, d, per, k)
        if not (isinstance(value, int) and value <= 0):
            eng.wait_ge(sem, value)


STATIC_HEAD = [(-1, 0), (-1, 1), (0, 0), (0, 1), (1, 0), (1, 1)]
LOOP_J = (2, 7)
STATIC_TAIL = [(7, 0), (7, 1), (8, 0), (8, 1), (9, 0)]


def run_steps(eng, step):
    for j, b in STATIC_HEAD:
        step(j, b)
    with eng.Fori(*LOOP_J) as j:
        step(j, 0)
        step(j, 1)
    for j, b in STATIC_TAIL:
        step(j, b)


def attention(nc, io, scr):
    with ExitStack() as ctx:
        def sb(name, shape, dt=F32):
            return ctx.enter_context(nc.sbuf_tensor(name, shape, dt))

        def sem(name):
            return ctx.enter_context(nc.semaphore(name))

        logits = io["logits"]
        wnames = ["k", "v", "q", "g", "o"]
        w_hi = {n: sb(f"w{n}_hi", [P, KC, D], F32R) for n in wnames}
        w_lo = {n: sb(f"w{n}_lo", [P, KC, D], F32R) for n in wnames}
        wr_hi, wr_lo = sb("wr_hi", [P, KC, RW], F32R), sb("wr_lo", [P, KC, RW], F32R)
        ident = sb("ident", [P, P])
        group_mask = sb("group_mask", [P, SW])
        c_silu = sb("c_silu", [P, KC, B, P // B])
        cT = sb("cT", [P, KC, B])
        cS = sb("cS", [P, KC, B])
        mod = {n: sb(f"mod_{n}", [P, B, D]) for n in ("sa", "ca1", "ga", "gabo", "sb", "cb1")}
        bias_k, bias_v, bias_q, bias_g = (sb(f"bias_{n}", [P, D]) for n in "kvqg")
        cos_t, sin_t = sb("cos_t", [P, TPB, DK]), sb("sin_t", [P, TPB, DK])
        NSTAGE = 3
        scratch = sb("scratch", [P, NSTAGE * KC * D])
        stage = [scratch[:, s * KC * D:(s + 1) * KC * D] for s in range(NSTAGE)]
        y = scratch[:, 0:2 * D]
        t1 = scratch[:, 2 * D:4 * D]
        t2 = scratch[:, 4 * D:6 * D]
        feat = [scratch[:, 6 * D:8 * D], scratch[:, 8 * D:10 * D]]
        o_buf = scratch[:, 10 * D:11 * D]
        o1_buf = scratch[:, 11 * D:12 * D]
        xin = [sb(f"xin{i}", [P, D]) for i in range(2)]
        xhat = sb("xhat", [P, D])
        h_buf = [sb(f"h{i}", [P, D]) for i in range(2)]
        hT = [sb(f"hT{i}", [P, 2, KC, P], F32R) for i in range(2)]
        v_buf = [sb(f"v{i}", [P, NG, SW]) for i in range(2)]
        th = [sb(f"th{i}", [P, D]) for i in range(2)]
        qT = sb("qT", [P, NG, P])
        state = [[sb(f"state{b}{c}", [P, NG, SW]) for c in range(2)] for b in range(2)]
        blocks = [sb(f"blocks{c}", [P, NG, SW]) for c in range(2)]
        rden = sb("rden", [P, H])
        rden2 = sb("rden2", [P, H])
        oT = sb("oT", [P, 2, KC, P], F32R)
        xres = [sb(f"xres{i}", [P, D]) for i in range(2)]
        proj = sb("proj", [P, D])
        x2 = [sb(f"x2_{i}", [P, D]) for i in range(2)]
        xhat2 = proj
        h2_both = sb("h2_both", [P, B, D])
        h2 = [h2_both[:, i, :] for i in range(2)]
        proj_gb = h2_both
        h2T = sb("h2T", [P, 2, KC, P], F32R)
        st1, st2 = sb("st1", [P, 6]), sb("st2", [P, 6])
        mv1, mv2 = [sb(f"mv1_{i}", [P, 2]) for i in range(2)], [sb(f"mv2_{i}", [P, 2]) for i in range(2)]
        rs1, rs2 = [sb(f"rs1_{i}", [P, 2]) for i in range(2)], [sb(f"rs2_{i}", [P, 2]) for i in range(2)]
        minus_half = sb("minus_half", [P, 1])

        bank = [ctx.enter_context(nc.psum_tensor(f"bank{i}", [P, D], F32)) for i in range(4)]
        psS = ctx.enter_context(nc.psum_tensor("psS", [P, 2, 512], F32))
        psN = ctx.enter_context(nc.psum_tensor("psN", [P, 2, 512], F32))

        waited_pool, waited_dve, waited_sp = sem("waited_pool"), sem("waited_dve"), sem("waited_sp")
        small_in = sem("small_in")
        stage_in = [sem(f"stage_in{s}") for s in range(NSTAGE)]
        hi_done, lo_done = sem("hi_done"), sem("lo_done")
        const_ready, const_ready2 = sem("const_ready"), sem("const_ready2")
        csilu_a, csilu_s, csilu_ready = sem("csilu_a"), sem("csilu_s"), sem("csilu_ready")
        mod_mm, mod_free, mod_tmp = sem("mod_mm"), sem("mod_free"), sem("mod_tmp")
        mod_ready = sem("mod_ready")
        gb_out = sem("gb_out")
        x_in = [sem(f"x_in{i}") for i in range(2)]
        xres_in = [sem(f"xres_in{i}") for i in range(2)]
        st1_done, mv1_done, rs1_a, rs1_done = sem("st1_done"), sem("mv1_done"), sem("rs1_a"), sem("rs1_done")
        xhat_done, h_a, h_done = sem("xhat_done"), sem("h_a"), sem("h_done")
        hT_mm, hT_hi, hT_lo = sem("hT_mm"), sem("hT_hi"), sem("hT_lo")
        k_mm, v_mm, q_mm, g_mm = sem("k_mm"), sem("v_mm"), sem("q_mm"), sem("g_mm")
        k_out, v_out, q_out, g_out = sem("k_out"), sem("v_out"), sem("q_out"), sem("g_out")
        tanh_done = sem("tanh_done")
        rope_cos, rope_sin, rope_done = sem("rope_cos"), sem("rope_sin"), sem("rope_done")
        exp_done, exp_cap, feat_done = sem("exp_done"), sem("exp_cap"), sem("feat_done")
        qT_mm, qT_done = sem("qT_mm"), sem("qT_done")
        s_mm, state_done, blocks_done = sem("s_mm"), sem("state_done"), sem("blocks_done")
        n_mm = sem("n_mm")
        den_a, den_done, o_half, o_done = sem("den_a"), sem("den_done"), sem("o_half"), sem("o_done")
        oT_mm, oT_hi, oT_lo = sem("oT_mm"), sem("oT_hi"), sem("oT_lo")
        o_mm, proj_done, xg_done, x2_done = sem("o_mm"), sem("proj_done"), sem("xg_done"), sem("x2_done")
        st2_done, mv2_done, rs2_a, rs2_done = sem("st2_done"), sem("mv2_done"), sem("rs2_a"), sem("rs2_done")
        xhat2_done, h2_a, h2_done = sem("xhat2_done"), sem("h2_a"), sem("h2_done")
        h2T_mm, h2T_hi, h2T_lo = sem("h2T_mm"), sem("h2T_hi"), sem("h2T_lo")
        r_mm, logits_done = sem("r_mm"), sem("logits_done")
        x2_out = [sem(f"x2_out{i}") for i in range(2)]
        h2_out = [sem(f"h2_out{i}") for i in range(2)]
        h2T_out = sem("h2T_out")

        MODS = ["sa", "ca", "ga", "sb", "cb", "gb"]
        jobs = ["sa", "ca", "k", "v", "q", "g", "ga", "o", "cb", "sb", "gb"]
        mod_no = {n: i for i, n in enumerate(x for x in jobs if x in MODS)}
        split_no = {n: i for i, n in enumerate(x for x in jobs if x not in MODS)}
        copies_before = {n: 4 * i for n, i in mod_no.items()}

        def slot_free(eng, i):
            if i >= NSTAGE:
                old = jobs[i - NSTAGE]
                if old in MODS:
                    eng.wait_ge(mod_mm, mod_no[old] + 1)
                else:
                    eng.wait_ge(lo_done, split_no[old] + 1)

        wT = {n: io[f"w{n}"].rearrange("(p c) n -> p c n", c=KC) for n in wnames}
        wmod = io["wmod"].rearrange("(p c) (m n) -> m p c n", c=KC, m=6)
        x_t = io["x"].rearrange("b (j p) d -> b j p d", p=P)

        with nc.Block() as block:
            @block.sync
            def _(sp):
                sp.dma_start(cT[:], io["c"]).then_inc(small_in, 16)
                for n, bt in (("k", bias_k), ("v", bias_v), ("q", bias_q), ("g", bias_g)):
                    sp.dma_start(bt[:], io[f"b{n}"].partition_broadcast(P)).then_inc(small_in, 16)
                sp.dma_start(mod["gabo"][:, 0, :], io["bo"].partition_broadcast(P)).then_inc(small_in, 16)
                sp.dma_start(cos_t[:], io["cos"]).then_inc(small_in, 16)
                sp.dma_start(sin_t[:], io["sin"]).then_inc(small_in, 16)
                sp.dma_start(group_mask[:], io["mask"]).then_inc(small_in, 16)
                sp.dma_start(proj[:, 0:KC * RW].rearrange("p (c n) -> p c n", c=KC),
                             io["wr"].rearrange("(p c) n -> p c n", c=KC)).then_inc(small_in, 16)
                for i, n in enumerate(jobs):
                    slot_free(sp, i)
                    src = wmod[MODS.index(n)] if n in MODS else wT[n]
                    sp.dma_start(stage[i % NSTAGE].rearrange("p (c n) -> p c n", c=KC), src)\
                      .then_inc(stage_in[i % NSTAGE], 16)
                sp.wait_ge(mod_ready, copies_before["gb"] + 4)
                sp.dma_start(scr["gb"], proj_gb[:]).then_inc(gb_out, 16)

                def step(j, b):
                    if real(j, b, -2):
                        jn, bn = lag(j, b, -2)
                        wait_tile(sp, xhat_done, j, b, 0)
                        sp.dma_start(xin[bn][:], x_t[bn, jn]).then_inc(x_in[bn], 16)
                    if real(j, b, 3):
                        jl, bl = lag(j, b, 3)
                        wait_tile(sp, x2_done, j, b, 3)
                        sp.sem_inc(waited_sp, 1)
                        sp.dma_start(scr["x2"][bl, jl], x2[bl][:]).then_inc(x2_out[bl], 16)
                        wait_tile(sp, h2_done, j, b, 3)
                        sp.dma_start(scr["h2"][bl, jl], h2[bl]).then_inc(h2_out[bl], 16)
                    if real(j, b, 1):
                        jl, bl = lag(j, b, 1)
                        wait_tile(sp, x2_done, j, b, 3)
                        sp.dma_start(xres[bl][:], x_t[bl, jl]).then_inc(xres_in[bl], 16)
                    if real(j, b, 3):
                        jl, bl = lag(j, b, 3)
                        wait_tile(sp, h2T_lo, j, b, 3)
                        sp.dma_start(scr["h2T"][bl, jl], raw(h2T[:]).rearrange("p s c t -> p (s c t)"))\
                          .then_inc(h2T_out, 16)

                run_steps(sp, step)
                sp.wait_ge(gb_out, 16)
                sp.wait_ge(h2T_out, 16 * NT)
                for s in (x2_out, h2_out):
                    for i in range(2):
                        sp.wait_ge(s[i], 16 * TPB)

            @block.gpsimd
            def _(pool):
                pool.memset(ident[:], 0.0).then_inc(const_ready, 1)
                pool.memset(minus_half[:], -0.5).then_inc(const_ready, 1)
                for i in range(2):
                    pool.memset(v_buf[i][:, :, P:SW], 1.0).then_inc(const_ready, 1)
                    pool.memset(state[i][1][:], 0.0).then_inc(const_ready, 1)
                pool.wait_ge(const_ready, 6)
                pool.affine_select(out=ident[:], in_=ident[:], compare_op=ALU.not_equal, fill=1.0, base=0,
                                   pattern=[[-1, P]], channel_multiplier=1).then_inc(const_ready2, 1)

                pool.wait_ge(gb_out, 16)

                def step(j, b):
                    if real(j, b, 2):
                        jl, bl = lag(j, b, 2)
                        pool.wait_ge(xres_in[bl], 16 * (jl + 1))
                        pool.tensor_tensor(xres[bl][:], xres[bl][:], mod["gabo"][:, bl, :], ALU.add)\
                            .then_inc(xg_done, 1)
                        wait_tile(pool, mv2_done, j, b, 2)
                        pool.sem_inc(waited_pool, 1)
                        pool.tensor_scalar(rs2[bl][:, 0:1], mv2[bl][:, 1:2], LN_EPS, None, ALU.add).then_inc(rs2_a, 1)
                        wait_tile(pool, rs2_a, j, b, 2)
                        pool.tensor_tensor(rs2[bl][:, 1:2], rs2[bl][:, 0:1], minus_half[:], ALU.pow)\
                            .then_inc(rs2_done, 1)
                    if real(j, b, -2):
                        jn, bn = lag(j, b, -2)
                        wait_tile(pool, mv1_done, j, b, -2)
                        pool.sem_inc(waited_pool, 1)
                        pool.tensor_scalar(rs1[bn][:, 0:1], mv1[bn][:, 1:2], LN_EPS, None, ALU.add).then_inc(rs1_a, 1)
                        wait_tile(pool, rs1_a, j, b, -2)
                        pool.tensor_tensor(rs1[bn][:, 1:2], rs1[bn][:, 0:1], minus_half[:], ALU.pow)\
                            .then_inc(rs1_done, 1)
                    if real(j, b, 1):
                        jl, bl = lag(j, b, 1)
                        for c in range(2):
                            wait_tile(pool, state_done, j, b, 1, 2, c + 1)
                            wait_tile(pool, n_mm, j, b, 2)
                            pool.tensor_tensor(blocks[c][:], state[bl][c][:],
                                               group_mask[:].unsqueeze(1).broadcast_to((P, NG, SW)),
                                               ALU.mult).then_inc(blocks_done, 1)
                    if real(j, b, 2):
                        jl, bl = lag(j, b, 2)
                        wait_tile(pool, xhat2_done, j, b, 2)
                        pool.wait_ge(mod_ready, 24)
                        if real(j, b, 4):
                            pool.wait_ge(h2_out[bl], 16 * jl)
                            wait_tile(pool, h2T_mm, j, b, 4)
                        pool.tensor_tensor(h2[bl], xhat2[:], mod["cb1"][:, bl, :], ALU.mult).then_inc(h2_a, 1)
                        wait_tile(pool, h2_a, j, b, 2)
                        pool.tensor_tensor(h2[bl], h2[bl], mod["sb"][:, bl, :], ALU.add).then_inc(h2_done, 1)
                    if real(j, b, -2):
                        jn, bn = lag(j, b, -2)
                        wait_tile(pool, xhat_done, j, b, -2)
                        pool.wait_ge(mod_ready, copies_before["ca"] + 4)
                        wait_tile(pool, hT_mm, j, b, 0)
                        pool.tensor_tensor(h_buf[bn][:], xhat[:], mod["ca1"][:, bn, :], ALU.mult).then_inc(h_a, 1)
                        wait_tile(pool, h_a, j, b, -2)
                        pool.tensor_tensor(h_buf[bn][:], h_buf[bn][:], mod["sa"][:, bn, :], ALU.add)\
                            .then_inc(h_done, 1)
                    if real(j, b, 0):
                        wait_tile(pool, q_out, j, b)
                        wait_tile(pool, rope_done, j, b, 1)
                        pool.sem_inc(waited_pool, 1)
                        pool.tensor_tensor(t2.rearrange("p (h e) -> p h e", e=DK), y.rearrange("p (h e) -> p h e", e=DK),
                                           sin_t[:, j, :].unsqueeze(1).broadcast_to((P, 2 * H, DK)),
                                           ALU.mult).then_inc(rope_sin, 1)

                run_steps(pool, step)

            @block.scalar
            def _(act):
                act.wait_ge(small_in, 160)
                nc.scalar.activation(cS[:], cT[:], ACT.Silu).then_inc(csilu_a, 1)
                nc.scalar.copy(wr_hi[:], proj[:, 0:KC * RW].rearrange("p (c n) -> p c n", c=KC)).then_inc(csilu_s, 1)
                for i, n in enumerate(jobs):
                    if n not in MODS:
                        act.wait_ge(stage_in[i % NSTAGE], 16 * (i // NSTAGE + 1))
                        nc.scalar.copy(w_hi[n][:], stage[i % NSTAGE].rearrange("p (c n) -> p c n", c=KC))\
                            .then_inc(hi_done, 1)

                def step(j, b):
                    if real(j, b, 3):
                        jl, bl = lag(j, b, 3)
                        wait_tile(act, h2T_mm, j, b, 3)
                        if real(j, b, 4):
                            act.wait_ge(h2T_out, 16 * (2 * j + b - 3))
                            wait_tile(act, r_mm, j, b, 4)
                        nc.scalar.copy(h2T[:, 0], bank[2][:].rearrange("p (c t) -> p c t", c=KC)).then_inc(h2T_hi, 1)
                    if real(j, b, 2):
                        wait_tile(act, oT_mm, j, b, 2)
                        wait_tile(act, o_mm, j, b, 3)
                        nc.scalar.copy(oT[:, 0], bank[3][:].rearrange("p (c t) -> p c t", c=KC)).then_inc(oT_hi, 1)
                    if real(j, b, 0):
                        wait_tile(act, g_out, j, b)
                        nc.scalar.activation(th[b][:], th[b][:], ACT.Tanh, scale=0.5).then_inc(tanh_done, 1)
                    if real(j, b, 1):
                        wait_tile(act, qT_mm, j, b, 1)
                        wait_tile(act, n_mm, j, b, 2)
                        nc.scalar.copy(qT[:], bank[3][:].rearrange("p (g t) -> p g t", g=NG)).then_inc(qT_done, 1)
                    if real(j, b, -1):
                        jn, bn = lag(j, b, -1)
                        wait_tile(act, hT_mm, j, b, -1)
                        wait_tile(act, g_mm, j, b, 1)
                        nc.scalar.copy(hT[bn][:, 0], bank[0][:].rearrange("p (c t) -> p c t", c=KC)).then_inc(hT_hi, 1)
                    if real(j, b, 0):
                        wait_tile(act, exp_cap, j, b)
                        nc.scalar.activation(t1, t1, ACT.Exp).then_inc(exp_done, 1)

                run_steps(act, step)

            @block.vector
            def _(dve):
                dve.wait_ge(csilu_a, 1)
                nc.vector.tensor_copy(c_silu[:], cS[:].unsqueeze(3).broadcast_to((P, KC, B, P // B)))\
                    .then_inc(csilu_ready, 1)
                dve.wait_ge(csilu_s, 1)
                nc.vector.tensor_tensor(wr_lo[:], proj[:, 0:KC * RW].rearrange("p (c n) -> p c n", c=KC),
                                        raw(wr_hi[:]), ALU.subtract).then_inc(csilu_ready, 1)
                dve.wait_ge(csilu_ready, 2)
                tmp_count = [0]

                def tmp(ins):
                    tmp_count[0] += 1
                    ins.then_inc(mod_tmp, 1)
                    dve.wait_ge(mod_tmp, tmp_count[0])

                for i, n in enumerate(jobs):
                    if n not in MODS:
                        dve.wait_ge(hi_done, split_no[n] + 1)
                        nc.vector.tensor_tensor(w_lo[n][:], stage[i % NSTAGE].rearrange("p (c n) -> p c n", c=KC),
                                                raw(w_hi[n][:]), ALU.subtract).then_inc(lo_done, 1)
                        continue
                    m = mod_no[n]
                    dve.wait_ge(mod_mm, m + 1)
                    if m:
                        dve.wait_ge(mod_ready, 4 * m)
                    src = bank[m % 4]
                    if n in ("ga", "gb"):
                        tmp(nc.vector.tensor_scalar(proj[:], src[:], 0.0, 2.0, ALU.is_ge, ALU.mult))
                        tmp(nc.vector.tensor_scalar(proj[:], proj[:], -1.0, None, ALU.add))
                        tmp(nc.vector.tensor_tensor(xhat[:], src[:], proj[:], ALU.mult))
                        tmp(nc.vector.scalar_tensor_tensor(proj[:], xhat[:], 0.25, proj[:], ALU.max, ALU.mult))
                        src = proj
                    elif n in ("ca", "cb"):
                        tmp(nc.vector.tensor_scalar(proj[:], src[:], 1.0, None, ALU.add))
                        src = proj
                    dst = {"sa": mod["sa"], "ca": mod["ca1"], "ga": mod["ga"], "sb": mod["sb"], "cb": mod["cb1"],
                           "gb": proj_gb}[n]
                    for bb in range(B):
                        for half in range(2):
                            nc.vector.tensor_copy(dst[64 * half:64 * half + 64, bb, :], src[64 * bb:64 * bb + 64, :])\
                                .then_inc(mod_ready, 1)
                    if n == "ga":
                        dve.wait_ge(mod_ready, copies_before["ga"] + 4)
                        for bb in (1, 0):
                            tmp(nc.vector.tensor_tensor(mod["gabo"][:, bb, :], mod["ga"][:, bb, :],
                                                        mod["gabo"][:, 0, :], ALU.mult))
                dve.wait_ge(mod_ready, 24)
                dve.wait_ge(const_ready, 6)

                def step(j, b):
                    if real(j, b, 0):
                        wait_tile(dve, k_mm, j, b)
                        wait_tile(dve, feat_done, j, b, 1)
                        nc.vector.tensor_tensor(y[:, D:2 * D], bank[0][:], bias_k[:], ALU.add).then_inc(k_out, 1)
                        wait_tile(dve, v_mm, j, b)
                        wait_tile(dve, s_mm, j, b, 2, 2)
                        nc.vector.tensor_tensor(v_buf[b][:, :, 0:P], bank[1][:].rearrange("p (g e) -> p g e", g=NG),
                                                bias_v[:].rearrange("p (g e) -> p g e", g=NG), ALU.add)\
                            .then_inc(v_out, 1)
                    if real(j, b, 3):
                        jl, bl = lag(j, b, 3)
                        wait_tile(dve, h2T_hi, j, b, 3)
                        nc.vector.tensor_tensor(h2T[:, 1], bank[2][:].rearrange("p (c t) -> p c t", c=KC),
                                                raw(h2T[:, 0]), ALU.subtract).then_inc(h2T_lo, 1)
                    if real(j, b, 2):
                        wait_tile(dve, oT_hi, j, b, 2)
                        nc.vector.tensor_tensor(oT[:, 1], bank[3][:].rearrange("p (c t) -> p c t", c=KC),
                                                raw(oT[:, 0]), ALU.subtract).then_inc(oT_lo, 1)
                    if real(j, b, 0):
                        wait_tile(dve, q_mm, j, b)
                        nc.vector.tensor_tensor(y[:, 0:D], bank[0][:], bias_q[:], ALU.add).then_inc(q_out, 1)
                    if real(j, b, 3):
                        jl, bl = lag(j, b, 3)
                        wait_tile(dve, r_mm, j, b, 3)
                        nc.vector.tensor_copy(logits[:, bl * TPB + jl, :], psN[:, 1, 300:300 + RW]).then_inc(logits_done, 1)
                    if real(j, b, 2):
                        jl, bl = lag(j, b, 2)
                        wait_tile(dve, o_mm, j, b, 2)
                        wait_tile(dve, h2_a, j, b, 3)
                        nc.vector.tensor_tensor(proj[:], bank[2][:], mod["ga"][:, bl, :], ALU.mult).then_inc(proj_done, 1)
                        wait_tile(dve, proj_done, j, b, 2)
                        wait_tile(dve, xg_done, j, b, 2)
                        if real(j, b, 4):
                            dve.wait_ge(x2_out[bl], 16 * jl)
                        nc.vector.tensor_tensor(x2[bl][:], proj[:], xres[bl][:], ALU.add).then_inc(x2_done, 1)
                        wait_tile(dve, x2_done, j, b, 2)
                        nc.vector.bn_stats(st2[:], x2[bl][:]).then_inc(st2_done, 1)
                        wait_tile(dve, st2_done, j, b, 2)
                        wait_tile(dve, xhat2_done, j, b, 4)
                        dve.sem_inc(waited_dve, 1)
                        nc.vector.bn_aggr(mv2[bl][:], st2[:]).then_inc(mv2_done, 1)
                    if real(j, b, 0):
                        wait_tile(dve, g_mm, j, b)
                        nc.vector.tensor_tensor(th[b][:], bank[1][:], bias_g[:], ALU.add).then_inc(g_out, 1)
                    if real(j, b, -2):
                        jn, bn = lag(j, b, -2)
                        dve.wait_ge(x_in[bn], 16 * (jn + 1))
                        nc.vector.bn_stats(st1[:], xin[bn][:]).then_inc(st1_done, 1)
                        wait_tile(dve, st1_done, j, b, -2)
                        dve.sem_inc(waited_dve, 1)
                        nc.vector.bn_aggr(mv1[bn][:], st1[:]).then_inc(mv1_done, 1)
                    if real(j, b, 2):
                        jl, bl = lag(j, b, 2)
                        wait_tile(dve, rs2_done, j, b, 2)
                        nc.vector.tensor_scalar(xhat2[:], x2[bl][:], mv2[bl][:, 0:1], rs2[bl][:, 1:2],
                                                ALU.subtract, ALU.mult).then_inc(xhat2_done, 1)
                    if real(j, b, 1):
                        jl, bl = lag(j, b, 1)
                        for c in range(2):
                            wait_tile(dve, s_mm, j, b, 1, 2, c + 1)
                            wait_tile(dve, state_done, j, b, 1, 2, c)
                            wait_tile(dve, blocks_done, j, b, 3, 2, c + 1)
                            nc.vector.tensor_tensor(state[bl][c][:].rearrange("p (s g) e -> p s (g e)", s=2),
                                                    psS[:, :, 0:2 * SW],
                                                    state[bl][1 - c][:].rearrange("p (s g) e -> p s (g e)", s=2),
                                                    ALU.add).then_inc(state_done, 1)
                    if real(j, b, -2):
                        jn, bn = lag(j, b, -2)
                        wait_tile(dve, rs1_done, j, b, -2)
                        wait_tile(dve, h_a, j, b, -1)
                        nc.vector.tensor_scalar(xhat[:], xin[bn][:], mv1[bn][:, 0:1], rs1[bn][:, 1:2],
                                                ALU.subtract, ALU.mult).then_inc(xhat_done, 1)
                    if real(j, b, -1):
                        jn, bn = lag(j, b, -1)
                        wait_tile(dve, hT_hi, j, b, -1)
                        nc.vector.tensor_tensor(hT[bn][:, 1], bank[0][:].rearrange("p (c t) -> p c t", c=KC),
                                                raw(hT[bn][:, 0]), ALU.subtract).then_inc(hT_lo, 1)
                    if real(j, b, 1):
                        jl, bl = lag(j, b, 1)
                        wait_tile(dve, n_mm, j, b, 1)
                        wait_tile(dve, o_done, j, b, 2)
                        num = psN[:, :, 0:2 * SW].rearrange("p s (g e) -> p s g e", e=SW)
                        nc.vector.tensor_scalar(rden[:].rearrange("p (s g h) -> p s g h", s=2, g=2), num[:, :, :, P:SW],
                                                2.0, 2 * DEN_EPS, ALU.mult, ALU.add).then_inc(den_a, 1)
                        wait_tile(dve, den_a, j, b, 1)
                        nc.vector.reciprocal(rden2[:], rden[:]).then_inc(den_done, 1)
                        wait_tile(dve, tanh_done, j, b, 1)
                        for s in range(2):
                            nc.vector.scalar_tensor_tensor(
                                o1_buf[:, s * 256:(s + 1) * 256].rearrange("p (g e) -> p g e", g=2),
                                th[bl][:, s * 256:(s + 1) * 256].rearrange("p (g e) -> p g e", g=2), 1.0,
                                num[:, s, :, 0:P], ALU.add, ALU.mult).then_inc(o_half, 1)
                        wait_tile(dve, o_half, j, b, 1, 2)
                        wait_tile(dve, den_done, j, b, 1)
                        wait_tile(dve, oT_mm, j, b, 2)
                        nc.vector.tensor_tensor(o_buf.rearrange("p (h e) -> p h e", e=DK),
                                                o1_buf.rearrange("p (h e) -> p h e", e=DK),
                                                rden2[:].unsqueeze(2).broadcast_to((P, H, DK)), ALU.mult)\
                            .then_inc(o_done, 1)
                    if real(j, b, 0):
                        wait_tile(dve, q_out, j, b)
                        wait_tile(dve, k_out, j, b)
                        nc.vector.tensor_tensor(t1.rearrange("p (h e) -> p h e", e=DK), y.rearrange("p (h e) -> p h e", e=DK),
                                                cos_t[:, j, :].unsqueeze(1).broadcast_to((P, 2 * H, DK)),
                                                ALU.mult).then_inc(rope_cos, 1)
                        wait_tile(dve, rope_cos, j, b)
                        wait_tile(dve, rope_sin, j, b)
                        nc.vector.tensor_tensor(y.rearrange("p (i two) -> p i two", two=2),
                                                t1.rearrange("p (i two) -> p i two", two=2),
                                                t2.rearrange("p (i two) -> p i two", two=2)[:, :, ::-1],
                                                ALU.add).then_inc(rope_done, 1)
                        wait_tile(dve, rope_done, j, b)
                        nc.vector.tensor_scalar(t1, y, 0.0, None, ALU.min).then_inc(exp_cap, 1)
                        wait_tile(dve, exp_done, j, b)
                        wait_tile(dve, s_mm, j, b, 2, 2)
                        nc.vector.scalar_tensor_tensor(feat[b], y, 1.0, t1, ALU.add, ALU.max).then_inc(feat_done, 1)

                run_steps(dve, step)

            @block.tensor
            def _(pe):
                def product(out, pairs):
                    passes = [(l[u], r[w]) for l, r in pairs for u, w in ((0, 0), (0, 1), (1, 0))]
                    for n, (l, r) in enumerate(passes):
                        last = nc.tensor.matmul(out, l, r, start=n == 0, stop=n == len(passes) - 1)
                    return last

                def transpose_tile(out, src):
                    v = src.rearrange("t (q c) -> t c q", c=KC)
                    for c in range(KC):
                        last = nc.tensor.transpose(out[:, c * P:(c + 1) * P], v[:, c, :], ident[:])
                    return last

                pe.wait_ge(csilu_ready, 1)
                for i, n in enumerate(jobs):
                    if n in MODS:
                        m = mod_no[n]
                        pe.wait_ge(stage_in[i % NSTAGE], 16 * (i // NSTAGE + 1))
                        if m >= 4:
                            pe.wait_ge(mod_ready, 4 * (m - 3))
                        for c in range(KC):
                            last = nc.tensor.matmul(bank[m % 4][:], c_silu[:, c].rearrange("p b m -> p (b m)"),
                                                    stage[i % NSTAGE][:, c * D:(c + 1) * D],
                                                    start=c == 0, stop=c == KC - 1)
                        last.then_inc(mod_mm, 1)
                pe.wait_ge(mod_ready, 24)
                pe.wait_ge(const_ready2, 1)
                pe.wait_ge(lo_done, 5)

                def project(n, out, hb):
                    return product(out, [((hb[:, 0, c], hb[:, 1, c]), (w_hi[n][:, c], w_lo[n][:, c]))
                                         for c in range(KC)])

                def step(j, b):
                    if real(j, b, 0):
                        wait_tile(pe, hT_lo, j, b)
                        project("k", bank[0][:], hT[b]).then_inc(k_mm, 1)
                        wait_tile(pe, g_out, j, b, 1)
                        project("v", bank[1][:], hT[b]).then_inc(v_mm, 1)
                    if real(j, b, 3):
                        jl, bl = lag(j, b, 3)
                        wait_tile(pe, h2_done, j, b, 3)
                        wait_tile(pe, proj_done, j, b, 3)
                        transpose_tile(bank[2][:], h2[bl]).then_inc(h2T_mm, 1)
                    if real(j, b, 2):
                        wait_tile(pe, o_done, j, b, 2)
                        wait_tile(pe, qT_done, j, b, 2)
                        transpose_tile(bank[3][:], o_buf).then_inc(oT_mm, 1)
                    if real(j, b, 0):
                        wait_tile(pe, k_out, j, b)
                        project("q", bank[0][:], hT[b]).then_inc(q_mm, 1)
                    if real(j, b, 3):
                        jl, bl = lag(j, b, 3)
                        wait_tile(pe, h2T_lo, j, b, 3)
                        wait_tile(pe, logits_done, j, b, 4)
                        wait_tile(pe, o_done, j, b, 2)
                        product(psN[:, 1, 300:300 + RW],
                                [((h2T[:, 0, c], h2T[:, 1, c]), (wr_hi[:, c], wr_lo[:, c])) for c in range(KC)])\
                            .then_inc(r_mm, 1)
                    if real(j, b, 2):
                        wait_tile(pe, oT_lo, j, b, 2)
                        wait_tile(pe, h2T_lo, j, b, 3)
                        project("o", bank[2][:], oT).then_inc(o_mm, 1)
                    if real(j, b, 0):
                        wait_tile(pe, v_out, j, b)
                        project("g", bank[1][:], hT[b]).then_inc(g_mm, 1)
                    if real(j, b, 1):
                        jl, bl = lag(j, b, 1)
                        wait_tile(pe, feat_done, j, b, 1)
                        wait_tile(pe, oT_lo, j, b, 2)
                        for g in range(NG):
                            last = nc.tensor.transpose(bank[3][:, g * P:(g + 1) * P], feat[bl][:, g * P:(g + 1) * P],
                                                       ident[:])
                        last.then_inc(qT_mm, 1)
                        wait_tile(pe, v_out, j, b, 1)
                        for c in range(2):
                            wait_tile(pe, state_done, j, b, 1, 2, c)
                            rows = slice(c * CS, (c + 1) * CS)
                            for g in range(NG):
                                last = nc.tensor.matmul(psS[:, g // 2, (g % 2) * SW:(g % 2 + 1) * SW],
                                                        feat[bl][rows, D + g * P:D + (g + 1) * P],
                                                        v_buf[bl][rows, g, :], start=True, stop=True)
                            last.then_inc(s_mm, 1)
                    if real(j, b, -1):
                        jn, bn = lag(j, b, -1)
                        wait_tile(pe, h_done, j, b, -1)
                        wait_tile(pe, q_out, j, b)
                        transpose_tile(bank[0][:], h_buf[bn][:]).then_inc(hT_mm, 1)
                    if real(j, b, 1):
                        jl, bl = lag(j, b, 1)
                        wait_tile(pe, qT_done, j, b, 1)
                        wait_tile(pe, o_done, j, b, 2)
                        wait_tile(pe, logits_done, j, b, 3)
                        for c in range(2):
                            wait_tile(pe, blocks_done, j, b, 1, 2, c + 1)
                            for g in range(NG):
                                last = nc.tensor.matmul(psN[c * CS:(c + 1) * CS, g // 2, (g % 2) * SW:(g % 2 + 1) * SW],
                                                        qT[:, g, c * CS:(c + 1) * CS], blocks[c][:, g, :],
                                                        start=True, stop=True)
                        last.then_inc(n_mm, 1)

                run_steps(pe, step)


FCH = FS // P
GROUP = 3
NGROUPS = -(-FCH // GROUP)
SUB = 4
UNITS = NT // SUB
XPU = 4
FIRST_X = 2
LAST_X = FIRST_X + E // XPU
TABLE_COLS = 8 + E + 2 * NT + P
FX = -(-F // P)
RAW_SLOTS = 4
S1 = CAP // 8


def chunks_of(g):
    return GROUP if g < NGROUPS - 1 else FCH - GROUP * (NGROUPS - 1)


def chunk_no(u, c, last):
    if last:
        return GROUP * UNITS * (NGROUPS - 1) + chunks_of(NGROUPS - 1) * (u - UNITS * (NGROUPS - 1)) + c
    return GROUP * u + c


ROUTING0 = [("gate", 0), ("up", 0), ("route", 0), ("gate", 1), ("up", 1), ("route", 1), ("gate", 2), ("up", 2),
            ("route", 2), ("down", 0), ("down", 1), ("down", 2), ("down", 3)]
ROUTING1 = [("gate", 0), ("route", 3), ("up", 0), ("route", 4), ("gate", 1), ("up", 1), ("gate", 2), ("up", 2),
            ("down", 0), ("down", 1), ("down", 2), ("down", 3)]
WITH_X = [("gather", 0), ("gather", 1), ("split_gu", 0), ("gate", 0), ("rows", 0), ("up", 0), ("split_d", 0),
          ("gu", 0), ("split_gu", 1), ("gate", 1), ("mid", 0), ("up", 1), ("gu", 1), ("split_gu", 2),
          ("exp_down", 0), ("split_d", 1), ("gate", 2), ("mid", 1), ("rows", 1), ("up", 2), ("gu", 2),
          ("split_gu", 3), ("exp_down", 1), ("split_d", 2), ("down", 0), ("mid", 2), ("down", 1), ("gu", 3),
          ("exp_down", 2), ("split_d", 3), ("down", 2), ("mid", 3), ("down", 3), ("exp_down", 3)]
COMBINE4 = [("fetch", 0), ("gate", 0), ("up", 0), ("fetch", 1), ("combine", 0), ("gate", 1), ("up", 1), ("fetch", 2),
            ("combine", 1), ("gate", 2), ("up", 2), ("fetch", 3), ("combine", 2), ("down", 0), ("down", 1),
            ("down", 2), ("down", 3), ("combine", 3)]
COMBINE2 = [("fetch", 0), ("gate", 0), ("up", 0), ("fetch", 1), ("combine", 0), ("gate", 1), ("up", 1),
            ("combine", 1), ("down", 0), ("down", 1), ("down", 2), ("down", 3), ("store", 0)]


def run_units(eng, unit, weights):
    weights(0)
    unit(0, 0, ROUTING0)
    unit(0, 1, ROUTING1)
    with eng.Fori(2, 4) as s:
        unit(0, s, WITH_X)
    weights(1)
    with eng.Fori(0, 4) as s:
        unit(1, s, WITH_X)
    weights(2)
    with eng.Fori(0, 2) as s:
        unit(2, s, WITH_X)
    with eng.Fori(2, 4) as s:
        unit(2, s, COMBINE4)
    weights(3)
    with eng.Fori(0, 4) as s:
        unit(3, s, COMBINE2)


def ffn(nc, io, scr, out):
    with ExitStack() as ctx:
        def sb(name, shape, dt=F32):
            return ctx.enter_context(nc.sbuf_tensor(name, shape, dt))

        def sem(name):
            return ctx.enter_context(nc.semaphore(name))

        logits = io["logits"]
        FD = GROUP * D
        x2s = sb("x2s", [P, NT, D])
        gb = sb("gb", [P, B, D])
        ws = [sb(f"ws{c}", [P, 2, 3 * D], F32R) for c in range(GROUP)]
        ws_raw = sb("ws_raw", [P, 3 * D])
        hT = sb("h2T_unit", [P, SUB, 2, KC, P], F32R)
        guT = [sb(f"guT{c}", [P, 2, SUB * P], F32R) for c in range(GROUP)]
        sil = sb("sil", [P, SUB * P])
        gu = sb("gu", [P, SUB * P])
        dn_tmp = [sb(f"dn_tmp{i}", [P, D]) for i in range(2)]
        sig4 = sb("sig4", [P, SUB])
        wx_raw = sb("wx_raw", [P, RAW_SLOTS, FX * D])
        wx = [sb(f"wx_{n}", [P, 2, FX * D], F32R) for n in ("gate", "up", "down")]
        rows = [sb(f"rows{i}", [P, D]) for i in range(2)]
        xs = [sb(f"xs{i}", [P, 2, KC, P], F32R) for i in range(2)]
        low_g, low_u = sb("low_g", [CAP, F]), sb("low_u", [CAP, F])
        xg, xu = sb("xg", [CAP, F]), sb("xu", [CAP, F])
        xgu = sb("xgu", [CAP, FX * P])
        xguT = sb("xguT", [P, FX, P], F32R)
        low_y = sb("low_y", [CAP, D])
        ye = sb("ye", [CAP, D])
        ident = sb("ident_f", [P, P])
        sig = sb("sig", [P, NT])
        w_top = sb("w_top", [P, NT, TOPK])
        slot_top = sb("slot_top", [P, NT, TOPK], I32)
        w_now = sb("w_now", [P, TOPK])
        slot_now = sb("slot_now", [P, TOPK], I32)
        tok_of_slot = sb("tok_of_slot", [P, E // 2], I32)
        tok_now = sb("tok_now", [P, 2], I32)
        free = wx_raw[:].rearrange("p s n -> p (s n)")
        used = [0]

        def take(n):
            used[0] += n
            return free[:, used[0] - n:used[0]]

        def by_tile(ap, n=E):
            return ap.rearrange("p (t e) -> p t e", e=n)

        PE_ = NT * E
        prob = by_tile(take(PE_))
        one_hot_flat, picked_flat = take(TOPK * PE_), take(TOPK * PE_)
        one_hot = one_hot_flat.rearrange("p (t k e) -> p t k e", k=TOPK, e=E)
        picked = picked_flat.rearrange("p (t k e) -> p t k e", k=TOPK, e=E)
        digit1 = one_hot_flat.bitcast(F16).rearrange("p (t n) -> p t n", t=NT)
        digit0 = picked_flat.bitcast(F16).rearrange("p (t n) -> p t n", t=NT)
        posm = by_tile(take(PE_))
        mask = take(PE_ // 2).bitcast(BF16)
        before = take(P // 2).bitcast(BF16)
        ones = take(P // 2).bitcast(BF16)
        top = take(NT * 8).rearrange("p (t k) -> p t k", k=8)
        c1 = prob
        pos_i, c0 = by_tile(rows[0][:].bitcast(I32)), by_tile(rows[1][:])
        top_i = sb("top_i", [P, NT, 8], U32)
        idx_f = sb("idx_f", [P, NT, TOPK])
        small = sb("small", [P, 4, NT])
        tables = sb("tables", [P, TABLE_COLS])
        iota8, iota_e = tables[:, 0:8], tables[:, 8:8 + E]
        token_id = tables[:, 8 + E:8 + E + NT]
        own_half = tables[:, 8 + E + NT:8 + E + 2 * NT]
        pos_k = sb("pos_k", [P, NT, TOPK])
        valid = sb("valid", [P, NT, TOPK])
        inv = sb("inv", [P, 2, 8, NT])
        inv_f = sb("inv_f", [P, 2, 8])
        inv_i = sb("inv_i", [P, 2, 8], I32)

        bankA = [ctx.enter_context(nc.psum_tensor(f"bankA{i}", [P, D], F32)) for i in range(2)]
        bankB = [ctx.enter_context(nc.psum_tensor(f"bankB{i}", [P, D], F32)) for i in range(2)]
        psXG = ctx.enter_context(nc.psum_tensor("psXG", [P, D], F32))
        psXU = ctx.enter_context(nc.psum_tensor("psXU", [P, D], F32))
        psT = ctx.enter_context(nc.psum_tensor("psT", [P, D], F32))
        psY = ctx.enter_context(nc.psum_tensor("psY", [P, D], F32))
        pair = [bankA, bankB, bankA]
        down_bank = [bankB[0], bankB[1], bankA[0], bankA[1]]

        x2_in, gb_in, table_in, hT_in, ws_in = sem("x2_in"), sem("gb_in"), sem("table_in"), sem("hT_in"), sem("ws_in")
        ws_hi, ws_lo = sem("ws_hi"), sem("ws_lo")
        gate_mm, up_mm, sil_done, gu_done = sem("gate_mm"), sem("up_mm"), sem("sil_done"), sem("gu_done")
        gu_hi, gu_lo = sem("gu_hi"), sem("gu_lo")
        dn_mm, dn_evac, dn_added, sig4_done = sem("dn_mm"), sem("dn_evac"), sem("dn_added"), sem("sig4_done")
        wx_in = [sem(f"wx_in{i}") for i in range(RAW_SLOTS)]
        wxg_hi, wxd_hi = sem("wxg_hi"), sem("wxd_hi")
        wxg_lo, wxd_lo = sem("wxg_lo"), sem("wxd_lo")
        tok_copied, rows_in = sem("tok_copied"), [sem(f"rows_in{i}") for i in range(2)]
        rows_mm, rows_hi, rows_lo = sem("rows_mm"), sem("rows_hi"), sem("rows_lo")
        xgu_mm, xlow, xsum, xadd = sem("xgu_mm"), sem("xlow"), sem("xsum"), sem("xadd")
        xsil, xgu_done = sem("xsil"), sem("xgu_done")
        mid_mm, mid_hi, mid_lo = sem("mid_mm"), sem("mid_hi"), sem("mid_lo")
        xd_mm, y_low, ye_add, ye_out = sem("xd_mm"), sem("y_low"), sem("ye_add"), sem("ye_out")
        slot_copied, w_copied = sem("slot_copied"), sem("w_copied")
        y_in = [[sem(f"y_in{i}{k}") for k in range(TOPK)] for i in range(2)]
        cm_step, cm_done, cb_added = sem("cm_step"), sem("cm_done"), sem("cb_added")
        r_chain, r_exp, r_pos, r_inv, r_consts = sem("r_chain"), sem("r_exp"), sem("r_pos"), sem("r_inv"), sem("r_consts")
        r_max, r_mask, r_digits, r_slots = sem("r_max"), sem("r_mask"), sem("r_digits"), sem("r_slots")
        tok_out, tok_in, out_done = sem("tok_out"), sem("tok_in"), sem("out_done")
        ident_a, ident_b = sem("ident_a"), sem("ident_b")

        waited_pool, waited_pe = sem("waited_pool_f"), sem("waited_pe_f")

        ye_rows = scr["ye"].rearrange("e c d -> (e c) d")
        h2_rows = scr["h2"].rearrange("b j p d -> (b j p) d")
        h2T_tiles = scr["h2T"].rearrange("b j p n -> p (b j) n")
        x2_tiles = scr["x2"].rearrange("b j p d -> p (b j) d")
        out_tiles = out.rearrange("b (j p) d -> p (b j) d", p=P)
        y_buf = [[free[:, (4 * i + k) * D:(4 * i + k + 1) * D] for k in range(TOPK)] for i in range(2)]
        cm = [free[:, (8 + i) * D:(9 + i) * D] for i in range(2)]
        gate_w, up_w, down_w = (slice(i * D, (i + 1) * D) for i in range(3))

        def raw_value(m, x):
            per_unit = 64
            return per_unit * x + sum(32 if k % 3 == 2 else 16 for k in range(m % RAW_SLOTS, m + 1, RAW_SLOTS))

        def tile_no(order, s, r):
            return 4 * (s - 2) + r if order is COMBINE4 else 2 * UNITS + 2 * s + r

        def tile_uses(order, s, r):
            return 2 * (s - 2) + r // 2 + 1 if order is COMBINE4 else UNITS + s + 1

        def tile_batch(order, s, r):
            return 0 if order is COMBINE4 else 1

        with nc.Block() as block:
            @block.sync
            def _(sp):
                sp.dma_start(tables[:], io["tables"]).then_inc(table_in, 16)

                def weights(g):
                    for c in range(chunks_of(g)):
                        n = GROUP * g + c
                        if n:
                            sp.wait_ge(ws_lo, n)
                        sp.dma_start(ws_raw[:], io["ws"][n]).then_inc(ws_in, 16)
                        if n == 0:
                            sp.dma_start(raw(hT[:].rearrange("p i s c t -> p i (s c t)")), h2T_tiles[:, 0:SUB, :])\
                              .then_inc(hT_in, 16)
                    if g == 0:
                        sp.dma_start(x2s[:], x2_tiles).then_inc(x2_in, 16)
                        sp.dma_start(gb[:], scr["gb"]).then_inc(gb_in, 16)

                def unit(g, s, order):
                    u = UNITS * g + s
                    if not (isinstance(u, int) and u == 0):
                        sp.wait_ge(up_mm, chunk_no(u, 0, g == NGROUPS - 1))
                        sp.dma_start(raw(hT[:].rearrange("p i s c t -> p i (s c t)")), h2T_tiles[:, bass.ds(s * SUB, SUB), :])\
                          .then_inc(hT_in, 16)
                    if order is ROUTING1:
                        sp.wait_ge(r_slots, 1)
                        sp.dma_start(scr["slots"].rearrange("(h p c) -> p h c", h=2, p=P), inv_i[:]).then_inc(tok_out, 16)
                        sp.wait_ge(tok_out, 16)
                        with nc.allow_non_contiguous_dma("2048 slot numbers, once"):
                            sp.dma_start(tok_of_slot[:], scr["slots"].rearrange("(n p) -> p n", p=P)).then_inc(tok_in, 16)
                        sp.wait_ge(tok_in, 16)
                    if order is WITH_X:
                        x = u - FIRST_X
                        for m in range(3 * XPU):
                            e, slot = x * XPU + m // 3, m % RAW_SLOTS
                            old = m - RAW_SLOTS
                            old_e = x * XPU + old // 3
                            if old % 3 == 2:
                                sp.wait_ge(wxd_lo, 2 + old_e + 1)
                            else:
                                sp.wait_ge(wxg_lo, 2 + 2 * old_e + old % 3 + 1)
                            if m % 3 < 2:
                                w = io["wg_x"] if m % 3 == 0 else io["wu_x"]
                                sp.dma_start(wx_raw[:, slot, 0:KC * F], w[e].rearrange("(p c) f -> p (c f)", c=KC))\
                                  .then_inc(wx_in[slot], 16)
                            else:
                                w, full = io["wd_x"][e], F // P
                                sp.dma_start(wx_raw[:, slot, 0:full * D].rearrange("p (c n) -> p c n", n=D),
                                             w[0:full * P].rearrange("(c p) n -> p c n", p=P)).then_inc(wx_in[slot], 16)
                                sp.dma_start(wx_raw[0:F - full * P, slot, full * D:FX * D], w[full * P:F])\
                                  .then_inc(wx_in[slot], 16)
                    if order is COMBINE2:
                        sp.wait_ge(dn_added, SUB * (u + 1))
                        sp.dma_start(out_tiles[:, bass.ds(s * SUB, SUB), :], x2s[:, bass.ds(s * SUB, SUB), :])\
                          .then_inc(out_done, 16)

                run_units(sp, unit, weights)
                sp.wait_ge(out_done, 16 * UNITS)

            @block.gpsimd
            def _(pool):
                pool.memset(ident[:], 0.0).then_inc(ident_a, 1)
                pool.memset(xgu[:, F:FX * P], 0.0).then_inc(r_consts, 1)
                pool.wait_ge(ident_a, 1)
                pool.affine_select(out=ident[:], in_=ident[:], compare_op=ALU.not_equal, fill=1.0, base=0,
                                   pattern=[[-1, P]], channel_multiplier=1).then_inc(ident_b, 1)
                pool.memset(ones, 1.0).then_inc(r_consts, 1)
                pool.wait_ge(x2_in, 16)

                def unit(g, s, order):
                    u = UNITS * g + s
                    for what, r in order:
                        if what == "gather":
                            x = u - FIRST_X
                            if r == 0:
                                pool.wait_ge(rows_mm, 1 + 2 * x)
                                pool.wait_ge(tok_in, 16)
                                pool.tensor_copy(tok_now[:], tok_of_slot[:, bass.ds(x * 2, 2)]).then_inc(tok_copied, 1)
                                pool.wait_ge(tok_copied, x + 1)
                                pool.sem_inc(waited_pool, 1)
                            pool.indirect_dma_start(rows[r][:], None, h2_rows,
                                                    bass.IndirectOffsetOnAxis(tok_now[:, r:r + 1], 0))\
                                .then_inc(rows_in[r], 16)
                        elif what == "down":
                            i = s * SUB + r
                            pool.wait_ge(dn_evac, SUB * u + r + 1)
                            if r == 0 and not (isinstance(u, int) and u == 0):
                                pool.wait_ge(dn_added, SUB * u)
                            if r == 0 and order is COMBINE4:
                                pool.wait_ge(cb_added, tile_no(order, s, 2) + 1)
                            if r == 0 and order is COMBINE2:
                                pool.wait_ge(cb_added, tile_no(order, s, 1) + 1)
                            pool.tensor_tensor(x2s[:, i], x2s[:, i], dn_tmp[r % 2][:], ALU.add).then_inc(dn_added, 1)
                        elif what == "fetch":
                            i = tile_no(order, s, r)
                            if r == 0:
                                pool.wait_ge(wxg_lo, 2 + 2 * E)
                                pool.wait_ge(wxd_lo, 2 + E)
                            pool.wait_ge(cm_done, i + 1)
                            if r:
                                pool.wait_ge(y_in[1 - r % 2][TOPK - 1], 16 * tile_uses(order, s, r - 1))
                            pool.tensor_copy(slot_now[:], slot_top[:, i, :]).then_inc(slot_copied, 1)
                            pool.wait_ge(ye_out, 16 * (E + 1))
                            pool.wait_ge(slot_copied, i + 1)
                            pool.sem_inc(waited_pool, 1)
                            for k in range(TOPK):
                                pool.indirect_dma_start(y_buf[r % 2][k], None, ye_rows,
                                                        bass.IndirectOffsetOnAxis(slot_now[:, k:k + 1], 0))\
                                    .then_inc(y_in[r % 2][k], 16)
                        elif what == "combine":
                            i = tile_no(order, s, r)
                            pool.wait_ge(cm_done, 3 + i)
                            pool.wait_ge(dn_added, SUB * u + (SUB if r == 3 else 0))
                            pool.tensor_tensor(x2s[:, i], x2s[:, i], cm[r % 2], ALU.add).then_inc(cb_added, 1)

                run_units(pool, unit, lambda g: None)

            @block.scalar
            def _(act):
                act.sem_inc(ye_out, 16)

                def weights(g):
                    for c in range(chunks_of(g)):
                        act.wait_ge(ws_in, 16 * (GROUP * g + c + 1))
                        if g:
                            act.wait_ge(dn_mm, NT * g)
                        nc.scalar.copy(ws[c][:, 0], ws_raw[:]).then_inc(ws_hi, 1)

                def unit(g, s, order):
                    u, x = UNITS * g + s, UNITS * g + s - FIRST_X
                    e0 = x * XPU
                    for what, r in order:
                        q, e = chunk_no(u, r, g == NGROUPS - 1), e0 + r
                        if what == "gate":
                            act.wait_ge(gate_mm, q + 1)
                            if not (isinstance(q, int) and q == 0):
                                act.wait_ge(gu_done, q)
                            nc.scalar.activation(sil[:], pair[r][0][:], ACT.Silu).then_inc(sil_done, 1)
                        elif what == "up":
                            act.wait_ge(gu_done, q + 1)
                            if not (isinstance(u, int) and u == 0):
                                act.wait_ge(dn_mm, SUB * u)
                            nc.scalar.copy(guT[r][:, 0], gu[:]).then_inc(gu_hi, 1)
                        elif what == "route" and r == 0:
                            act.wait_ge(r_max, 1)
                            nc.scalar.activation(prob, prob, ACT.Exp).then_inc(r_exp, 1)
                            nc.scalar.activation(sig[:], logits[:, :, E], ACT.Sigmoid).then_inc(r_exp, 1)
                        elif what == "split_gu":
                            act.wait_ge(xgu_mm, 1 + e)
                            for i in range(2):
                                act.wait_ge(wx_in[(3 * r + i) % RAW_SLOTS], raw_value(3 * r + i, x))
                                nc.scalar.copy(wx[i][:, 0, 0:KC * F], wx_raw[:, (3 * r + i) % RAW_SLOTS, 0:KC * F])\
                                    .then_inc(wxg_hi, 1)
                        elif what == "split_d":
                            act.wait_ge(xd_mm, 1 + e)
                            slot = (3 * r + 2) % RAW_SLOTS
                            act.wait_ge(wx_in[slot], raw_value(3 * r + 2, x))
                            nc.scalar.copy(wx[2][:, 0], wx_raw[:, slot]).then_inc(wxd_hi, 1)
                        elif what == "rows":
                            act.wait_ge(rows_mm, 1 + 2 * x + r + 1)
                            act.wait_ge(xgu_mm, 1 + e0)
                            nc.scalar.copy(xs[r][:].rearrange("p h c m -> p c h m")[:, :, :, 0:CAP],
                                           psT[:].rearrange("p (c h m) -> p c h m", c=KC, h=2)).then_inc(rows_hi, 1)
                        elif what == "gu":
                            act.wait_ge(xgu_mm, 1 + e + 1)
                            act.wait_ge(xadd, 1 + e)
                            nc.scalar.copy(low_g[:], psXG[CAP:P, 0:F]).then_inc(xlow, 1)
                            nc.scalar.copy(low_u[:], psXU[CAP:P, 0:F]).then_inc(xlow, 1)
                            act.wait_ge(xsum, e + 1)
                            nc.scalar.activation(xg[:], xg[:], ACT.Silu).then_inc(xsil, 1)
                        elif what == "mid":
                            act.wait_ge(mid_mm, 1 + e + 1)
                            act.wait_ge(xd_mm, 1 + e)
                            nc.scalar.copy(xguT[:, :, 0:CAP], psT[:, 0:FX * CAP].rearrange("p (c m) -> p c m", c=FX))\
                                .then_inc(mid_hi, 1)
                        elif what == "exp_down":
                            act.wait_ge(xd_mm, 1 + e + 1)
                            act.wait_ge(ye_add, 1 + e)
                            nc.scalar.copy(low_y[:], psY[CAP:P, :]).then_inc(y_low, 1)
                            act.wait_ge(ye_add, 1 + e + 1)
                            act.dma_start(scr["ye"][e], ye[:]).then_inc(ye_out, 16)

                run_units(act, unit, weights)

            @block.vector
            def _(dve):
                for s_, v_ in ((wxg_lo, 2), (wxd_lo, 2), (rows_lo, 1), (xadd, 1), (xgu_done, 1), (mid_lo, 1),
                               (ye_add, 1), (cm_done, 2)):
                    dve.sem_inc(s_, v_)
                links = [0]

                def link(ins):
                    links[0] += 1
                    ins.then_inc(r_chain, 1)
                    dve.wait_ge(r_chain, links[0])

                def weights(g):
                    for c in range(chunks_of(g)):
                        dve.wait_ge(ws_hi, GROUP * g + c + 1)
                        nc.vector.tensor_tensor(ws[c][:, 1], ws_raw[:], raw(ws[c][:, 0]), ALU.subtract).then_inc(ws_lo, 1)

                def route(r):
                    v = nc.vector
                    if r == 0:
                        dve.wait_ge(table_in, 16)
                        link(v.memset(free[:, used[0]:RAW_SLOTS * FX * D], 0.0))
                        link(v.reduce_max(small[:, 0], logits[:, :, 0:E], mybir.AxisListType.X))
                        v.tensor_tensor(prob, logits[:, :, 0:E], small[:, 0].unsqueeze(2).broadcast_to((P, NT, E)),
                                        ALU.subtract).then_inc(r_max, 1)
                        dve.wait_ge(r_exp, 1)
                        link(v.reduce_sum(small[:, 1], prob, mybir.AxisListType.X))
                        link(v.reciprocal(small[:, 2], small[:, 1]))
                        link(v.tensor_tensor(prob, prob, small[:, 2].unsqueeze(2).broadcast_to((P, NT, E)), ALU.mult))
                        for t in range(NT):
                            last = v.max(top[:, t], prob[:, t])
                        link(last)
                        for t in range(NT):
                            last = v.max_index(top_i[:, t], top[:, t], prob[:, t])
                        link(last)
                    elif r == 1:
                        link(v.tensor_copy(idx_f[:], top_i[:, :, 0:TOPK]))
                        link(v.tensor_tensor(one_hot, idx_f[:].unsqueeze(3).broadcast_to((P, NT, TOPK, E)),
                                             iota_e.unsqueeze(1).unsqueeze(1).broadcast_to((P, NT, TOPK, E)), ALU.is_equal))
                        link(v.tensor_copy(before, tables[:, TABLE_COLS - P:TABLE_COLS]))
                        with nc.allow_low_precision("zeros and ones"):
                            v.tensor_reduce(by_tile(mask), one_hot.rearrange("p t k e -> p t e k"),
                                            axis=mybir.AxisListType.X, op=ALU.add).then_inc(r_mask, 1)
                    elif r == 2:
                        dve.wait_ge(r_pos, 1)
                        dve.wait_ge(r_mask, 1)
                        pos = by_tile(psXG[:])
                        link(v.tensor_tensor(picked, one_hot, pos.unsqueeze(2).broadcast_to((P, NT, TOPK, E)), ALU.mult))
                        link(v.tensor_reduce(pos_k[:], picked, axis=mybir.AxisListType.X, op=ALU.add))
                        link(v.tensor_scalar(valid[:], pos_k[:], float(CAP), None, ALU.is_lt))
                        link(v.tensor_scalar(pos_k[:], pos_k[:], float(CAP - 1), None, ALU.min))
                        link(v.scalar_tensor_tensor(pos_k[:], idx_f[:], float(CAP), pos_k[:], ALU.mult, ALU.add))
                        link(v.tensor_copy(slot_top[:], pos_k[:]))
                        link(v.reduce_sum(small[:, 3], top[:, :, 0:TOPK], mybir.AxisListType.X))
                        link(v.reciprocal(small[:, 1], small[:, 3]))
                        link(v.tensor_tensor(valid[:], valid[:], top[:, :, 0:TOPK], ALU.mult))
                        link(v.tensor_tensor(w_top[:], valid[:], small[:, 1].unsqueeze(2).broadcast_to((P, NT, TOPK)),
                                             ALU.mult))
                        link(v.scalar_tensor_tensor(posm, pos, 1.0, by_tile(mask), ALU.add, ALU.mult))
                        link(v.tensor_scalar(posm, posm, -1.0, None, ALU.add))
                        link(v.tensor_copy(pos_i, posm))
                        link(v.tensor_scalar(c1.bitcast(I32), pos_i, 3, None, ALU.arith_shift_right))
                        link(v.tensor_scalar(pos_i, pos_i, 7, None, ALU.bitwise_and))
                        link(v.tensor_copy(posm, c1.bitcast(I32)))
                        link(v.tensor_copy(c0, pos_i))
                    elif r == 3:
                        shape = (P, PE_, S1)
                        digit = lambda d: d.rearrange("p t (e c) -> p (t e) c", c=S1)
                        flat = lambda a: a.rearrange("p t e -> p (t e)").unsqueeze(2).broadcast_to(shape)
                        link(v.tensor_tensor(digit(digit1), flat(posm), iota8.unsqueeze(1).broadcast_to(shape), ALU.is_equal))
                        link(v.tensor_tensor(digit(digit0), flat(c0), iota8.unsqueeze(1).broadcast_to(shape), ALU.is_equal))
                        v.tensor_tensor(digit0, digit0, token_id.unsqueeze(2).broadcast_to((P, NT, E * S1)), ALU.mult)\
                            .then_inc(r_digits, 1)
                    else:
                        dve.wait_ge(r_inv, 1)
                        for h in range(2):
                            src = (psXG if h == 0 else psXU)[:, 0:P].rearrange("p (e c) -> p c e", c=S1)
                            link(v.tensor_tensor(inv[:, h], src, own_half.unsqueeze(1).broadcast_to((P, S1, NT)), ALU.mult))
                        link(v.tensor_reduce(inv_f[:], inv[:], axis=mybir.AxisListType.X, op=ALU.add))
                        v.tensor_copy(inv_i[:], inv_f[:]).then_inc(r_slots, 1)

                def unit(g, s, order):
                    u, x = UNITS * g + s, UNITS * g + s - FIRST_X
                    e0 = x * XPU
                    for what, r in order:
                        q, e = chunk_no(u, r, g == NGROUPS - 1), e0 + r
                        if what == "up":
                            dve.wait_ge(up_mm, q + 1)
                            dve.wait_ge(sil_done, q + 1)
                            if not (isinstance(q, int) and q == 0):
                                dve.wait_ge(gu_hi, q)
                                dve.wait_ge(gu_lo, q)
                            nc.vector.tensor_tensor(gu[:], sil[:], pair[r][1][:], ALU.mult).then_inc(gu_done, 1)
                            dve.wait_ge(gu_hi, q + 1)
                            nc.vector.tensor_tensor(guT[r][:, 1], gu[:], raw(guT[r][:, 0]), ALU.subtract).then_inc(gu_lo, 1)
                        elif what == "down":
                            if r == 0:
                                dve.wait_ge(r_exp, 2)
                                if g == 0 and isinstance(s, int) and s == 0:
                                    dve.wait_ge(gb_in, 16)
                                else:
                                    dve.wait_ge(dn_evac, SUB * u)
                                nc.vector.tensor_copy(sig4[:], sig[:, bass.ds(s * SUB, SUB)]).then_inc(sig4_done, 1)
                                dve.wait_ge(sig4_done, u + 1)
                            dve.wait_ge(dn_mm, SUB * u + r + 1)
                            if not (isinstance(u, int) and u == 0 and r < 2):
                                dve.wait_ge(dn_added, SUB * u + r - 1)
                            nc.vector.scalar_tensor_tensor(dn_tmp[r % 2][:], down_bank[r][:], sig4[:, r:r + 1],
                                                           gb[:, s // 2, :], ALU.mult, ALU.mult).then_inc(dn_evac, 1)
                        elif what == "route":
                            route(r)
                        elif what == "split_gu":
                            for i in range(2):
                                dve.wait_ge(wxg_hi, 2 * e + i + 1)
                                nc.vector.tensor_tensor(wx[i][:, 1, 0:KC * F], wx_raw[:, (3 * r + i) % RAW_SLOTS, 0:KC * F],
                                                        raw(wx[i][:, 0, 0:KC * F]), ALU.subtract).then_inc(wxg_lo, 1)
                        elif what == "split_d":
                            dve.wait_ge(wxd_hi, e + 1)
                            nc.vector.tensor_tensor(wx[2][:, 1], wx_raw[:, (3 * r + 2) % RAW_SLOTS], raw(wx[2][:, 0]),
                                                    ALU.subtract).then_inc(wxd_lo, 1)
                        elif what == "rows":
                            dve.wait_ge(rows_hi, 2 * x + r + 1)
                            v = xs[r][:].rearrange("p h c m -> p c h m")
                            nc.vector.tensor_tensor(v[:, :, :, CAP:P], psT[:].rearrange("p (c h m) -> p c h m", c=KC, h=2),
                                                    raw(v[:, :, :, 0:CAP]), ALU.subtract).then_inc(rows_lo, 1)
                        elif what == "gu":
                            dve.wait_ge(xlow, 2 * e + 2)
                            dve.wait_ge(xgu_done, 1 + e)
                            nc.vector.tensor_tensor(xg[:], psXG[0:CAP, 0:F], low_g[:], ALU.add).then_inc(xsum, 1)
                            nc.vector.tensor_tensor(xu[:], psXU[0:CAP, 0:F], low_u[:], ALU.add).then_inc(xadd, 1)
                            dve.wait_ge(xsil, e + 1)
                            dve.wait_ge(xadd, 1 + e + 1)
                            dve.wait_ge(mid_mm, 1 + e)
                            nc.vector.tensor_tensor(xgu[:, 0:F], xg[:], xu[:], ALU.mult).then_inc(xgu_done, 1)
                        elif what == "mid":
                            dve.wait_ge(mid_hi, e + 1)
                            nc.vector.tensor_tensor(xguT[:, :, CAP:P], psT[:, 0:FX * CAP].rearrange("p (c m) -> p c m", c=FX),
                                                    raw(xguT[:, :, 0:CAP]), ALU.subtract).then_inc(mid_lo, 1)
                        elif what == "exp_down":
                            dve.wait_ge(y_low, e + 1)
                            dve.wait_ge(ye_out, 16 * (1 + e))
                            nc.vector.tensor_tensor(ye[:], psY[0:CAP, :], low_y[:], ALU.add).then_inc(ye_add, 1)
                        elif what == "combine":
                            i = tile_no(order, s, r)
                            nc.vector.tensor_copy(w_now[:], w_top[:, i, :]).then_inc(w_copied, 1)
                            dve.wait_ge(w_copied, i + 1)
                            dve.wait_ge(y_in[r % 2][0], 16 * tile_uses(order, s, r))
                            if r >= 2:
                                dve.wait_ge(cb_added, i - 1)
                            nc.vector.tensor_scalar(cm[r % 2], y_buf[r % 2][0], w_now[:, 0:1], None, ALU.mult)\
                                .then_inc(cm_step, 1)
                            for k in range(1, TOPK):
                                dve.wait_ge(cm_step, TOPK * i + k)
                                dve.wait_ge(y_in[r % 2][k], 16 * tile_uses(order, s, r))
                                nc.vector.scalar_tensor_tensor(cm[r % 2], y_buf[r % 2][k], w_now[:, k:k + 1], cm[r % 2],
                                                               ALU.mult, ALU.add).then_inc(cm_step, 1)
                            dve.wait_ge(cm_step, TOPK * (i + 1))
                            nc.vector.tensor_tensor(cm[r % 2], cm[r % 2], gb[:, tile_batch(order, s, r), :], ALU.mult)\
                                .then_inc(cm_done, 1)

                run_units(dve, unit, weights)

            @block.tensor
            def _(pe):
                for s_ in (rows_mm, xgu_mm, mid_mm, xd_mm):
                    pe.sem_inc(s_, 1)

                def product(out_, pairs):
                    passes = [(l[i], r[k]) for l, r in pairs for i, k in ((0, 0), (0, 1), (1, 0))]
                    for n, (l, r) in enumerate(passes):
                        last = nc.tensor.matmul(out_, l, r, start=n == 0, stop=n == len(passes) - 1)
                    return last

                def halves(ap, cols):
                    return ap[:, 0, cols], ap[:, 1, cols]

                def in_unit(part, c):
                    return hT[:, :, part, c, :]

                pe.wait_ge(ident_b, 1)

                def unit(g, s, order):
                    u, x = UNITS * g + s, UNITS * g + s - FIRST_X
                    e0, nch = x * XPU, chunks_of(g)
                    first = isinstance(u, int) and u == 0
                    for what, r in order:
                        q, e = chunk_no(u, r, g == NGROUPS - 1), e0 + r
                        if what in ("gate", "up"):
                            which = 0 if what == "gate" else 1
                            if what == "gate":
                                pe.wait_ge(ws_lo, GROUP * g + r + 1)
                                if r == 0:
                                    pe.wait_ge(hT_in, 16 * (u + 1))
                            if r == 0 and not first:
                                pe.wait_ge(dn_evac, SUB * u - 1 + which)
                            if r == 2:
                                pe.wait_ge(gu_done, q - 1)
                            product(pair[r][which][:],
                                    [(halves(ws[r][:], slice(which * D + c * P, which * D + (c + 1) * P)),
                                      (in_unit(0, c), in_unit(1, c))) for c in range(KC)])\
                                .then_inc(gate_mm if which == 0 else up_mm, 1)
                        elif what == "down":
                            if r == 0:
                                pe.wait_ge(gu_lo, chunk_no(u, nch, g == NGROUPS - 1))
                            product(down_bank[r][:], [(halves(guT[c][:], slice(r * P, (r + 1) * P)), halves(ws[c][:], down_w))
                                                      for c in range(nch)]).then_inc(dn_mm, 1)
                        elif what == "route" and r == 1:
                            pe.wait_ge(r_mask, 1)
                            pe.wait_ge(r_consts, 2)
                            nc.tensor.matmul(psXG[:], before, mask, start=True, stop=False)
                            for t in range(NT - 1):
                                left = NT - 1 - t
                                last = nc.tensor.matmul(psXG[:, (t + 1) * E:NT * E], ones,
                                                        mask[:, t * E:(t + 1) * E].unsqueeze(1).broadcast_to((P, left, E)),
                                                        start=False, stop=t == NT - 2)
                            last.then_inc(r_pos, 1)
                        elif what == "route" and r == 3:
                            pe.wait_ge(r_digits, 1)
                            for h, ps in ((0, psXG), (1, psXU)):
                                for t in range(NT):
                                    last = nc.tensor.matmul(ps[:, 0:P], digit1[:, t, h * P:(h + 1) * P],
                                                            digit0[:, t, h * P:(h + 1) * P], start=t == 0, stop=t == NT - 1)
                            last.then_inc(r_inv, 1)
                        elif what == "rows":
                            pe.wait_ge(rows_in[r], 16 * (x + 1))
                            pe.wait_ge(mid_lo, 1 + e0 + 2 * r)
                            v = rows[r][:].rearrange("t (q c) -> t c q", c=KC)
                            for c in range(KC):
                                last = nc.tensor.transpose(psT[:, c * P:(c + 1) * P], v[:, c, :], ident[:])
                            last.then_inc(rows_mm, 1)
                        elif what == "gu":
                            pe.wait_ge(rows_lo, 1 + 2 * x + r // 2 + 1)
                            pe.wait_ge(wxg_lo, 2 + 2 * (e + 1))
                            pe.wait_ge(xadd, 1 + e)
                            for c in range(KC):
                                for ps, w in ((psXG, wx[0]), (psXU, wx[1])):
                                    for part in range(2):
                                        last = nc.tensor.matmul(ps[:, 0:F], xs[r // 2][:, r % 2, c, :],
                                                                w[:, part, c * F:(c + 1) * F],
                                                                start=c == 0 and part == 0, stop=c == KC - 1 and part == 1)
                            last.then_inc(xgu_mm, 1)
                        elif what == "mid":
                            pe.wait_ge(xgu_done, 1 + e + 1)
                            if r in (0, 2):
                                pe.wait_ge(rows_lo, 1 + 2 * x + r // 2 + 1)
                            else:
                                pe.wait_ge(mid_lo, 1 + e)
                            pe.sem_inc(waited_pe, 1)
                            for c in range(FX):
                                last = nc.tensor.transpose(psT[:, c * CAP:(c + 1) * CAP], xgu[:, c * P:(c + 1) * P],
                                                           ident[0:CAP, 0:CAP])
                            last.then_inc(mid_mm, 1)
                        elif what == "exp_down":
                            pe.wait_ge(mid_lo, 1 + e + 1)
                            pe.wait_ge(wxd_lo, 2 + e + 1)
                            pe.wait_ge(ye_add, 1 + e)
                            for c in range(FX):
                                k = min(P, F - c * P)
                                for part in range(2):
                                    last = nc.tensor.matmul(psY[:], xguT[0:k, c, :], wx[2][0:k, part, c * D:(c + 1) * D],
                                                            start=c == 0 and part == 0, stop=c == FX - 1 and part == 1)
                            last.then_inc(xd_mm, 1)

                run_units(pe, unit, lambda g: None)


def adaln_block(nc, ins, out):
    scr = {
        "ye": nc.dram_tensor("ye_scratch", (E, CAP, D), F32).ap(),
        "slots": nc.dram_tensor("slots_scratch", (E * CAP,), I32).ap(),
        "gb": nc.dram_tensor("gb_scratch", (P, B, D), F32).ap(),
        "x2": nc.dram_tensor("x2_scratch", (B, TPB, P, D), F32).ap(),
        "h2": nc.dram_tensor("h2_scratch", (B, TPB, P, D), F32).ap(),
        "h2T": nc.dram_tensor("h2T_scratch", (B, TPB, P, 2 * D), F32).ap(),
    }
    with ExitStack() as ctx:
        logits = ctx.enter_context(nc.sbuf_tensor("logits", [P, NT, RW], F32))
        attention(nc, {**ins, "logits": logits}, scr)
        ffn(nc, {**ins, "logits": logits}, scr, out)


_OUTS = [((B, T, D), "float32")]


def _layout(inputs):
    import numpy as np
    a = {k: np.asarray(v) for k, v in inputs.items()}
    pos = np.arange(T, dtype=np.float32)
    inv = (1.0 / 10000.0 ** (np.arange(0, DK, 2, dtype=np.float32) / DK)).astype(np.float32)
    ang = (pos[:, None] * inv[None, :]).astype(np.float32)
    cos = np.repeat(np.cos(ang), 2, axis=1).astype(np.float32)
    sin = np.repeat(np.sin(ang), 2, axis=1).astype(np.float32)
    sin[:, 1::2] *= -1
    per_tile = lambda t: np.ascontiguousarray(t.reshape(TPB, P, DK).transpose(1, 0, 2))
    rows, cols = np.arange(P)[:, None] // DK, np.concatenate([np.arange(P) // DK, np.arange(HG)])[None]
    d = {
        "x": a["L0_attn_x"],
        "c": np.ascontiguousarray(a["L0_c"].reshape(B, P, KC).transpose(1, 2, 0)),
        "wmod": a["L0_wmod"],
        "cos": per_tile(cos), "sin": per_tile(sin), "mask": (rows == cols).astype(np.float32),
        "wr": np.concatenate([a["L0_ffn_Wr"], a["L0_ffn_Wse"], np.zeros((D, 1), np.float32)], axis=1),
    }
    gate_up = lambda w: w.reshape(P, KC, FCH, P).transpose(2, 0, 1, 3).reshape(FCH, P, D)
    d["ws"] = np.ascontiguousarray(np.concatenate(
        [gate_up(a["L0_ffn_Wsg"]), gate_up(a["L0_ffn_Wsu"]), a["L0_ffn_Wsd"].reshape(FCH, P, D)], axis=2))
    d["wg_x"], d["wu_x"], d["wd_x"] = a["L0_ffn_Wg"], a["L0_ffn_Wu"], a["L0_ffn_Wd"]
    const = lambda row: np.broadcast_to(np.asarray(row, np.float32), (P, len(row)))
    p = np.arange(P)[:, None]
    d["tables"] = np.ascontiguousarray(np.concatenate(
        [const(range(8)), const(range(E)), p + P * np.arange(NT)[None], p // 8 == np.arange(NT)[None],
         p < np.arange(P)[None]], axis=1).astype(np.float32))
    for n in "kvqgo":
        d[f"w{n}"] = np.ascontiguousarray(a[f"L0_attn_W{n}"].T)
        d[f"b{n}"] = a[f"L0_attn_b{n}"]
    return d


def kernel(**inputs):
    import numpy as _np
    import concourse.bacc as _bacc
    from concourse.bass_utils import run_bass_kernel_spmd as _run

    nc = _bacc.Bacc("TRN2", target_bir_lowering=False, num_devices=1)
    arrays, ins = {}, {}
    for name, a in _layout(inputs).items():
        arrays[f"in_{name}"] = a
        ins[name] = nc.dram_tensor(f"in_{name}", a.shape, mybir.dt.from_np(a.dtype), kind="ExternalInput").ap()
    shape, dtype = _OUTS[0]
    out = nc.dram_tensor("out_0", shape, mybir.dt.from_np(_np.dtype(dtype)), kind="ExternalOutput").ap()
    adaln_block(nc, ins, out)
    r = _run(nc, [arrays], core_ids=[0])
    return r.results[0]["out_0"]
```

```python
import concourse.bass as bass
from concourse import mybir
from contextlib import ExitStack

F32 = mybir.dt.float32
F32R = mybir.dt.float32r
BF16 = mybir.dt.bfloat16
F16 = mybir.dt.float16
I32 = mybir.dt.int32
U32 = mybir.dt.uint32
ALU = mybir.AluOpType
ACT = mybir.ActivationFunctionType

P = 128
B, T, D = 2, 1024, 512
H, DK = 16, 32
CS = 64
KC = D // P
TPB = T // P
NT = B * TPB
HG = P // DK
NG = H // HG
SW = P + HG
LN_EPS = 1e-5
DEN_EPS = 1e-6
E, TOPK, CAP = 32, 4, 64
RW = E + 2
F, FS = 352, 1408


def raw(ap):
    return ap.bitcast(F32)


def lag(j, b, d):
    return j + (b - d) // 2, (b - d) % 2


def real(j, b, d):
    return not isinstance(j, int) or 0 <= 2 * j + b - d < NT


def done(j, b, d=0, per=1, k=None):
    return per * (2 * j + b - d) + (per if k is None else k)


def wait_tile(eng, sem, j, b, d=0, per=1, k=None):
    if real(j, b, d):
        value = done(j, b, d, per, k)
        if not (isinstance(value, int) and value <= 0):
            eng.wait_ge(sem, value)


STATIC_HEAD = [(-1, 0), (-1, 1), (0, 0), (0, 1), (1, 0), (1, 1)]
LOOP_J = (2, 7)
STATIC_TAIL = [(7, 0), (7, 1), (8, 0), (8, 1), (9, 0)]


def run_steps(eng, step):
    for j, b in STATIC_HEAD:
        step(j, b)
    with eng.Fori(*LOOP_J) as j:
        step(j, 0)
        step(j, 1)
    for j, b in STATIC_TAIL:
        step(j, b)


def attention(nc, io, scr):
    with ExitStack() as ctx:
        def sb(name, shape, dt=F32):
            return ctx.enter_context(nc.sbuf_tensor(name, shape, dt))

        def sem(name):
            return ctx.enter_context(nc.semaphore(name))

        logits, ident = io["logits"], io["ident"]
        wnames = ["k", "v", "q", "g", "o"]
        w_hi = {n: sb(f"w{n}_hi", [P, KC, D], F32R) for n in wnames}
        w_lo = {n: sb(f"w{n}_lo", [P, KC, D], F32R) for n in wnames}
        wr_hi, wr_lo = sb("wr_hi", [P, KC, RW], F32R), sb("wr_lo", [P, KC, RW], F32R)
        group_mask = sb("group_mask", [P, SW])
        c_silu = sb("c_silu", [P, KC, B, P // B])
        cT = sb("cT", [P, KC, B])
        cS = sb("cS", [P, KC, B])
        mod = {n: sb(f"mod_{n}", [P, B, D]) for n in ("sa", "ca1", "ga", "gabo", "sb", "cb1")}
        bias_k, bias_v, bias_q, bias_g = (sb(f"bias_{n}", [P, D]) for n in "kvqg")
        cos_t, sin_t = sb("cos_t", [P, TPB, DK]), sb("sin_t", [P, TPB, DK])
        NSTAGE = 3
        scratch = sb("scratch", [P, NSTAGE * KC * D])
        stage = [scratch[:, s * KC * D:(s + 1) * KC * D] for s in range(NSTAGE)]
        y = scratch[:, 0:2 * D]
        t1 = scratch[:, 2 * D:4 * D]
        t2 = scratch[:, 4 * D:6 * D]
        qk = {"q": slice(0, D), "k": slice(D, 2 * D)}
        feat = [scratch[:, 6 * D:8 * D], scratch[:, 8 * D:10 * D]]
        o_buf = scratch[:, 10 * D:11 * D]
        o1_buf = scratch[:, 11 * D:12 * D]
        xin = [sb(f"xin{i}", [P, D]) for i in range(2)]
        xhat = sb("xhat", [P, D])
        h_buf = [sb(f"h{i}", [P, D]) for i in range(2)]
        hT = [sb(f"hT{i}", [P, 2, KC, P], F32R) for i in range(2)]
        v_buf = [sb(f"v{i}", [P, NG, SW]) for i in range(2)]
        th = [sb(f"th{i}", [P, D]) for i in range(2)]
        qT = sb("qT", [P, NG, P])
        state = [[sb(f"state{b}{c}", [P, NG, SW]) for c in range(2)] for b in range(2)]
        blocks = [sb(f"blocks{c}", [P, NG, SW]) for c in range(2)]
        rden = sb("rden", [P, H])
        rden2 = sb("rden2", [P, H])
        oT = sb("oT", [P, 2, KC, P], F32R)
        xres = [sb(f"xres{i}", [P, D]) for i in range(2)]
        proj = sb("proj", [P, D])
        x2 = [sb(f"x2_{i}", [P, D]) for i in range(2)]
        xhat2 = proj
        h2_both = sb("h2_both", [P, B, D])
        h2 = [h2_both[:, i, :] for i in range(2)]
        proj_gb = h2_both
        h2T = sb("h2T", [P, 2, KC, P], F32R)
        st1, st2 = sb("st1", [P, 6]), sb("st2", [P, 6])
        mv1, mv2 = [sb(f"mv1_{i}", [P, 2]) for i in range(2)], [sb(f"mv2_{i}", [P, 2]) for i in range(2)]
        rs1, rs2 = [sb(f"rs1_{i}", [P, 2]) for i in range(2)], [sb(f"rs2_{i}", [P, 2]) for i in range(2)]
        minus_half = sb("minus_half", [P, 1])

        bank = [ctx.enter_context(nc.psum_tensor(f"bank{i}", [P, D], F32)) for i in range(4)]
        psS = ctx.enter_context(nc.psum_tensor("psS", [P, 2, 512], F32))
        psN = ctx.enter_context(nc.psum_tensor("psN", [P, 2, 512], F32))

        waited_pool, waited_dve, waited_sp = (io[f"waited_{e}"] for e in ("pool", "dve", "sp"))
        small_in = sem("small_in")
        stage_in = [sem(f"stage_in{s}") for s in range(NSTAGE)]
        hi_done, lo_done = sem("hi_done"), sem("lo_done")
        const_ready = sem("const_ready")
        csilu_act, csilu_ready = sem("csilu_act"), sem("csilu_ready")
        mod_mm, mod_tmp = sem("mod_mm"), sem("mod_tmp")
        mod_ready = sem("mod_ready")
        gb_out = sem("gb_out")
        x_in = [sem(f"x_in{i}") for i in range(2)]
        xres_in = [sem(f"xres_in{i}") for i in range(2)]
        st1_done, mv1_done, rs1_a, rs1_done = sem("st1_done"), sem("mv1_done"), sem("rs1_a"), sem("rs1_done")
        xhat_done, h_a, h_done = sem("xhat_done"), sem("h_a"), sem("h_done")
        hT_mm, hT_hi, hT_lo = sem("hT_mm"), sem("hT_hi"), sem("hT_lo")
        k_mm, v_mm, q_mm, g_mm = sem("k_mm"), sem("v_mm"), sem("q_mm"), sem("g_mm")
        k_out, v_out, q_out, g_out = sem("k_out"), sem("v_out"), sem("q_out"), sem("g_out")
        tanh_done = sem("tanh_done")
        rope_cos, rope_sin, rope_done, relu_done, exp_done, feat_done = (
            {n: sem(f"{what}_{n}") for n in "qk"}
            for what in ("rope_cos", "rope_sin", "rope_done", "relu_done", "exp_done", "feat_done"))
        qT_mm, qT_done = sem("qT_mm"), sem("qT_done")
        s_mm, state_done, blocks_done = sem("s_mm"), sem("state_done"), sem("blocks_done")
        n_mm = sem("n_mm")
        den_a, den_done, o_half, o_done = sem("den_a"), sem("den_done"), sem("o_half"), sem("o_done")
        oT_mm, oT_hi, oT_lo = sem("oT_mm"), sem("oT_hi"), sem("oT_lo")
        o_mm, proj_done, xg_done, x2_done = sem("o_mm"), sem("proj_done"), sem("xg_done"), sem("x2_done")
        st2_done, mv2_done, rs2_a, rs2_done = sem("st2_done"), sem("mv2_done"), sem("rs2_a"), sem("rs2_done")
        xhat2_done, h2_a, h2_done = sem("xhat2_done"), sem("h2_a"), sem("h2_done")
        h2T_mm, h2T_hi, h2T_lo = sem("h2T_mm"), sem("h2T_hi"), sem("h2T_lo")
        r_mm, logits_done = sem("r_mm"), sem("logits_done")
        x2_out = [sem(f"x2_out{i}") for i in range(2)]
        h2_out = [sem(f"h2_out{i}") for i in range(2)]
        h2T_out = sem("h2T_out")

        MODS = ["sa", "ca", "ga", "sb", "cb", "gb"]
        jobs = ["sa", "ca", "k", "v", "q", "g", "ga", "o", "cb", "sb", "gb"]
        mod_no = {n: i for i, n in enumerate(x for x in jobs if x in MODS)}
        split_no = {n: i for i, n in enumerate(x for x in jobs if x not in MODS)}
        copies_before = {n: 4 * i for n, i in mod_no.items()}

        def slot_free(eng, i):
            if i >= NSTAGE:
                old = jobs[i - NSTAGE]
                if old in MODS:
                    eng.wait_ge(mod_mm, mod_no[old] + 1)
                else:
                    eng.wait_ge(lo_done, split_no[old] + 1)

        wT = {n: io[f"w{n}"].rearrange("(p c) n -> p c n", c=KC) for n in wnames}
        wmod = io["wmod"].rearrange("(p c) (m n) -> m p c n", c=KC, m=6)
        x_t = io["x"].rearrange("b (j p) d -> b j p d", p=P)

        with nc.Block() as block:
            @block.sync
            def _(sp):
                sp.dma_start(cT[:], io["c"]).then_inc(small_in, 16)
                for n, bt in (("k", bias_k), ("v", bias_v), ("q", bias_q), ("g", bias_g)):
                    sp.dma_start(bt[:], io[f"b{n}"].partition_broadcast(P)).then_inc(small_in, 16)
                sp.dma_start(mod["gabo"][:, 0, :], io["bo"].partition_broadcast(P)).then_inc(small_in, 16)
                sp.dma_start(cos_t[:], io["cos"]).then_inc(small_in, 16)
                sp.dma_start(sin_t[:], io["sin"]).then_inc(small_in, 16)
                sp.dma_start(group_mask[:], io["mask"]).then_inc(small_in, 16)
                sp.dma_start(proj[:, 0:KC * RW].rearrange("p (c n) -> p c n", c=KC),
                             io["wr"].rearrange("(p c) n -> p c n", c=KC)).then_inc(small_in, 16)
                for i, n in enumerate(jobs):
                    slot_free(sp, i)
                    src = wmod[MODS.index(n)] if n in MODS else wT[n]
                    sp.dma_start(stage[i % NSTAGE].rearrange("p (c n) -> p c n", c=KC), src)\
                      .then_inc(stage_in[i % NSTAGE], 16)
                sp.wait_ge(mod_ready, copies_before["gb"] + 4)
                sp.dma_start(scr["gb"], proj_gb[:]).then_inc(gb_out, 16)

                def step(j, b):
                    if real(j, b, -2):
                        jn, bn = lag(j, b, -2)
                        wait_tile(sp, xhat_done, j, b, 0)
                        sp.dma_start(xin[bn][:], x_t[bn, jn]).then_inc(x_in[bn], 16)
                    if real(j, b, 3):
                        jl, bl = lag(j, b, 3)
                        wait_tile(sp, x2_done, j, b, 3)
                        sp.sem_inc(waited_sp, 1)
                        sp.dma_start(scr["x2"][bl, jl], x2[bl][:]).then_inc(x2_out[bl], 16)
                        wait_tile(sp, h2_done, j, b, 3)
                        sp.dma_start(scr["h2"][bl, jl], h2[bl]).then_inc(h2_out[bl], 16)
                    if real(j, b, 1):
                        jl, bl = lag(j, b, 1)
                        wait_tile(sp, x2_done, j, b, 3)
                        sp.dma_start(xres[bl][:], x_t[bl, jl]).then_inc(xres_in[bl], 16)
                    if real(j, b, 3):
                        jl, bl = lag(j, b, 3)
                        wait_tile(sp, h2T_lo, j, b, 3)
                        sp.dma_start(scr["h2T"][bl, jl], raw(h2T[:]).rearrange("p s c t -> p (s c t)"))\
                          .then_inc(h2T_out, 16)

                run_steps(sp, step)
                sp.wait_ge(gb_out, 16)
                sp.wait_ge(h2T_out, 16 * NT)
                for s in (x2_out, h2_out):
                    for i in range(2):
                        sp.wait_ge(s[i], 16 * TPB)

            @block.gpsimd
            def _(pool):
                pool.memset(ident[:], 0.0).then_inc(const_ready, 1)
                pool.memset(minus_half[:], -0.5).then_inc(const_ready, 1)
                for i in range(2):
                    pool.memset(v_buf[i][:, :, P:SW], 1.0).then_inc(const_ready, 1)
                    pool.memset(state[i][1][:], 0.0).then_inc(const_ready, 1)
                pool.wait_ge(const_ready, 6)
                pool.affine_select(out=ident[:], in_=ident[:], compare_op=ALU.not_equal, fill=1.0, base=0,
                                   pattern=[[-1, P]], channel_multiplier=1).then_inc(const_ready, 1)

                pool.wait_ge(gb_out, 16)

                def sine(j, b, n):
                    wait_tile(pool, (q_out if n == "q" else k_out), j, b)
                    wait_tile(pool, rope_done[n], j, b, 1)
                    pool.sem_inc(waited_pool, 1)
                    pool.tensor_tensor(t2[:, qk[n]].rearrange("p (h e) -> p h e", e=DK),
                                       y[:, qk[n]].rearrange("p (h e) -> p h e", e=DK),
                                       sin_t[:, j, :].unsqueeze(1).broadcast_to((P, H, DK)),
                                       ALU.mult).then_inc(rope_sin[n], 1)

                def step(j, b):
                    if real(j, b, 0):
                        sine(j, b, "k")
                    if real(j, b, 1):
                        jl, bl = lag(j, b, 1)
                        for c in range(2):
                            wait_tile(pool, state_done, j, b, 1, 2, c + 1)
                            wait_tile(pool, n_mm, j, b, 2)
                            pool.tensor_tensor(blocks[c][:], state[bl][c][:],
                                               group_mask[:].unsqueeze(1).broadcast_to((P, NG, SW)),
                                               ALU.mult).then_inc(blocks_done, 1)
                    if real(j, b, 2):
                        jl, bl = lag(j, b, 2)
                        pool.wait_ge(xres_in[bl], 16 * (jl + 1))
                        pool.tensor_tensor(xres[bl][:], xres[bl][:], mod["gabo"][:, bl, :], ALU.add)\
                            .then_inc(xg_done, 1)
                    if real(j, b, -2):
                        jn, bn = lag(j, b, -2)
                        wait_tile(pool, mv1_done, j, b, -2)
                        pool.sem_inc(waited_pool, 1)
                        pool.tensor_scalar(rs1[bn][:, 0:1], mv1[bn][:, 1:2], LN_EPS, None, ALU.add).then_inc(rs1_a, 1)
                        wait_tile(pool, rs1_a, j, b, -2)
                        pool.tensor_tensor(rs1[bn][:, 1:2], rs1[bn][:, 0:1], minus_half[:], ALU.pow)\
                            .then_inc(rs1_done, 1)
                    if real(j, b, 0):
                        sine(j, b, "q")
                    if real(j, b, -2):
                        jn, bn = lag(j, b, -2)
                        wait_tile(pool, xhat_done, j, b, -2)
                        pool.wait_ge(mod_ready, copies_before["ca"] + 4)
                        wait_tile(pool, hT_mm, j, b, 0)
                        pool.tensor_tensor(h_buf[bn][:], xhat[:], mod["ca1"][:, bn, :], ALU.mult).then_inc(h_a, 1)
                        wait_tile(pool, h_a, j, b, -2)
                        pool.tensor_tensor(h_buf[bn][:], h_buf[bn][:], mod["sa"][:, bn, :], ALU.add)\
                            .then_inc(h_done, 1)
                    if real(j, b, 2):
                        jl, bl = lag(j, b, 2)
                        wait_tile(pool, mv2_done, j, b, 2)
                        pool.sem_inc(waited_pool, 1)
                        pool.tensor_scalar(rs2[bl][:, 0:1], mv2[bl][:, 1:2], LN_EPS, None, ALU.add).then_inc(rs2_a, 1)
                        wait_tile(pool, rs2_a, j, b, 2)
                        pool.tensor_tensor(rs2[bl][:, 1:2], rs2[bl][:, 0:1], minus_half[:], ALU.pow)\
                            .then_inc(rs2_done, 1)
                    if real(j, b, 2):
                        jl, bl = lag(j, b, 2)
                        wait_tile(pool, xhat2_done, j, b, 2)
                        pool.wait_ge(mod_ready, 24)
                        if real(j, b, 4):
                            pool.wait_ge(h2_out[bl], 16 * jl)
                            wait_tile(pool, h2T_mm, j, b, 4)
                        pool.tensor_tensor(h2[bl], xhat2[:], mod["cb1"][:, bl, :], ALU.mult).then_inc(h2_a, 1)
                        wait_tile(pool, h2_a, j, b, 2)
                        pool.tensor_tensor(h2[bl], h2[bl], mod["sb"][:, bl, :], ALU.add).then_inc(h2_done, 1)

                run_steps(pool, step)

            @block.scalar
            def _(act):
                act.wait_ge(small_in, 160)
                nc.scalar.activation(cS[:], cT[:], ACT.Silu).then_inc(csilu_act, 1)
                nc.scalar.copy(wr_hi[:], proj[:, 0:KC * RW].rearrange("p (c n) -> p c n", c=KC)).then_inc(csilu_act, 1)
                for i, n in enumerate(jobs):
                    if n not in MODS:
                        act.wait_ge(stage_in[i % NSTAGE], 16 * (i // NSTAGE + 1))
                        nc.scalar.copy(w_hi[n][:], stage[i % NSTAGE].rearrange("p (c n) -> p c n", c=KC))\
                            .then_inc(hi_done, 1)

                def exponential(j, b, n):
                    wait_tile(act, rope_done[n], j, b)
                    nc.scalar.activation(t1[:, qk[n]], y[:, qk[n]], ACT.Relu, scale=-1.0).then_inc(relu_done[n], 1)
                    wait_tile(act, relu_done[n], j, b)
                    nc.scalar.activation(t1[:, qk[n]], t1[:, qk[n]], ACT.Exp, scale=-1.0).then_inc(exp_done[n], 1)

                def step(j, b):
                    if real(j, b, 3):
                        jl, bl = lag(j, b, 3)
                        wait_tile(act, h2T_mm, j, b, 3)
                        if real(j, b, 4):
                            act.wait_ge(h2T_out, 16 * (2 * j + b - 3))
                            wait_tile(act, r_mm, j, b, 4)
                        nc.scalar.copy(h2T[:, 0], bank[2][:].rearrange("p (c t) -> p c t", c=KC)).then_inc(h2T_hi, 1)
                    if real(j, b, 0):
                        exponential(j, b, "k")
                    if real(j, b, 2):
                        wait_tile(act, oT_mm, j, b, 2)
                        wait_tile(act, o_mm, j, b, 3)
                        nc.scalar.copy(oT[:, 0], bank[3][:].rearrange("p (c t) -> p c t", c=KC)).then_inc(oT_hi, 1)
                    if real(j, b, 1):
                        wait_tile(act, qT_mm, j, b, 1)
                        wait_tile(act, n_mm, j, b, 2)
                        nc.scalar.copy(qT[:], bank[3][:].rearrange("p (g t) -> p g t", g=NG)).then_inc(qT_done, 1)
                    if real(j, b, 0):
                        exponential(j, b, "q")
                    if real(j, b, -1):
                        jn, bn = lag(j, b, -1)
                        wait_tile(act, hT_mm, j, b, -1)
                        wait_tile(act, g_mm, j, b, 1)
                        nc.scalar.copy(hT[bn][:, 0], bank[0][:].rearrange("p (c t) -> p c t", c=KC)).then_inc(hT_hi, 1)
                    if real(j, b, 0):
                        wait_tile(act, g_out, j, b)
                        nc.scalar.activation(th[b][:], th[b][:], ACT.Tanh, scale=0.5).then_inc(tanh_done, 1)

                run_steps(act, step)

            @block.vector
            def _(dve):
                dve.wait_ge(csilu_act, 1)
                nc.vector.tensor_copy(c_silu[:], cS[:].unsqueeze(3).broadcast_to((P, KC, B, P // B)))\
                    .then_inc(csilu_ready, 1)
                dve.wait_ge(csilu_act, 2)
                nc.vector.tensor_tensor(wr_lo[:], proj[:, 0:KC * RW].rearrange("p (c n) -> p c n", c=KC),
                                        raw(wr_hi[:]), ALU.subtract).then_inc(csilu_ready, 1)
                dve.wait_ge(csilu_ready, 2)
                tmp_count = [0]

                def tmp(ins):
                    tmp_count[0] += 1
                    ins.then_inc(mod_tmp, 1)
                    dve.wait_ge(mod_tmp, tmp_count[0])

                for i, n in enumerate(jobs):
                    if n not in MODS:
                        dve.wait_ge(hi_done, split_no[n] + 1)
                        nc.vector.tensor_tensor(w_lo[n][:], stage[i % NSTAGE].rearrange("p (c n) -> p c n", c=KC),
                                                raw(w_hi[n][:]), ALU.subtract).then_inc(lo_done, 1)
                        continue
                    m = mod_no[n]
                    dve.wait_ge(mod_mm, m + 1)
                    if m:
                        dve.wait_ge(mod_ready, 4 * m)
                    src = bank[m % 4]
                    if n in ("ga", "gb"):
                        tmp(nc.vector.tensor_scalar(proj[:], src[:], 0.0, 2.0, ALU.is_ge, ALU.mult))
                        tmp(nc.vector.tensor_scalar(proj[:], proj[:], -1.0, None, ALU.add))
                        tmp(nc.vector.tensor_tensor(xhat[:], src[:], proj[:], ALU.mult))
                        tmp(nc.vector.scalar_tensor_tensor(proj[:], xhat[:], 0.25, proj[:], ALU.max, ALU.mult))
                        src = proj
                    elif n in ("ca", "cb"):
                        tmp(nc.vector.tensor_scalar(proj[:], src[:], 1.0, None, ALU.add))
                        src = proj
                    dst = {"sa": mod["sa"], "ca": mod["ca1"], "ga": mod["ga"], "sb": mod["sb"], "cb": mod["cb1"],
                           "gb": proj_gb}[n]
                    for bb in range(B):
                        for half in range(2):
                            nc.vector.tensor_copy(dst[64 * half:64 * half + 64, bb, :], src[64 * bb:64 * bb + 64, :])\
                                .then_inc(mod_ready, 1)
                    if n == "ga":
                        dve.wait_ge(mod_ready, copies_before["ga"] + 4)
                        for bb in (1, 0):
                            tmp(nc.vector.tensor_tensor(mod["gabo"][:, bb, :], mod["ga"][:, bb, :],
                                                        mod["gabo"][:, 0, :], ALU.mult))
                dve.wait_ge(mod_ready, 24)
                dve.wait_ge(const_ready, 6)

                def cosine(j, b, n):
                    wait_tile(dve, (q_out if n == "q" else k_out), j, b)
                    nc.vector.tensor_tensor(t1[:, qk[n]].rearrange("p (h e) -> p h e", e=DK),
                                            y[:, qk[n]].rearrange("p (h e) -> p h e", e=DK),
                                            cos_t[:, j, :].unsqueeze(1).broadcast_to((P, H, DK)),
                                            ALU.mult).then_inc(rope_cos[n], 1)

                def rotated(j, b, n):
                    wait_tile(dve, rope_cos[n], j, b)
                    wait_tile(dve, rope_sin[n], j, b)
                    pairs = lambda a: a[:, qk[n]].rearrange("p (i two) -> p i two", two=2)
                    nc.vector.tensor_tensor(pairs(y), pairs(t1), pairs(t2)[:, :, ::-1], ALU.add)\
                        .then_inc(rope_done[n], 1)

                def features(j, b, n):
                    wait_tile(dve, exp_done[n], j, b)
                    wait_tile(dve, rope_done[n], j, b)
                    if n == "k":
                        wait_tile(dve, s_mm, j, b, 2, 2)
                    else:
                        wait_tile(dve, qT_mm, j, b, 2)
                    nc.vector.scalar_tensor_tensor(feat[b][:, qk[n]], y[:, qk[n]], 1.0, t1[:, qk[n]], ALU.add,
                                                   ALU.max).then_inc(feat_done[n], 1)

                def step(j, b):
                    if real(j, b, 0):
                        wait_tile(dve, k_mm, j, b)
                        wait_tile(dve, feat_done["k"], j, b, 1)
                        nc.vector.tensor_tensor(y[:, D:2 * D], bank[0][:], bias_k[:], ALU.add).then_inc(k_out, 1)
                    if real(j, b, 0):
                        cosine(j, b, "k")
                    if real(j, b, 3):
                        jl, bl = lag(j, b, 3)
                        wait_tile(dve, h2T_hi, j, b, 3)
                        nc.vector.tensor_tensor(h2T[:, 1], bank[2][:].rearrange("p (c t) -> p c t", c=KC),
                                                raw(h2T[:, 0]), ALU.subtract).then_inc(h2T_lo, 1)
                    if real(j, b, 0):
                        rotated(j, b, "k")
                    if real(j, b, 1):
                        jl, bl = lag(j, b, 1)
                        for c in range(2):
                            wait_tile(dve, s_mm, j, b, 1, 2, c + 1)
                            wait_tile(dve, state_done, j, b, 1, 2, c)
                            wait_tile(dve, blocks_done, j, b, 3, 2, c + 1)
                            nc.vector.tensor_tensor(state[bl][c][:].rearrange("p (s g) e -> p s (g e)", s=2),
                                                    psS[:, :, 0:2 * SW],
                                                    state[bl][1 - c][:].rearrange("p (s g) e -> p s (g e)", s=2),
                                                    ALU.add).then_inc(state_done, 1)
                    if real(j, b, 0):
                        features(j, b, "k")
                    if real(j, b, 0):
                        wait_tile(dve, v_mm, j, b)
                        wait_tile(dve, s_mm, j, b, 2, 2)
                        nc.vector.tensor_tensor(v_buf[b][:, :, 0:P], bank[1][:].rearrange("p (g e) -> p g e", g=NG),
                                                bias_v[:].rearrange("p (g e) -> p g e", g=NG), ALU.add)\
                            .then_inc(v_out, 1)
                    if real(j, b, 2):
                        wait_tile(dve, oT_hi, j, b, 2)
                        nc.vector.tensor_tensor(oT[:, 1], bank[3][:].rearrange("p (c t) -> p c t", c=KC),
                                                raw(oT[:, 0]), ALU.subtract).then_inc(oT_lo, 1)
                    if real(j, b, 3):
                        jl, bl = lag(j, b, 3)
                        wait_tile(dve, r_mm, j, b, 3)
                        nc.vector.tensor_copy(logits[:, bl * TPB + jl, :], psN[:, 1, 300:300 + RW]).then_inc(logits_done, 1)
                    if real(j, b, -2):
                        jn, bn = lag(j, b, -2)
                        dve.wait_ge(x_in[bn], 16 * (jn + 1))
                        nc.vector.bn_stats(st1[:], xin[bn][:]).then_inc(st1_done, 1)
                        wait_tile(dve, st1_done, j, b, -2)
                        dve.sem_inc(waited_dve, 1)
                        nc.vector.bn_aggr(mv1[bn][:], st1[:]).then_inc(mv1_done, 1)
                    if real(j, b, 0):
                        wait_tile(dve, q_mm, j, b)
                        wait_tile(dve, feat_done["q"], j, b, 1)
                        nc.vector.tensor_tensor(y[:, 0:D], bank[0][:], bias_q[:], ALU.add).then_inc(q_out, 1)
                    if real(j, b, 0):
                        cosine(j, b, "q")
                    if real(j, b, -2):
                        jn, bn = lag(j, b, -2)
                        wait_tile(dve, rs1_done, j, b, -2)
                        wait_tile(dve, h_a, j, b, -1)
                        nc.vector.tensor_scalar(xhat[:], xin[bn][:], mv1[bn][:, 0:1], rs1[bn][:, 1:2],
                                                ALU.subtract, ALU.mult).then_inc(xhat_done, 1)
                    if real(j, b, 0):
                        rotated(j, b, "q")
                    if real(j, b, 2):
                        jl, bl = lag(j, b, 2)
                        wait_tile(dve, o_mm, j, b, 2)
                        wait_tile(dve, h2_a, j, b, 3)
                        nc.vector.tensor_tensor(proj[:], bank[2][:], mod["ga"][:, bl, :], ALU.mult).then_inc(proj_done, 1)
                        wait_tile(dve, proj_done, j, b, 2)
                        wait_tile(dve, xg_done, j, b, 2)
                        if real(j, b, 4):
                            dve.wait_ge(x2_out[bl], 16 * jl)
                        nc.vector.tensor_tensor(x2[bl][:], proj[:], xres[bl][:], ALU.add).then_inc(x2_done, 1)
                        wait_tile(dve, x2_done, j, b, 2)
                        nc.vector.bn_stats(st2[:], x2[bl][:]).then_inc(st2_done, 1)
                        wait_tile(dve, st2_done, j, b, 2)
                        wait_tile(dve, xhat2_done, j, b, 4)
                        dve.sem_inc(waited_dve, 1)
                        nc.vector.bn_aggr(mv2[bl][:], st2[:]).then_inc(mv2_done, 1)
                    if real(j, b, 0):
                        features(j, b, "q")
                    if real(j, b, -1):
                        jn, bn = lag(j, b, -1)
                        wait_tile(dve, hT_hi, j, b, -1)
                        nc.vector.tensor_tensor(hT[bn][:, 1], bank[0][:].rearrange("p (c t) -> p c t", c=KC),
                                                raw(hT[bn][:, 0]), ALU.subtract).then_inc(hT_lo, 1)
                    if real(j, b, 2):
                        jl, bl = lag(j, b, 2)
                        wait_tile(dve, rs2_done, j, b, 2)
                        nc.vector.tensor_scalar(xhat2[:], x2[bl][:], mv2[bl][:, 0:1], rs2[bl][:, 1:2],
                                                ALU.subtract, ALU.mult).then_inc(xhat2_done, 1)
                    if real(j, b, 0):
                        wait_tile(dve, g_mm, j, b)
                        nc.vector.tensor_tensor(th[b][:], bank[1][:], bias_g[:], ALU.add).then_inc(g_out, 1)
                    if real(j, b, 1):
                        jl, bl = lag(j, b, 1)
                        wait_tile(dve, n_mm, j, b, 1)
                        wait_tile(dve, o_done, j, b, 2)
                        num = psN[:, :, 0:2 * SW].rearrange("p s (g e) -> p s g e", e=SW)
                        nc.vector.tensor_scalar(rden[:].rearrange("p (s g h) -> p s g h", s=2, g=2), num[:, :, :, P:SW],
                                                2.0, 2 * DEN_EPS, ALU.mult, ALU.add).then_inc(den_a, 1)
                        wait_tile(dve, den_a, j, b, 1)
                        nc.vector.reciprocal(rden2[:], rden[:]).then_inc(den_done, 1)
                        wait_tile(dve, tanh_done, j, b, 1)
                        for s in range(2):
                            nc.vector.scalar_tensor_tensor(
                                o1_buf[:, s * 256:(s + 1) * 256].rearrange("p (g e) -> p g e", g=2),
                                th[bl][:, s * 256:(s + 1) * 256].rearrange("p (g e) -> p g e", g=2), 1.0,
                                num[:, s, :, 0:P], ALU.add, ALU.mult).then_inc(o_half, 1)
                        wait_tile(dve, o_half, j, b, 1, 2)
                        wait_tile(dve, den_done, j, b, 1)
                        wait_tile(dve, oT_mm, j, b, 2)
                        nc.vector.tensor_tensor(o_buf.rearrange("p (h e) -> p h e", e=DK),
                                                o1_buf.rearrange("p (h e) -> p h e", e=DK),
                                                rden2[:].unsqueeze(2).broadcast_to((P, H, DK)), ALU.mult)\
                            .then_inc(o_done, 1)

                run_steps(dve, step)

            @block.tensor
            def _(pe):
                def product(out, pairs):
                    passes = [(l[u], r[w]) for l, r in pairs for u, w in ((0, 0), (0, 1), (1, 0))]
                    for n, (l, r) in enumerate(passes):
                        last = nc.tensor.matmul(out, l, r, start=n == 0, stop=n == len(passes) - 1)
                    return last

                def transpose_tile(out, src):
                    v = src.rearrange("t (q c) -> t c q", c=KC)
                    for c in range(KC):
                        last = nc.tensor.transpose(out[:, c * P:(c + 1) * P], v[:, c, :], ident[:])
                    return last

                pe.wait_ge(csilu_ready, 1)
                for i, n in enumerate(jobs):
                    if n in MODS:
                        m = mod_no[n]
                        pe.wait_ge(stage_in[i % NSTAGE], 16 * (i // NSTAGE + 1))
                        if m >= 4:
                            pe.wait_ge(mod_ready, 4 * (m - 3))
                        for c in range(KC):
                            last = nc.tensor.matmul(bank[m % 4][:], c_silu[:, c].rearrange("p b m -> p (b m)"),
                                                    stage[i % NSTAGE][:, c * D:(c + 1) * D],
                                                    start=c == 0, stop=c == KC - 1)
                        last.then_inc(mod_mm, 1)
                pe.wait_ge(mod_ready, 24)
                pe.wait_ge(const_ready, 7)
                pe.wait_ge(lo_done, 5)

                def project(n, out, hb):
                    return product(out, [((hb[:, 0, c], hb[:, 1, c]), (w_hi[n][:, c], w_lo[n][:, c]))
                                         for c in range(KC)])

                def step(j, b):
                    if real(j, b, 0):
                        wait_tile(pe, hT_lo, j, b)
                        project("k", bank[0][:], hT[b]).then_inc(k_mm, 1)
                    if real(j, b, 3):
                        jl, bl = lag(j, b, 3)
                        wait_tile(pe, h2_done, j, b, 3)
                        wait_tile(pe, proj_done, j, b, 3)
                        transpose_tile(bank[2][:], h2[bl]).then_inc(h2T_mm, 1)
                    if real(j, b, 1):
                        jl, bl = lag(j, b, 1)
                        wait_tile(pe, feat_done["k"], j, b, 1)
                        wait_tile(pe, v_out, j, b, 1)
                        for c in range(2):
                            wait_tile(pe, state_done, j, b, 1, 2, c)
                            rows = slice(c * CS, (c + 1) * CS)
                            for g in range(NG):
                                last = nc.tensor.matmul(psS[:, g // 2, (g % 2) * SW:(g % 2 + 1) * SW],
                                                        feat[bl][rows, D + g * P:D + (g + 1) * P],
                                                        v_buf[bl][rows, g, :], start=True, stop=True)
                            last.then_inc(s_mm, 1)
                    if real(j, b, 0):
                        wait_tile(pe, g_out, j, b, 1)
                        project("v", bank[1][:], hT[b]).then_inc(v_mm, 1)
                    if real(j, b, 2):
                        wait_tile(pe, o_done, j, b, 2)
                        wait_tile(pe, qT_done, j, b, 2)
                        transpose_tile(bank[3][:], o_buf).then_inc(oT_mm, 1)
                    if real(j, b, 3):
                        wait_tile(pe, h2T_lo, j, b, 3)
                        wait_tile(pe, logits_done, j, b, 4)
                        wait_tile(pe, o_done, j, b, 2)
                        product(psN[:, 1, 300:300 + RW],
                                [((h2T[:, 0, c], h2T[:, 1, c]), (wr_hi[:, c], wr_lo[:, c])) for c in range(KC)])\
                            .then_inc(r_mm, 1)
                    if real(j, b, 0):
                        wait_tile(pe, k_out, j, b)
                        project("q", bank[0][:], hT[b]).then_inc(q_mm, 1)
                    if real(j, b, 1):
                        jl, bl = lag(j, b, 1)
                        wait_tile(pe, feat_done["q"], j, b, 1)
                        wait_tile(pe, oT_lo, j, b, 2)
                        for g in range(NG):
                            last = nc.tensor.transpose(bank[3][:, g * P:(g + 1) * P], feat[bl][:, g * P:(g + 1) * P],
                                                       ident[:])
                        last.then_inc(qT_mm, 1)
                    if real(j, b, 2):
                        wait_tile(pe, oT_lo, j, b, 2)
                        wait_tile(pe, h2T_lo, j, b, 3)
                        project("o", bank[2][:], oT).then_inc(o_mm, 1)
                    if real(j, b, -1):
                        jn, bn = lag(j, b, -1)
                        wait_tile(pe, h_done, j, b, -1)
                        wait_tile(pe, q_out, j, b)
                        transpose_tile(bank[0][:], h_buf[bn][:]).then_inc(hT_mm, 1)
                    if real(j, b, 0):
                        wait_tile(pe, v_out, j, b)
                        project("g", bank[1][:], hT[b]).then_inc(g_mm, 1)
                    if real(j, b, 1):
                        jl, bl = lag(j, b, 1)
                        wait_tile(pe, qT_done, j, b, 1)
                        wait_tile(pe, o_done, j, b, 2)
                        wait_tile(pe, logits_done, j, b, 3)
                        for c in range(2):
                            wait_tile(pe, blocks_done, j, b, 1, 2, c + 1)
                            for g in range(NG):
                                last = nc.tensor.matmul(psN[c * CS:(c + 1) * CS, g // 2, (g % 2) * SW:(g % 2 + 1) * SW],
                                                        qT[:, g, c * CS:(c + 1) * CS], blocks[c][:, g, :],
                                                        start=True, stop=True)
                        last.then_inc(n_mm, 1)

                run_steps(pe, step)


FCH = FS // P
GROUP = 3
NGROUPS = -(-FCH // GROUP)
SUB = 4
UNITS = NT // SUB
XPU = 4
FIRST_X = 2
LAST_X = FIRST_X + E // XPU
TABLE_COLS = 8 + E + 2 * NT + P
FX = -(-F // P)
RAW_SLOTS = 4
S1 = CAP // 8


def chunks_of(g):
    return GROUP if g < NGROUPS - 1 else FCH - GROUP * (NGROUPS - 1)


def chunk_no(u, c, last):
    if last:
        return GROUP * UNITS * (NGROUPS - 1) + chunks_of(NGROUPS - 1) * (u - UNITS * (NGROUPS - 1)) + c
    return GROUP * u + c


def per_engine(order):
    fine = []
    for what, r in order:
        fine += [("mult", r), ("gu_lo", r)] if what == "up" else [(what, r)]
    return {"pe": order, "act": order, "pool": order, "dve": fine, "sp": [("hT", 0)]}


ROUTING0 = {
    "pe": [("gate", 0), ("up", 0), ("gate", 1), ("up", 1), ("route", "positions"), ("gate", 2), ("up", 2), ("down", 0),
           ("down", 1), ("down", 2), ("down", 3)],
    "act": [("route", "exp"), ("first_gu", 0), ("first_gu", 1), ("first_down", 0), ("gate", 0), ("up", 0),
            ("first_gu", 2), ("first_down", 1), ("gate", 1), ("up", 1), ("first_down", 2), ("gate", 2), ("up", 2)],
    "dve": [("route", "softmax"), ("first_gu", 0), ("first_gu", 1), ("first_down", 0), ("route", "one_hot"),
            ("mult", 0), ("gu_lo", 0), ("first_gu", 2), ("first_down", 1), ("mult", 1), ("gu_lo", 1),
            ("first_down", 2), ("route", "picks"), ("mult", 2), ("gu_lo", 2), ("route", "digits"), ("down", 0),
            ("down", 1), ("down", 2), ("down", 3), ("route", "high")],
    "pool": [],
    "sp": [("hT", 0)],
}
ROUTING1 = {
    "pe": [("gate", 0), ("up", 0), ("gate", 1), ("up", 1), ("route", "tokens"), ("gate", 2), ("up", 2), ("down", 0),
           ("down", 1), ("down", 2), ("down", 3)],
    "act": [("gate", 0), ("up", 0), ("gate", 1), ("up", 1), ("gate", 2), ("up", 2),
            ("split_g", 4), ("split_u", 4)],
    "dve": [("mult", 0), ("gu_lo", 0), ("route", "low"), ("mult", 1), ("gu_lo", 1), ("route", "slots"),
            ("mult", 2), ("gu_lo", 2), ("down", 0), ("down", 1), ("down", 2), ("down", 3), ("split_g", 4),
            ("split_u", 4)],
    "pool": [("gather", 0), ("gather", 1)],
    "sp": [("route", "out"), ("first_x", 0), ("route", "columns"), ("first_x", 1), ("first_x", 2), ("hT", 0)],
}
WITH_X = {
    "pe": [("rows", 0), ("gate", 0), ("gu", 0), ("up", 0), ("mid", 0), ("gate", 1), ("exp_down", 0), ("gu", 1),
           ("up", 1), ("mid", 1), ("gate", 2), ("rows", 1), ("exp_down", 1), ("gu", 2), ("up", 2), ("mid", 2),
           ("exp_down", 2), ("down", 0), ("gu", 3), ("down", 1), ("down", 2), ("mid", 3), ("down", 3), ("exp_down", 3)],
    "act": [("rows", 0), ("split_d", 0), ("gate", 0), ("low", 0), ("silu", 0), ("split_g", 1), ("split_u", 1), ("up", 0), ("mid", 0),
            ("gate", 1), ("exp_down", 0), ("split_d", 1), ("low", 1), ("silu", 1), ("split_g", 2), ("split_u", 2),
            ("up", 1), ("mid", 1), ("gate", 2), ("rows", 1), ("exp_down", 1), ("split_d", 2), ("low", 2),
            ("silu", 2), ("split_g", 3), ("mid", 2), ("up", 2), ("split_u", 3), ("exp_down", 2), ("split_d", 3),
            ("low", 3), ("silu", 3), ("split_g", 4), ("split_u", 4), ("mid", 3), ("exp_down", 3)],
    "dve": [("rows", 0), ("split_d", 0), ("sum", 0), ("xmul", 0), ("mult", 0), ("split_g", 1), ("mid", 0), ("split_u", 1), ("gu_lo", 0),
            ("exp_down", 0), ("split_d", 1), ("sum", 1), ("xmul", 1), ("mult", 1), ("split_g", 2), ("mid", 1),
            ("split_u", 2), ("gu_lo", 1), ("rows", 1), ("exp_down", 1), ("split_d", 2), ("sum", 2), ("xmul", 2),
            ("mult", 2), ("mid", 2), ("gu_lo", 2), ("split_g", 3), ("split_u", 3), ("exp_down", 2), ("down", 0),
            ("split_d", 3), ("sum", 3), ("xmul", 3), ("down", 1), ("split_g", 4), ("down", 2), ("mid", 3),
            ("split_u", 4), ("down", 3), ("exp_down", 3)],
    "pool": [("ye_out", 0), ("ye_out", 1), ("gather", 0), ("gather", 1), ("ye_out", 2), ("ye_out", 3)],
    "sp": [("weights", 1), ("weights", 2), ("weights", 3), ("hT", 0), ("weights", 4)],
}
COMBINE4 = {
    "pe": [("gate", 0), ("up", 0), ("gate", 1), ("up", 1), ("gate", 2), ("up", 2), ("down", 0), ("down", 1),
           ("down", 2), ("down", 3)],
    "act": [("gate", 0), ("up", 0), ("gate", 1), ("up", 1), ("gate", 2), ("up", 2)],
    "dve": [("mult", 0), ("gu_lo", 0), ("combine", 0), ("mult", 1), ("gu_lo", 1), ("combine", 1), ("mult", 2),
            ("gu_lo", 2), ("combine", 2), ("down", 0), ("down", 1), ("down", 2), ("down", 3), ("combine", 3)],
    "pool": [("fetch", 2), ("fetch", 3), ("fetch", 4), ("fetch", 5)],
    "sp": [("hT", 0)],
}
COMBINE2 = {
    "pe": [("gate", 0), ("up", 0), ("gate", 1), ("up", 1), ("down", 0), ("down", 1), ("down", 2), ("down", 3)],
    "act": [("gate", 0), ("up", 0), ("gate", 1), ("up", 1)],
    "dve": [("mult", 0), ("gu_lo", 0), ("combine", 0), ("mult", 1), ("gu_lo", 1), ("combine", 1), ("down", 0),
            ("down", 1), ("down", 2), ("down", 3), ("times_gb", 0), ("times_gb", 1), ("times_gb", 2), ("times_gb", 3)],
    "pool": [("fetch", 2), ("fetch", 3), ("add_x2", 0), ("add_x2", 1), ("add_x2", 2), ("add_x2", 3)],
    "sp": [("x2", 0), ("hT", 0)],
}
LAST = {
    **COMBINE2,
    "dve": COMBINE2["dve"][:6] + [(what, r) for r in range(SUB) for what in ("down", "times_gb", "add_x2")],
    "pool": [],
    "sp": [("store", 1), ("x2", 0), ("last", 0), ("last", 1), ("last", 2), ("last", 3)],
}


def last_experts(order):
    return {e: [x for x in items if x[0] != "gather" and x[1] != 4] for e, items in order.items()}


def insert(items, at, after):
    out = []
    for x in items:
        new = at.get(x, [])
        out += [x] + new if after else new + [x]
    return out


def free_time(act):
    return "mid" if ("mid", 0) in act else "up"


def with_next_group(order, chunks):
    gu = [("new_gu", c) for c in range(chunks)]
    sp = order["sp"]
    if ("weights", 1) in sp:
        sp = insert(sp, {("weights", c + 1): [gu[c]] for c in range(chunks)}, False)
    else:
        sp = gu + sp
    return {**order, "act": insert(order["act"], {(free_time(order["act"]), c): [gu[c]] for c in range(chunks)}, True),
            "dve": insert(order["dve"], {("gu_lo", c): [gu[c]] for c in range(chunks)}, True),
            "sp": insert(sp, {("hT", 0): [("next_down", 0)]}, True)}


def with_new_down(order, chunks):
    new = [("new_down", c) for c in range(chunks)]
    later = lambda name: {(name, c - 1): [new[c]] for c in range(1, chunks)}
    sp = order["sp"]
    sp = insert(sp, {("weights", c): [new[c]] for c in range(1, chunks)}, True) \
        if ("weights", 1) in sp else new[1:] + sp
    return {**order, "act": insert(insert(order["act"], {("up", 0): [new[0]]}, False), later(free_time(order["act"])), True),
            "dve": insert(insert(order["dve"], {("mult", 0): [new[0]]}, False), later("gu_lo"), True), "sp": sp}


def run_units(eng, name, unit):
    def run(g, s, kind, order):
        unit(g, s, kind, order[name])

    run(0, 0, "routing0", ROUTING0)
    run(0, 1, "routing1", ROUTING1)
    run(0, 2, "experts", WITH_X)
    run(0, 3, "experts", with_next_group(WITH_X, chunks_of(1)))
    run(1, 0, "experts", with_new_down(WITH_X, chunks_of(1)))
    with eng.Fori(1, 3) as s:
        run(1, s, "experts", WITH_X)
    run(1, 3, "experts", with_next_group(WITH_X, chunks_of(2)))
    run(2, 0, "experts", with_new_down(WITH_X, chunks_of(2)))
    run(2, 1, "experts", last_experts(WITH_X))
    run(2, 2, "combine4", {**COMBINE4, "pool": [("fetch", 0), ("fetch", 1)] + COMBINE4["pool"]})
    run(2, 3, "combine4", with_next_group(COMBINE4, chunks_of(3)))
    run(3, 0, "combine2", with_new_down(COMBINE2, chunks_of(3)))
    with eng.Fori(1, 3) as s:
        run(3, s, "combine2", {**COMBINE2, "sp": [("store", 1)] + COMBINE2["sp"]})
    run(3, 3, "combine2", LAST)


def ffn(nc, io, scr, out):
    with ExitStack() as ctx:
        def sb(name, shape, dt=F32):
            return ctx.enter_context(nc.sbuf_tensor(name, shape, dt))

        def sem(name):
            return ctx.enter_context(nc.semaphore(name))

        logits, ident = io["logits"], io["ident"]
        FD = GROUP * D
        acc = sb("acc", [P, NT, D])
        gb = sb("gb", [P, B, D])
        ws = [sb(f"ws{c}", [P, 2, 3 * D], F32R) for c in range(GROUP)]
        ws_raw = sb("ws_raw", [P, 3 * D])
        hT = sb("h2T_unit", [P, SUB, 2, KC, P], F32R)
        guT = [sb(f"guT{c}", [P, 2, SUB * P], F32R) for c in range(GROUP)]
        sil = sb("sil", [P, SUB * P])
        gu = sb("gu", [P, SUB * P])
        sig4 = sb("sig4", [P, SUB])
        wx_raw = sb("wx_raw", [P, RAW_SLOTS, FX * D])
        wx = [sb(f"wx_{n}", [P, 2, FX * D], F32R) for n in ("gate", "up", "down")]
        rows = [sb(f"rows{i}", [P, D]) for i in range(2)]
        xs = [sb(f"xs{i}", [P, 2, KC, P], F32R) for i in range(2)]
        low_g, low_u = sb("low_g", [CAP, F]), sb("low_u", [CAP, F])
        xg, xu = sb("xg", [CAP, F]), sb("xu", [CAP, F])
        xgu = sb("xgu", [CAP, FX * P])
        xguT = sb("xguT", [P, FX, P], F32R)
        low_y = sb("low_y", [CAP, D])
        ye = sb("ye", [CAP, D])
        sig = sb("sig", [P, NT])
        w_top = sb("w_top", [P, NT, TOPK])
        slot_top = sb("slot_top", [P, NT, TOPK], I32)
        w_now = sb("w_now", [P, TOPK])
        slot_now = [sb(f"slot_now{i}", [P, TOPK], I32) for i in range(2)]
        tok_of_slot = sb("tok_of_slot", [P, E // 2], I32)
        tok_now = sb("tok_now", [P, 2], I32)
        free = wx_raw[:].rearrange("p s n -> p (s n)")
        used = [0]

        def take(n):
            used[0] += n
            return free[:, used[0] - n:used[0]]

        def by_tile(ap, n=E):
            return ap.rearrange("p (t e) -> p t e", e=n)

        PE_ = NT * E
        prob = by_tile(take(PE_))
        one_hot_flat, picked_flat = take(TOPK * PE_), take(TOPK * PE_)
        one_hot = one_hot_flat.rearrange("p (t k e) -> p t k e", k=TOPK, e=E)
        picked = picked_flat.rearrange("p (t k e) -> p t k e", k=TOPK, e=E)
        digit1 = one_hot_flat.bitcast(F16).rearrange("p (t n) -> p t n", t=NT)
        digit0 = picked_flat.bitcast(F16).rearrange("p (t n) -> p t n", t=NT)
        posm = by_tile(take(PE_))
        mask = take(PE_ // 2).bitcast(BF16)
        before = take(P // 2).bitcast(BF16)
        ones = take(P // 2).bitcast(BF16)
        top = take(NT * 8).rearrange("p (t k) -> p t k", k=8)
        c1 = prob
        pos_i, c0 = by_tile(rows[0][:].bitcast(I32)), by_tile(rows[1][:])
        top_i = sb("top_i", [P, NT, 8], U32)
        idx_f = sb("idx_f", [P, NT, TOPK])
        small = sb("small", [P, 4, NT])
        tables = sb("tables", [P, TABLE_COLS])
        iota8, iota_e = tables[:, 0:8], tables[:, 8:8 + E]
        token_id = tables[:, 8 + E:8 + E + NT]
        own_half = tables[:, 8 + E + NT:8 + E + 2 * NT]
        pos_k = sb("pos_k", [P, NT, TOPK])
        valid = sb("valid", [P, NT, TOPK])
        inv = sb("inv", [P, 2, 8, NT])
        inv_f = sb("inv_f", [P, 2, 8])
        inv_i = sb("inv_i", [P, 2, 8], I32)

        bankA = [ctx.enter_context(nc.psum_tensor(f"bankA{i}", [P, D], F32)) for i in range(2)]
        bankB = [ctx.enter_context(nc.psum_tensor(f"bankB{i}", [P, D], F32)) for i in range(2)]
        psXG = ctx.enter_context(nc.psum_tensor("psXG", [P, D], F32))
        psXU = ctx.enter_context(nc.psum_tensor("psXU", [P, D], F32))
        psT = ctx.enter_context(nc.psum_tensor("psT", [P, D], F32))
        psY = ctx.enter_context(nc.psum_tensor("psY", [P, D], F32))
        pair = [bankA, bankB, bankA]
        down_bank = [bankB[0], bankB[1], bankA[0], bankA[1]]

        x2u_in, gb_in, table_in, hT_in = sem("x2u_in"), sem("gb_in"), sem("table_in"), sem("hT_in")
        wgu_in, wgu_hi, wgu_lo = sem("wgu_in"), sem("wgu_hi"), sem("wgu_lo")
        wdn_in, wdn_hi, wdn_lo = sem("wdn_in"), sem("wdn_hi"), sem("wdn_lo")
        gate_mm, up_mm, sil_done, gu_done = sem("gate_mm"), sem("up_mm"), sem("sil_done"), sem("gu_done")
        gu_hi, gu_lo = sem("gu_hi"), sem("gu_lo")
        dn_mm, dn_evac, sig4_done = sem("dn_mm"), sem("dn_evac"), sem("sig4_done")
        wx_in = [sem(f"wx_in{i}") for i in range(RAW_SLOTS)]
        wxg_hi, wxd_hi = sem("wxg_hi"), sem("wxd_hi")
        wxg_lo, wxd_lo = sem("wxg_lo"), sem("wxd_lo")
        tok_copied, rows_in = sem("tok_copied"), [sem(f"rows_in{i}") for i in range(2)]
        rows_mm, rows_hi, rows_lo = sem("rows_mm"), sem("rows_hi"), sem("rows_lo")
        xgu_mm, xlow, xsum, xadd = sem("xgu_mm"), sem("xlow"), sem("xsum"), sem("xadd")
        xsil, xgu_done = sem("xsil"), sem("xgu_done")
        mid_mm, mid_hi, mid_lo = sem("mid_mm"), sem("mid_hi"), sem("mid_lo")
        xd_mm, y_low, ye_add, ye_out = sem("xd_mm"), sem("y_low"), sem("ye_add"), sem("ye_out")
        slot_copied, w_copied = sem("slot_copied"), sem("w_copied")
        y_in = [[sem(f"y_in{i}{k}") for k in range(TOPK)] for i in range(2)]
        cm_step, gb_mul, x2_add, last_add = sem("cm_step"), sem("gb_mul"), sem("x2_add"), sem("last_add")
        scaled = sem("scaled")
        r_chain, r_exp, r_pe, r_consts = sem("r_chain"), sem("r_exp"), sem("r_pe"), sem("r_consts")
        r_dve, tok_moved, out_done = sem("r_dve"), sem("tok_moved"), sem("out_done")

        waited_pool, waited_pe = io["waited_pool"], io["waited_pe"]

        ye_rows = scr["ye"].rearrange("e c d -> (e c) d")
        h2_rows = scr["h2"].rearrange("b j p d -> (b j p) d")
        h2T_tiles = scr["h2T"].rearrange("b j p n -> p (b j) n")
        x2_tiles = scr["x2"].rearrange("b j p d -> p (b j) d")
        out_tiles = out.rearrange("b (j p) d -> p (b j) d", p=P)
        y_buf = [[free[:, (4 * i + k) * D:(4 * i + k + 1) * D] for k in range(TOPK)] for i in range(2)]
        x2u = free[:, 8 * D:12 * D].rearrange("p (i d) -> p i d", d=D)
        gu_w, down_w = slice(0, 2 * D), slice(2 * D, 3 * D)

        def raw_value(m, x):
            per_unit = 64
            return per_unit * x + sum(32 if k % 3 == 2 else 16 for k in range(m % RAW_SLOTS, m + 1, RAW_SLOTS))

        def tile_no(kind, s, r):
            return 4 * (s - 2) + r if kind == "combine4" else 2 * UNITS + 2 * s + r

        def tile_uses(kind, s, r):
            return 2 * (s - 2) + r // 2 + 1 if kind == "combine4" else UNITS + s + r // 2 + 1

        with nc.Block() as block:
            @block.sync
            def _(sp):
                sp.dma_start(tables[:], io["tables"]).then_inc(table_in, 16)

                def load_gu(n):
                    if n:
                        sp.wait_ge(wgu_lo, n)
                    sp.dma_start(ws_raw[:, gu_w], io["ws"][n][:, gu_w]).then_inc(wgu_in, 16)

                def load_down(n):
                    if n:
                        sp.wait_ge(wdn_lo, n)
                    sp.dma_start(ws_raw[:, down_w], io["ws"][n][:, down_w]).then_inc(wdn_in, 16)

                load_gu(0)
                sp.dma_start(raw(hT[:].rearrange("p i s c t -> p i (s c t)")), h2T_tiles[:, 0:SUB, :]).then_inc(hT_in, 16)
                load_gu(1)
                load_down(0)
                load_gu(2)
                load_down(1)
                load_down(2)
                sp.dma_start(gb[:], scr["gb"]).then_inc(gb_in, 16)

                def load_matrix(x, m):
                    e, slot = x * XPU + m // 3, m % RAW_SLOTS
                    old_e, old = x * XPU + (m - RAW_SLOTS) // 3, (m - RAW_SLOTS) % 3
                    if not (isinstance(old_e, int) and old_e < 0):
                        if old == 2:
                            sp.wait_ge(wxd_lo, 2 + old_e + 1)
                        else:
                            sp.wait_ge(wxg_lo, 2 + 2 * old_e + old + 1)
                    if m % 3 < 2:
                        w = io["wg_x"] if m % 3 == 0 else io["wu_x"]
                        sp.dma_start(wx_raw[:, slot, 0:KC * F], w[e].rearrange("(p c) f -> p (c f)", c=KC))\
                          .then_inc(wx_in[slot], 16)
                    else:
                        w, full = io["wd_x"][e], F // P
                        sp.dma_start(wx_raw[:, slot, 0:full * D].rearrange("p (c n) -> p c n", n=D),
                                     w[0:full * P].rearrange("(c p) n -> p c n", p=P)).then_inc(wx_in[slot], 16)
                        sp.dma_start(wx_raw[0:F - full * P, slot, full * D:FX * D], w[full * P:F])\
                          .then_inc(wx_in[slot], 16)

                def unit(g, s, kind, order):
                    u = UNITS * g + s
                    x = u - FIRST_X
                    for what, r in order:
                        if (what, r) == ("route", "out"):
                            sp.wait_ge(r_dve, 3)
                            sp.dma_start(scr["slots"].rearrange("(h p c) -> p h c", h=2, p=P), inv_i[:])\
                              .then_inc(tok_moved, 16)
                        elif what == "route":
                            sp.wait_ge(tok_moved, 16)
                            with nc.allow_non_contiguous_dma("2048 slot numbers, once"):
                                sp.dma_start(tok_of_slot[:], scr["slots"].rearrange("(n p) -> p n", p=P))\
                                  .then_inc(tok_moved, 16)
                        elif what == "first_x":
                            sp.wait_ge(r_pe, 2)
                            load_matrix(x, 3 * XPU + r)
                        elif what == "weights":
                            for m in range(3 * r, 3 * r + 3):
                                load_matrix(x, m)
                        elif what == "hT":
                            sp.wait_ge(up_mm, chunk_no(u, chunks_of(g), g == NGROUPS - 1))
                            nxt = (s + 1) % UNITS if isinstance(s, int) else s + 1
                            sp.dma_start(raw(hT[:].rearrange("p i s c t -> p i (s c t)")),
                                         h2T_tiles[:, bass.ds(nxt * SUB, SUB), :]).then_inc(hT_in, 16)
                        elif what == "new_gu":
                            load_gu(GROUP * (g + 1) + r)
                        elif what == "next_down":
                            load_down(GROUP * (g + 1))
                        elif what == "new_down":
                            load_down(GROUP * g + r)
                        elif what == "x2":
                            if not (isinstance(s, int) and s == 0):
                                sp.wait_ge(x2_add, SUB * s)
                            else:
                                sp.wait_ge(wxg_lo, 2 + 2 * E)
                                sp.wait_ge(wxd_lo, 2 + E)
                            sp.dma_start(x2u, x2_tiles[:, bass.ds(s * SUB, SUB), :]).then_inc(x2u_in, 16)
                        elif what == "store":
                            sp.wait_ge(x2_add, SUB * s)
                            sp.dma_start(out_tiles[:, bass.ds((s - r) * SUB, SUB), :],
                                         acc[:, bass.ds((s - r) * SUB, SUB), :]).then_inc(out_done, 16)
                        elif what == "last":
                            i = s * SUB + r
                            sp.wait_ge(last_add, r + 1)
                            sp.dma_start(out_tiles[:, i:i + 1, :], acc[:, i:i + 1, :]).then_inc(out_done, 16)

                run_units(sp, "sp", unit)
                sp.wait_ge(out_done, 16 * (UNITS - 1 + SUB))

            @block.gpsimd
            def _(pool):
                pool.memset(xgu[:, F:FX * P], 0.0).then_inc(r_consts, 1)
                pool.memset(ones, 1.0).then_inc(r_consts, 1)

                def unit(g, s, kind, order):
                    u = UNITS * g + s
                    for what, r in order:
                        if what == "gather":
                            x = u - FIRST_X + 1
                            if r == 0:
                                pool.wait_ge(rows_mm, 1 + 2 * x)
                                pool.wait_ge(tok_moved, 32)
                                pool.tensor_copy(tok_now[:], tok_of_slot[:, bass.ds(x * 2, 2)]).then_inc(tok_copied, 1)
                                pool.wait_ge(tok_copied, x + 1)
                                pool.sem_inc(waited_pool, 1)
                            pool.indirect_dma_start(rows[r][:], None, h2_rows,
                                                    bass.IndirectOffsetOnAxis(tok_now[:, r:r + 1], 0))\
                                .then_inc(rows_in[r], 16)
                        elif what == "ye_out":
                            e = (u - FIRST_X) * XPU + r
                            pool.wait_ge(ye_add, 1 + e + 1)
                            pool.sem_inc(waited_pool, 1)
                            pool.dma_start(scr["ye"][e], ye[:]).then_inc(ye_out, 16)
                        elif what == "add_x2":
                            i = s * SUB + r
                            pool.wait_ge(x2u_in, 16 * (s + 1))
                            pool.wait_ge(gb_mul, i + 1)
                            pool.tensor_tensor(acc[:, i], acc[:, i], x2u[:, r], ALU.add).then_inc(x2_add, 1)
                        elif what == "fetch":
                            i = tile_no(kind, s, r)
                            if r == 0:
                                pool.wait_ge(wxg_lo, 2 + 2 * E)
                                pool.wait_ge(wxd_lo, 2 + E)
                            if not (isinstance(i, int) and i < 2):
                                pool.wait_ge(cm_step, TOPK * (i - 1))
                            pool.tensor_copy(slot_now[r % 2][:], slot_top[:, i, :]).then_inc(slot_copied, 1)
                            pool.wait_ge(ye_out, 16 * E)
                            pool.wait_ge(slot_copied, i + 1)
                            pool.sem_inc(waited_pool, 1)
                            for k in range(TOPK):
                                pool.indirect_dma_start(y_buf[r % 2][k], None, ye_rows,
                                                        bass.IndirectOffsetOnAxis(slot_now[r % 2][:, k:k + 1], 0))\
                                    .then_inc(y_in[r % 2][k], 16)

                run_units(pool, "pool", unit)

            @block.scalar
            def _(act):
                def split_gu_w(n, c):
                    act.wait_ge(wgu_in, 16 * (n + 1))
                    nc.scalar.copy(ws[c][:, 0, gu_w], ws_raw[:, gu_w]).then_inc(wgu_hi, 1)

                def split_down_w(n, c):
                    act.wait_ge(wdn_in, 16 * (n + 1))
                    nc.scalar.copy(ws[c][:, 0, down_w], ws_raw[:, down_w]).then_inc(wdn_hi, 1)

                def unit(g, s, kind, order):
                    u, x = UNITS * g + s, UNITS * g + s - FIRST_X
                    e0 = x * XPU
                    for what, r in order:
                        if isinstance(r, int):
                            q, e = chunk_no(u, r, g == NGROUPS - 1), e0 + r
                        if what == "gate":
                            act.wait_ge(gate_mm, q + 1)
                            if not (isinstance(q, int) and q == 0):
                                act.wait_ge(gu_done, q)
                            nc.scalar.activation(sil[:], pair[r][0][:], ACT.Silu).then_inc(sil_done, 1)
                        elif what == "up":
                            act.wait_ge(gu_done, q + 1)
                            if not (isinstance(u, int) and u == 0):
                                act.wait_ge(dn_mm, SUB * u)
                            nc.scalar.copy(guT[r][:, 0], gu[:]).then_inc(gu_hi, 1)
                        elif what == "first_gu":
                            split_gu_w(r, r)
                        elif what == "first_down":
                            split_down_w(r, r)
                        elif what == "new_gu":
                            act.wait_ge(up_mm, q + 1)
                            split_gu_w(GROUP * (g + 1) + r, r)
                        elif what == "new_down":
                            act.wait_ge(dn_mm, SUB * u)
                            split_down_w(GROUP * g + r, r)
                        elif what == "route" and r == "exp":
                            act.wait_ge(r_dve, 1)
                            nc.scalar.activation(prob, prob, ACT.Exp).then_inc(r_exp, 1)
                            nc.scalar.activation(sig[:], logits[:, :, E], ACT.Sigmoid).then_inc(r_exp, 1)
                        elif what in ("split_g", "split_u"):
                            i = 0 if what == "split_g" else 1
                            slot = (3 * r + i) % RAW_SLOTS
                            act.wait_ge(xgu_mm, 1 + e)
                            act.wait_ge(wx_in[slot], raw_value(3 * r + i, x))
                            nc.scalar.copy(wx[i][:, 0, 0:KC * F], wx_raw[:, slot, 0:KC * F]).then_inc(wxg_hi, 1)
                        elif what == "split_d":
                            act.wait_ge(xd_mm, 1 + e)
                            slot = (3 * r + 2) % RAW_SLOTS
                            act.wait_ge(wx_in[slot], raw_value(3 * r + 2, x))
                            nc.scalar.copy(wx[2][:, 0], wx_raw[:, slot]).then_inc(wxd_hi, 1)
                        elif what == "rows":
                            act.wait_ge(rows_mm, 1 + 2 * x + r + 1)
                            act.wait_ge(xgu_mm, 1 + e0)
                            nc.scalar.copy(xs[r][:].rearrange("p h c m -> p c h m")[:, :, :, 0:CAP],
                                           psT[:].rearrange("p (c h m) -> p c h m", c=KC, h=2)).then_inc(rows_hi, 1)
                        elif what == "low":
                            act.wait_ge(xgu_mm, 1 + e + 1)
                            act.wait_ge(xadd, 1 + e)
                            nc.scalar.copy(low_g[:], psXG[CAP:P, 0:F]).then_inc(xlow, 1)
                            nc.scalar.copy(low_u[:], psXU[CAP:P, 0:F]).then_inc(xlow, 1)
                        elif what == "silu":
                            act.wait_ge(xsum, e + 1)
                            nc.scalar.activation(xg[:], xg[:], ACT.Silu).then_inc(xsil, 1)
                        elif what == "mid":
                            act.wait_ge(mid_mm, 1 + e + 1)
                            act.wait_ge(xd_mm, 1 + e)
                            nc.scalar.copy(xguT[:, :, 0:CAP], psT[:, 0:FX * CAP].rearrange("p (c m) -> p c m", c=FX))\
                                .then_inc(mid_hi, 1)
                        elif what == "exp_down":
                            act.wait_ge(xd_mm, 1 + e + 1)
                            act.wait_ge(ye_add, 1 + e)
                            nc.scalar.copy(low_y[:], psY[CAP:P, :]).then_inc(y_low, 1)

                run_units(act, "act", unit)

            @block.vector
            def _(dve):
                for s_, v_ in ((wxg_lo, 2), (wxd_lo, 2), (rows_lo, 1), (xadd, 1), (xgu_done, 1), (mid_lo, 1), (ye_add, 1)):
                    dve.sem_inc(s_, v_)
                links = [0]

                def link(ins):
                    links[0] += 1
                    ins.then_inc(r_chain, 1)
                    dve.wait_ge(r_chain, links[0])

                def split_gu_w(n, c):
                    dve.wait_ge(wgu_hi, n + 1)
                    nc.vector.tensor_tensor(ws[c][:, 1, gu_w], ws_raw[:, gu_w], raw(ws[c][:, 0, gu_w]), ALU.subtract)\
                        .then_inc(wgu_lo, 1)

                def split_down_w(n, c):
                    dve.wait_ge(wdn_hi, n + 1)
                    nc.vector.tensor_tensor(ws[c][:, 1, down_w], ws_raw[:, down_w], raw(ws[c][:, 0, down_w]), ALU.subtract)\
                        .then_inc(wdn_lo, 1)

                def route(r):
                    v = nc.vector
                    if r == "softmax":
                        dve.wait_ge(table_in, 16)
                        link(v.memset(free[:, used[0]:RAW_SLOTS * FX * D], 0.0))
                        link(v.reduce_max(small[:, 0], logits[:, :, 0:E], mybir.AxisListType.X))
                        v.tensor_tensor(prob, logits[:, :, 0:E], small[:, 0].unsqueeze(2).broadcast_to((P, NT, E)),
                                        ALU.subtract).then_inc(r_dve, 1)
                        dve.wait_ge(r_exp, 1)
                        link(v.reduce_sum(small[:, 1], prob, mybir.AxisListType.X))
                        link(v.reciprocal(small[:, 2], small[:, 1]))
                        link(v.tensor_tensor(prob, prob, small[:, 2].unsqueeze(2).broadcast_to((P, NT, E)), ALU.mult))
                        for t in range(NT):
                            last = v.max(top[:, t], prob[:, t])
                        link(last)
                        for t in range(NT):
                            last = v.max_index(top_i[:, t], top[:, t], prob[:, t])
                        link(last)
                    elif r == "one_hot":
                        link(v.tensor_copy(idx_f[:], top_i[:, :, 0:TOPK]))
                        link(v.tensor_tensor(one_hot, idx_f[:].unsqueeze(3).broadcast_to((P, NT, TOPK, E)),
                                             iota_e.unsqueeze(1).unsqueeze(1).broadcast_to((P, NT, TOPK, E)), ALU.is_equal))
                        link(v.tensor_copy(before, tables[:, TABLE_COLS - P:TABLE_COLS]))
                        with nc.allow_low_precision("zeros and ones"):
                            v.tensor_reduce(by_tile(mask), one_hot.rearrange("p t k e -> p t e k"),
                                            axis=mybir.AxisListType.X, op=ALU.add).then_inc(r_dve, 1)
                    elif r == "picks":
                        dve.wait_ge(r_pe, 1)
                        dve.wait_ge(r_dve, 2)
                        pos = by_tile(psXG[:])
                        link(v.tensor_tensor(picked, one_hot, pos.unsqueeze(2).broadcast_to((P, NT, TOPK, E)), ALU.mult))
                        link(v.tensor_reduce(pos_k[:], picked, axis=mybir.AxisListType.X, op=ALU.add))
                        link(v.tensor_scalar(valid[:], pos_k[:], float(CAP), None, ALU.is_lt))
                        link(v.tensor_scalar(pos_k[:], pos_k[:], float(CAP - 1), None, ALU.min))
                        link(v.scalar_tensor_tensor(pos_k[:], idx_f[:], float(CAP), pos_k[:], ALU.mult, ALU.add))
                        link(v.tensor_copy(slot_top[:], pos_k[:]))
                        link(v.reduce_sum(small[:, 3], top[:, :, 0:TOPK], mybir.AxisListType.X))
                        link(v.reciprocal(small[:, 1], small[:, 3]))
                        link(v.tensor_tensor(valid[:], valid[:], top[:, :, 0:TOPK], ALU.mult))
                        link(v.tensor_tensor(w_top[:], valid[:], small[:, 1].unsqueeze(2).broadcast_to((P, NT, TOPK)),
                                             ALU.mult))
                    elif r == "digits":
                        pos = by_tile(psXG[:])
                        link(v.scalar_tensor_tensor(posm, pos, 1.0, by_tile(mask), ALU.add, ALU.mult))
                        link(v.tensor_scalar(posm, posm, -1.0, None, ALU.add))
                        link(v.tensor_copy(pos_i, posm))
                        link(v.tensor_scalar(c1.bitcast(I32), pos_i, 3, None, ALU.arith_shift_right))
                        link(v.tensor_scalar(pos_i, pos_i, 7, None, ALU.bitwise_and))
                        link(v.tensor_copy(posm, c1.bitcast(I32)))
                        link(v.tensor_copy(c0, pos_i))
                    elif r in ("high", "low"):
                        shape = (P, PE_, S1)
                        digit, value = (digit1, posm) if r == "high" else (digit0, c0)
                        last = v.tensor_tensor(digit.rearrange("p t (e c) -> p (t e) c", c=S1),
                                               value.rearrange("p t e -> p (t e)").unsqueeze(2).broadcast_to(shape),
                                               iota8.unsqueeze(1).broadcast_to(shape), ALU.is_equal)
                        link(last)
                        if r == "low":
                            for t in range(NT):
                                v.tensor_scalar(digit0[:, t], digit0[:, t], token_id[:, t:t + 1], None, ALU.mult)\
                                    .then_inc(scaled, 1)
                    else:
                        dve.wait_ge(r_pe, 2)
                        for h in range(2):
                            src = (psXG if h == 0 else psXU)[:, 0:P].rearrange("p (e c) -> p c e", c=S1)
                            link(v.tensor_tensor(inv[:, h], src, own_half.unsqueeze(1).broadcast_to((P, S1, NT)), ALU.mult))
                        link(v.tensor_reduce(inv_f[:], inv[:], axis=mybir.AxisListType.X, op=ALU.add))
                        v.tensor_copy(inv_i[:], inv_f[:]).then_inc(r_dve, 1)

                def unit(g, s, kind, order):
                    u, x = UNITS * g + s, UNITS * g + s - FIRST_X
                    e0 = x * XPU
                    for what, r in order:
                        if isinstance(r, int):
                            q, e = chunk_no(u, r, g == NGROUPS - 1), e0 + r
                        if what == "mult":
                            dve.wait_ge(up_mm, q + 1)
                            dve.wait_ge(sil_done, q + 1)
                            if not (isinstance(q, int) and q == 0):
                                dve.wait_ge(gu_hi, q)
                                dve.wait_ge(gu_lo, q)
                            nc.vector.tensor_tensor(gu[:], sil[:], pair[r][1][:], ALU.mult).then_inc(gu_done, 1)
                        elif what == "gu_lo":
                            dve.wait_ge(gu_hi, q + 1)
                            nc.vector.tensor_tensor(guT[r][:, 1], gu[:], raw(guT[r][:, 0]), ALU.subtract).then_inc(gu_lo, 1)
                        elif what == "first_gu":
                            split_gu_w(r, r)
                        elif what == "first_down":
                            split_down_w(r, r)
                        elif what == "new_gu":
                            split_gu_w(GROUP * (g + 1) + r, r)
                        elif what == "new_down":
                            split_down_w(GROUP * g + r, r)
                        elif what == "down":
                            i = s * SUB + r
                            if r == 0:
                                dve.wait_ge(r_exp, 2)
                                if not (isinstance(u, int) and u == 0):
                                    dve.wait_ge(dn_evac, SUB * u)
                                nc.vector.tensor_copy(sig4[:], sig[:, bass.ds(s * SUB, SUB)]).then_inc(sig4_done, 1)
                                dve.wait_ge(sig4_done, u + 1)
                                if kind == "combine2":
                                    dve.wait_ge(cm_step, TOPK * (tile_no(kind, s, 1) + 1))
                            dve.wait_ge(dn_mm, SUB * u + r + 1)
                            if g == 0:
                                nc.vector.tensor_scalar(acc[:, i], down_bank[r][:], sig4[:, r:r + 1], None, ALU.mult)\
                                    .then_inc(dn_evac, 1)
                            else:
                                nc.vector.scalar_tensor_tensor(acc[:, i], down_bank[r][:], sig4[:, r:r + 1], acc[:, i],
                                                               ALU.mult, ALU.add).then_inc(dn_evac, 1)
                        elif what == "times_gb":
                            i = s * SUB + r
                            if r == 0:
                                dve.wait_ge(gb_in, 16)
                            dve.wait_ge(dn_evac, SUB * u + r + 1)
                            nc.vector.tensor_tensor(acc[:, i], acc[:, i], gb[:, s // 2, :], ALU.mult).then_inc(gb_mul, 1)
                        elif what == "add_x2":
                            i = s * SUB + r
                            if r == 0:
                                dve.wait_ge(x2u_in, 16 * UNITS)
                            dve.wait_ge(gb_mul, i + 1)
                            nc.vector.tensor_tensor(acc[:, i], acc[:, i], x2u[:, r], ALU.add).then_inc(last_add, 1)
                        elif what == "route":
                            route(r)
                        elif what in ("split_g", "split_u"):
                            i = 0 if what == "split_g" else 1
                            dve.wait_ge(wxg_hi, 2 * e + i + 1)
                            nc.vector.tensor_tensor(wx[i][:, 1, 0:KC * F], wx_raw[:, (3 * r + i) % RAW_SLOTS, 0:KC * F],
                                                    raw(wx[i][:, 0, 0:KC * F]), ALU.subtract).then_inc(wxg_lo, 1)
                        elif what == "split_d":
                            dve.wait_ge(wxd_hi, e + 1)
                            nc.vector.tensor_tensor(wx[2][:, 1], wx_raw[:, (3 * r + 2) % RAW_SLOTS], raw(wx[2][:, 0]),
                                                    ALU.subtract).then_inc(wxd_lo, 1)
                        elif what == "rows":
                            dve.wait_ge(rows_hi, 2 * x + r + 1)
                            v = xs[r][:].rearrange("p h c m -> p c h m")
                            nc.vector.tensor_tensor(v[:, :, :, CAP:P], psT[:].rearrange("p (c h m) -> p c h m", c=KC, h=2),
                                                    raw(v[:, :, :, 0:CAP]), ALU.subtract).then_inc(rows_lo, 1)
                        elif what == "sum":
                            dve.wait_ge(xlow, 2 * e + 2)
                            dve.wait_ge(xgu_done, 1 + e)
                            nc.vector.tensor_tensor(xg[:], psXG[0:CAP, 0:F], low_g[:], ALU.add).then_inc(xsum, 1)
                            nc.vector.tensor_tensor(xu[:], psXU[0:CAP, 0:F], low_u[:], ALU.add).then_inc(xadd, 1)
                        elif what == "xmul":
                            dve.wait_ge(xsil, e + 1)
                            dve.wait_ge(xadd, 1 + e + 1)
                            dve.wait_ge(mid_mm, 1 + e)
                            nc.vector.tensor_tensor(xgu[:, 0:F], xg[:], xu[:], ALU.mult).then_inc(xgu_done, 1)
                        elif what == "mid":
                            dve.wait_ge(mid_hi, e + 1)
                            nc.vector.tensor_tensor(xguT[:, :, CAP:P], psT[:, 0:FX * CAP].rearrange("p (c m) -> p c m", c=FX),
                                                    raw(xguT[:, :, 0:CAP]), ALU.subtract).then_inc(mid_lo, 1)
                        elif what == "exp_down":
                            dve.wait_ge(y_low, e + 1)
                            if not (isinstance(e, int) and e == 0):
                                dve.wait_ge(ye_out, 16 * e)
                            nc.vector.tensor_tensor(ye[:], psY[0:CAP, :], low_y[:], ALU.add).then_inc(ye_add, 1)
                        elif what == "combine":
                            i = tile_no(kind, s, r)
                            nc.vector.tensor_copy(w_now[:], w_top[:, i, :]).then_inc(w_copied, 1)
                            dve.wait_ge(w_copied, i + 1)
                            dve.wait_ge(dn_evac, SUB * u)
                            for k in range(TOPK):
                                if not (isinstance(i, int) and i + k == 0):
                                    dve.wait_ge(cm_step, TOPK * i + k)
                                dve.wait_ge(y_in[r % 2][k], 16 * tile_uses(kind, s, r))
                                nc.vector.scalar_tensor_tensor(acc[:, i], y_buf[r % 2][k], w_now[:, k:k + 1], acc[:, i],
                                                               ALU.mult, ALU.add).then_inc(cm_step, 1)

                run_units(dve, "dve", unit)

            @block.tensor
            def _(pe):
                for s_ in (rows_mm, xgu_mm, mid_mm, xd_mm):
                    pe.sem_inc(s_, 1)

                def product(out_, pairs):
                    passes = [(l[i], r[k]) for l, r in pairs for i, k in ((0, 0), (0, 1), (1, 0))]
                    for n, (l, r) in enumerate(passes):
                        last = nc.tensor.matmul(out_, l, r, start=n == 0, stop=n == len(passes) - 1)
                    return last

                def halves(ap, cols):
                    return ap[:, 0, cols], ap[:, 1, cols]

                def in_unit(part, c):
                    return hT[:, :, part, c, :]


                def unit(g, s, kind, order):
                    u, x = UNITS * g + s, UNITS * g + s - FIRST_X
                    e0, nch = x * XPU, chunks_of(g)
                    first = isinstance(u, int) and u == 0
                    for what, r in order:
                        if isinstance(r, int):
                            q, e = chunk_no(u, r, g == NGROUPS - 1), e0 + r
                        if what in ("gate", "up"):
                            which = 0 if what == "gate" else 1
                            if what == "gate":
                                pe.wait_ge(wgu_lo, GROUP * g + r + 1)
                                if r == 0:
                                    pe.wait_ge(hT_in, 16 * (u + 1))
                            if r == 0 and not first:
                                pe.wait_ge(dn_evac, SUB * u - 1 + which)
                            if r == 2:
                                pe.wait_ge(gu_done, q - 1)
                            product(pair[r][which][:],
                                    [(halves(ws[r][:], slice(which * D + c * P, which * D + (c + 1) * P)),
                                      (in_unit(0, c), in_unit(1, c))) for c in range(KC)])\
                                .then_inc(gate_mm if which == 0 else up_mm, 1)
                        elif what == "down":
                            if r == 0:
                                pe.wait_ge(wdn_lo, GROUP * g + nch)
                                pe.wait_ge(gu_lo, chunk_no(u, nch, g == NGROUPS - 1))
                            product(down_bank[r][:], [(halves(guT[c][:], slice(r * P, (r + 1) * P)), halves(ws[c][:], down_w))
                                                      for c in range(nch)]).then_inc(dn_mm, 1)
                        elif what == "route" and r == "positions":
                            pe.wait_ge(r_dve, 2)
                            pe.wait_ge(r_consts, 2)
                            nc.tensor.matmul(psXG[:], before, mask, start=True, stop=False)
                            for t in range(NT - 1):
                                left = NT - 1 - t
                                last = nc.tensor.matmul(psXG[:, (t + 1) * E:NT * E], ones,
                                                        mask[:, t * E:(t + 1) * E].unsqueeze(1).broadcast_to((P, left, E)),
                                                        start=False, stop=t == NT - 2)
                            last.then_inc(r_pe, 1)
                        elif what == "route":
                            pe.wait_ge(scaled, NT)
                            for h, ps in ((0, psXG), (1, psXU)):
                                for t in range(NT):
                                    last = nc.tensor.matmul(ps[:, 0:P], digit1[:, t, h * P:(h + 1) * P],
                                                            digit0[:, t, h * P:(h + 1) * P], start=t == 0, stop=t == NT - 1)
                            last.then_inc(r_pe, 1)
                        elif what == "rows":
                            pe.wait_ge(rows_in[r], 16 * (x + 1))
                            pe.wait_ge(mid_lo, 1 + e0 + 2 * r)
                            v = rows[r][:].rearrange("t (q c) -> t c q", c=KC)
                            for c in range(KC):
                                last = nc.tensor.transpose(psT[:, c * P:(c + 1) * P], v[:, c, :], ident[:])
                            last.then_inc(rows_mm, 1)
                        elif what == "gu":
                            pe.wait_ge(rows_lo, 1 + 2 * x + r // 2 + 1)
                            pe.wait_ge(wxg_lo, 2 + 2 * (e + 1))
                            pe.wait_ge(xadd, 1 + e)
                            for c in range(KC):
                                for ps, w in ((psXG, wx[0]), (psXU, wx[1])):
                                    for part in range(2):
                                        last = nc.tensor.matmul(ps[:, 0:F], xs[r // 2][:, r % 2, c, :],
                                                                w[:, part, c * F:(c + 1) * F],
                                                                start=c == 0 and part == 0, stop=c == KC - 1 and part == 1)
                            last.then_inc(xgu_mm, 1)
                        elif what == "mid":
                            pe.wait_ge(xgu_done, 1 + e + 1)
                            if r in (0, 2):
                                pe.wait_ge(rows_lo, 1 + 2 * x + r // 2 + 1)
                            else:
                                pe.wait_ge(mid_lo, 1 + e)
                            pe.sem_inc(waited_pe, 1)
                            for c in range(FX):
                                last = nc.tensor.transpose(psT[:, c * CAP:(c + 1) * CAP], xgu[:, c * P:(c + 1) * P],
                                                           ident[0:CAP, 0:CAP])
                            last.then_inc(mid_mm, 1)
                        elif what == "exp_down":
                            pe.wait_ge(mid_lo, 1 + e + 1)
                            pe.wait_ge(wxd_lo, 2 + e + 1)
                            pe.wait_ge(ye_add, 1 + e)
                            for c in range(FX):
                                k = min(P, F - c * P)
                                for part in range(2):
                                    last = nc.tensor.matmul(psY[:], xguT[0:k, c, :], wx[2][0:k, part, c * D:(c + 1) * D],
                                                            start=c == 0 and part == 0, stop=c == FX - 1 and part == 1)
                            last.then_inc(xd_mm, 1)

                run_units(pe, "pe", unit)


def adaln_block(nc, ins, out):
    scr = {
        "ye": nc.dram_tensor("ye_scratch", (E, CAP, D), F32).ap(),
        "slots": nc.dram_tensor("slots_scratch", (E * CAP,), I32).ap(),
        "gb": nc.dram_tensor("gb_scratch", (P, B, D), F32).ap(),
        "x2": nc.dram_tensor("x2_scratch", (B, TPB, P, D), F32).ap(),
        "h2": nc.dram_tensor("h2_scratch", (B, TPB, P, D), F32).ap(),
        "h2T": nc.dram_tensor("h2T_scratch", (B, TPB, P, 2 * D), F32).ap(),
    }
    with ExitStack() as ctx:
        both = {**ins, "logits": ctx.enter_context(nc.sbuf_tensor("logits", [P, NT, RW], F32)),
                "ident": ctx.enter_context(nc.sbuf_tensor("ident", [P, P], F32))}
        for e in ("pool", "dve", "sp", "pe"):
            both[f"waited_{e}"] = ctx.enter_context(nc.semaphore(f"waited_{e}"))
        attention(nc, both, scr)
        ffn(nc, both, scr, out)


_OUTS = [((B, T, D), "float32")]


def _layout(inputs):
    import numpy as np
    a = {k: np.asarray(v) for k, v in inputs.items()}
    pos = np.arange(T, dtype=np.float32)
    inv = (1.0 / 10000.0 ** (np.arange(0, DK, 2, dtype=np.float32) / DK)).astype(np.float32)
    ang = (pos[:, None] * inv[None, :]).astype(np.float32)
    cos = np.repeat(np.cos(ang), 2, axis=1).astype(np.float32)
    sin = np.repeat(np.sin(ang), 2, axis=1).astype(np.float32)
    sin[:, 1::2] *= -1
    per_tile = lambda t: np.ascontiguousarray(t.reshape(TPB, P, DK).transpose(1, 0, 2))
    rows, cols = np.arange(P)[:, None] // DK, np.concatenate([np.arange(P) // DK, np.arange(HG)])[None]
    d = {
        "x": a["L0_attn_x"],
        "c": np.ascontiguousarray(a["L0_c"].reshape(B, P, KC).transpose(1, 2, 0)),
        "wmod": a["L0_wmod"],
        "cos": per_tile(cos), "sin": per_tile(sin), "mask": (rows == cols).astype(np.float32),
        "wr": np.concatenate([a["L0_ffn_Wr"], a["L0_ffn_Wse"], np.zeros((D, 1), np.float32)], axis=1),
    }
    gate_up = lambda w: w.reshape(P, KC, FCH, P).transpose(2, 0, 1, 3).reshape(FCH, P, D)
    d["ws"] = np.ascontiguousarray(np.concatenate(
        [gate_up(a["L0_ffn_Wsg"]), gate_up(a["L0_ffn_Wsu"]), a["L0_ffn_Wsd"].reshape(FCH, P, D)], axis=2))
    d["wg_x"], d["wu_x"], d["wd_x"] = a["L0_ffn_Wg"], a["L0_ffn_Wu"], a["L0_ffn_Wd"]
    const = lambda row: np.broadcast_to(np.asarray(row, np.float32), (P, len(row)))
    p = np.arange(P)[:, None]
    d["tables"] = np.ascontiguousarray(np.concatenate(
        [const(range(8)), const(range(E)), p + P * np.arange(NT)[None], p // 8 == np.arange(NT)[None],
         p < np.arange(P)[None]], axis=1).astype(np.float32))
    for n in "kvqgo":
        d[f"w{n}"] = np.ascontiguousarray(a[f"L0_attn_W{n}"].T)
        d[f"b{n}"] = a[f"L0_attn_b{n}"]
    return d


def kernel(**inputs):
    import numpy as _np
    import concourse.bacc as _bacc
    from concourse.bass_utils import run_bass_kernel_spmd as _run

    nc = _bacc.Bacc("TRN2", target_bir_lowering=False, num_devices=1)
    arrays, ins = {}, {}
    for name, a in _layout(inputs).items():
        arrays[f"in_{name}"] = a
        ins[name] = nc.dram_tensor(f"in_{name}", a.shape, mybir.dt.from_np(a.dtype), kind="ExternalInput").ap()
    shape, dtype = _OUTS[0]
    out = nc.dram_tensor("out_0", shape, mybir.dt.from_np(_np.dtype(dtype)), kind="ExternalOutput").ap()
    adaln_block(nc, ins, out)
    r = _run(nc, [arrays], core_ids=[0])
    return r.results[0]["out_0"]
```

```python
import concourse.bass as bass
from concourse import mybir
from contextlib import ExitStack

F32 = mybir.dt.float32
F32R = mybir.dt.float32r
BF16 = mybir.dt.bfloat16
F16 = mybir.dt.float16
I32 = mybir.dt.int32
U32 = mybir.dt.uint32
ALU = mybir.AluOpType
ACT = mybir.ActivationFunctionType

P = 128
B, T, D = 2, 1024, 512
H, DK = 16, 32
CS = 64
KC = D // P
TPB = T // P
NT = B * TPB
HG = P // DK
NG = H // HG
SW = P + HG
LN_EPS = 1e-5
DEN_EPS = 1e-6
E, TOPK, CAP = 32, 4, 64
RW = E + 2
F, FS = 352, 1408


def raw(ap):
    return ap.bitcast(F32)


def lag(j, b, d):
    return j + (b - d) // 2, (b - d) % 2


def real(j, b, d):
    return not isinstance(j, int) or 0 <= 2 * j + b - d < NT


def done(j, b, d=0, per=1, k=None):
    return per * (2 * j + b - d) + (per if k is None else k)


def wait_tile(eng, sem, j, b, d=0, per=1, k=None):
    if real(j, b, d):
        value = done(j, b, d, per, k)
        if not (isinstance(value, int) and value <= 0):
            eng.wait_ge(sem, value)


LOOP_J = (2, 7)
STATIC_TAIL = [(7, 0), (7, 1), (8, 0)]


def run_steps(eng, step, prepare=lambda part: None, begin_ffn=lambda part: None):
    prepare(0)
    step(-1, 0)
    step(-1, 1)
    prepare(1)
    step(0, 0)
    prepare(2)
    step(0, 1)
    prepare(3)
    step(1, 0)
    step(1, 1)
    with eng.Fori(*LOOP_J) as j:
        step(j, 0)
        step(j, 1)
    for j, b in STATIC_TAIL:
        step(j, b)
    begin_ffn(0)
    step(8, 1)
    begin_ffn(1)
    step(9, 0)
    begin_ffn(2)


def product(nc, out, pairs):
    passes = [(l[u], r[w]) for l, r in pairs for u, w in ((0, 0), (0, 1), (1, 0))]
    for n, (l, r) in enumerate(passes):
        last = nc.tensor.matmul(out, l, r, start=n == 0, stop=n == len(passes) - 1)
    return last


class SharedFFN:

    def __init__(self, nc, io, scr, area, rows, psum, sem):
        self.nc, self.weights = nc, io["ws"]
        cols = 2 * 3 * D
        cut = lambda i, n: area[:, i:i + n]
        self.ws = [cut(c * cols, cols).rearrange("p (s n) -> p s n", s=2) for c in range(GROUP)]
        self.hT = cut(GROUP * cols, SUB * 2 * D).rearrange("p (i s c t) -> p i s c t", i=SUB, s=2, c=KC)
        used = GROUP * cols + SUB * 2 * D
        self.guT = [cut(used + c * 2 * D, 2 * D).rearrange("p (s t) -> p s t", s=2) for c in range(GROUP)]
        self.ws_raw, self.gu = rows[:, 0:3 * D], rows[:, 3 * D:4 * D]
        self.gu_w, self.down_w = slice(0, 2 * D), slice(2 * D, 3 * D)
        self.h2T = scr["h2T"].rearrange("b j p n -> p (b j) n")
        self.bankA, self.bankB = [psum[:, 0], psum[:, 1]], [psum[:, 4], psum[:, 5]]
        self.pair = [self.bankA, self.bankB, self.bankA]
        self.wgu_in, self.wgu_hi, self.wgu_lo = sem("wgu_in"), sem("wgu_hi"), sem("wgu_lo")
        self.wdn_in, self.wdn_hi, self.wdn_lo = sem("wdn_in"), sem("wdn_hi"), sem("wdn_lo")
        self.hT_in, self.gate_mm, self.up_mm = sem("hT_in"), sem("gate_mm"), sem("up_mm")

    def load_gu(self, sp, n):
        if n:
            sp.wait_ge(self.wgu_lo, n)
        sp.dma_start(self.ws_raw[:, self.gu_w], self.weights[n][:, self.gu_w]).then_inc(self.wgu_in, 16)

    def load_down(self, sp, n):
        if n:
            sp.wait_ge(self.wdn_lo, n)
        sp.dma_start(self.ws_raw[:, self.down_w], self.weights[n][:, self.down_w]).then_inc(self.wdn_in, 16)

    def load_tokens(self, sp, s):
        sp.dma_start(raw(self.hT.rearrange("p i s c t -> p i (s c t)")), self.h2T[:, bass.ds(s * SUB, SUB), :])\
          .then_inc(self.hT_in, 16)

    def gu_high(self, act, n, c):
        act.wait_ge(self.wgu_in, 16 * (n + 1))
        self.nc.scalar.copy(self.ws[c][:, 0, self.gu_w], self.ws_raw[:, self.gu_w]).then_inc(self.wgu_hi, 1)

    def down_high(self, act, n, c):
        act.wait_ge(self.wdn_in, 16 * (n + 1))
        self.nc.scalar.copy(self.ws[c][:, 0, self.down_w], self.ws_raw[:, self.down_w]).then_inc(self.wdn_hi, 1)

    def gu_low(self, dve, n, c):
        dve.wait_ge(self.wgu_hi, n + 1)
        self.nc.vector.tensor_tensor(self.ws[c][:, 1, self.gu_w], self.ws_raw[:, self.gu_w],
                                     raw(self.ws[c][:, 0, self.gu_w]), ALU.subtract).then_inc(self.wgu_lo, 1)

    def down_low(self, dve, n, c):
        dve.wait_ge(self.wdn_hi, n + 1)
        self.nc.vector.tensor_tensor(self.ws[c][:, 1, self.down_w], self.ws_raw[:, self.down_w],
                                     raw(self.ws[c][:, 0, self.down_w]), ALU.subtract).then_inc(self.wdn_lo, 1)

    def multiply(self, which, r):
        w = lambda c: slice(which * D + c * P, which * D + (c + 1) * P)
        product(self.nc, self.pair[r][which],
                [((self.ws[r][:, 0, w(c)], self.ws[r][:, 1, w(c)]), (self.hT[:, :, 0, c, :], self.hT[:, :, 1, c, :]))
                 for c in range(KC)]).then_inc(self.gate_mm if which == 0 else self.up_mm, 1)


def attention(nc, io, scr):
    with ExitStack() as ctx:
        def sb(name, shape, dt=F32):
            return ctx.enter_context(nc.sbuf_tensor(name, shape, dt))

        def sem(name):
            return ctx.enter_context(nc.semaphore(name))

        logits, ident = io["logits"], io["ident"]
        wnames = ["k", "v", "q", "g", "o"]
        area, psum, shared = io["area"], io["psum"], io["shared"]
        in_area = lambda i: area[:, i * KC * D:(i + 1) * KC * D].rearrange("p (c n) -> p c n", c=KC)
        w_hi = {n: in_area(2 * i) for i, n in enumerate("kvqg")}
        w_lo = {n: in_area(2 * i + 1) for i, n in enumerate("kvqg")}
        w_hi["o"], w_lo["o"] = sb("wo_hi", [P, KC, D], F32R), sb("wo_lo", [P, KC, D], F32R)
        wr_hi, wr_lo = sb("wr_hi", [P, KC, RW], F32R), sb("wr_lo", [P, KC, RW], F32R)
        group_mask = sb("group_mask", [P, SW])
        c_silu = sb("c_silu", [P, KC, B, P // B])
        cT = sb("cT", [P, KC, B])
        cS = sb("cS", [P, KC, B])
        mod = {n: sb(f"mod_{n}", [P, B, D]) for n in ("sa", "ca1", "ga", "gabo", "sb", "cb1")}
        bias_k, bias_v, bias_q, bias_g = (sb(f"bias_{n}", [P, D]) for n in "kvqg")
        cos_t, sin_t = sb("cos_t", [P, TPB, DK]), sb("sin_t", [P, TPB, DK])
        NSTAGE = 3
        scratch = sb("scratch", [P, NSTAGE * KC * D])
        stage = [scratch[:, s * KC * D:(s + 1) * KC * D] for s in range(NSTAGE)]
        y = scratch[:, 0:2 * D]
        t1 = scratch[:, 2 * D:4 * D]
        t2 = scratch[:, 4 * D:6 * D]
        qk = {"q": slice(0, D), "k": slice(D, 2 * D)}
        feat = [scratch[:, 6 * D:8 * D], scratch[:, 8 * D:10 * D]]
        o_buf = scratch[:, 10 * D:11 * D]
        o1_buf = scratch[:, 11 * D:12 * D]
        rows = io["rows"]
        xin = [rows[:, i * D:(i + 1) * D] for i in range(2)]
        xhat = sb("xhat", [P, D])
        h_buf = [rows[:, (2 + i) * D:(3 + i) * D] for i in range(2)]
        hT = [sb(f"hT{i}", [P, 2, KC, P], F32R) for i in range(2)]
        v_buf = [sb(f"v{i}", [P, NG, SW]) for i in range(2)]
        th = [sb(f"th{i}", [P, D]) for i in range(2)]
        qT = sb("qT", [P, NG, P])
        state = [[sb(f"state{b}{c}", [P, NG, SW]) for c in range(2)] for b in range(2)]
        blocks = [sb(f"blocks{c}", [P, NG, SW]) for c in range(2)]
        rden = sb("rden", [P, H])
        rden2 = sb("rden2", [P, H])
        oT = sb("oT", [P, 2, KC, P], F32R)
        xres = [sb(f"xres{i}", [P, D]) for i in range(2)]
        proj = sb("proj", [P, D])
        x2 = [sb(f"x2_{i}", [P, D]) for i in range(2)]
        xhat2 = proj
        h2_both = sb("h2_both", [P, B, D])
        h2 = [h2_both[:, i, :] for i in range(2)]
        mod_a, mod_b = h2
        h2T = sb("h2T", [P, 2, KC, P], F32R)
        st1, st2 = sb("st1", [P, 6]), sb("st2", [P, 6])
        mv1, mv2 = [sb(f"mv1_{i}", [P, 2]) for i in range(2)], [sb(f"mv2_{i}", [P, 2]) for i in range(2)]
        rs1, rs2 = [sb(f"rs1_{i}", [P, 2]) for i in range(2)], [sb(f"rs2_{i}", [P, 2]) for i in range(2)]
        minus_half = sb("minus_half", [P, 1])

        bank = [psum[:, i] for i in range(4)]
        psS, psN = psum[:, 4:6], psum[:, 6:8]

        waited_pool, waited_dve, waited_sp = (io[f"waited_{e}"] for e in ("pool", "dve", "sp"))
        c_in, small_in = sem("c_in"), sem("small_in")
        stage_in = [sem(f"stage_in{s}") for s in range(NSTAGE)]
        hi_done, lo_done = sem("hi_done"), sem("lo_done")
        const_ready = sem("const_ready")
        csilu_act, csilu_ready = sem("csilu_act"), sem("csilu_ready")
        mod_mm, mod_tmp = sem("mod_mm"), sem("mod_tmp")
        mod_ready = sem("mod_ready")
        gb_out = sem("gb_out")
        x_in = [sem(f"x_in{i}") for i in range(2)]
        xres_in = [sem(f"xres_in{i}") for i in range(2)]
        st1_done, mv1_done, rs1_a, rs1_done = sem("st1_done"), sem("mv1_done"), sem("rs1_a"), sem("rs1_done")
        xhat_done, h_a, h_done = sem("xhat_done"), sem("h_a"), sem("h_done")
        hT_mm, hT_hi, hT_lo = sem("hT_mm"), sem("hT_hi"), sem("hT_lo")
        k_mm, v_mm, q_mm, g_mm = sem("k_mm"), sem("v_mm"), sem("q_mm"), sem("g_mm")
        k_out, v_out, q_out, g_out = sem("k_out"), sem("v_out"), sem("q_out"), sem("g_out")
        tanh_done = sem("tanh_done")
        rope_cos, rope_sin, rope_done, relu_done, exp_done, feat_done = (
            {n: sem(f"{what}_{n}") for n in "qk"}
            for what in ("rope_cos", "rope_sin", "rope_done", "relu_done", "exp_done", "feat_done"))
        qT_mm, qT_done = sem("qT_mm"), sem("qT_done")
        s_mm, state_done, blocks_done = sem("s_mm"), sem("state_done"), sem("blocks_done")
        n_mm = sem("n_mm")
        den_a, den_done, o_half, o_done = sem("den_a"), sem("den_done"), sem("o_half"), sem("o_done")
        oT_mm, oT_hi, oT_lo = sem("oT_mm"), sem("oT_hi"), sem("oT_lo")
        o_mm, proj_done, xg_done, x2_done = sem("o_mm"), sem("proj_done"), sem("xg_done"), sem("x2_done")
        st2_done, mv2_done, rs2_a, rs2_done = sem("st2_done"), sem("mv2_done"), sem("rs2_a"), sem("rs2_done")
        xhat2_done, h2_a, h2_done = sem("xhat2_done"), sem("h2_a"), sem("h2_done")
        h2T_mm, h2T_hi, h2T_lo = sem("h2T_mm"), sem("h2T_hi"), sem("h2T_lo")
        r_mm, logits_done = sem("r_mm"), sem("logits_done")
        x2_out = [sem(f"x2_out{i}") for i in range(2)]
        h2_out = [sem(f"h2_out{i}") for i in range(2)]
        h2T_out = sem("h2T_out")

        MODS = ["sa", "ca", "ga", "sb", "cb", "gb"]
        jobs = ["sa", "ca", "k", "v", "q", "g", "ga", "o", "cb", "sb", "gb"]
        mod_no = {n: i for i, n in enumerate(x for x in jobs if x in MODS)}
        split_no = {n: i for i, n in enumerate(x for x in jobs if x not in MODS)}
        copies_before = {n: 4 * i for n, i in mod_no.items()}

        parts = [jobs[:6], jobs[6:-1], jobs[-1:]]
        slot = {n: i % NSTAGE for i, n in enumerate(jobs[:-1])}
        slot["gb"] = NSTAGE - 1
        uses = {n: sum(slot[x] == slot[n] for x in jobs[:i + 1]) for i, n in enumerate(jobs)}

        def slot_free(eng, n):
            old = [x for x in jobs[:jobs.index(n)] if slot[x] == slot[n]]
            if old and old[-1] in MODS:
                eng.wait_ge(mod_mm, mod_no[old[-1]] + 1)
            elif old:
                eng.wait_ge(lo_done, split_no[old[-1]] + 1)

        def slot_in(eng, n):
            eng.wait_ge(stage_in[slot[n]], 16 * uses[n])

        mod_bank = [psS[:, 0], psS[:, 1], psN[:, 0], psN[:, 1]]

        wT = {n: io[f"w{n}"].rearrange("(p c) n -> p c n", c=KC) for n in wnames}
        wmod = io["wmod"].rearrange("(p c) (m n) -> m p c n", c=KC, m=6)
        x_t = io["x"].rearrange("b (j p) d -> b j p d", p=P)

        with nc.Block() as block:
            @block.sync
            def _(sp):
                def load(n):
                    slot_free(sp, n)
                    src = wmod[MODS.index(n)] if n in MODS else wT[n]
                    sp.dma_start(stage[slot[n]].rearrange("p (c n) -> p c n", c=KC), src).then_inc(stage_in[slot[n]], 16)

                def prepare(part):
                    if part == 0:
                        sp.dma_start(cT[:], io["c"]).then_inc(c_in, 16)
                        for n in parts[0][:NSTAGE]:
                            load(n)
                        sp.dma_start(proj[:, 0:KC * RW].rearrange("p (c n) -> p c n", c=KC),
                                     io["wr"].rearrange("(p c) n -> p c n", c=KC)).then_inc(small_in, 16)
                        for n, bt in (("k", bias_k), ("v", bias_v), ("q", bias_q), ("g", bias_g)):
                            sp.dma_start(bt[:], io[f"b{n}"].partition_broadcast(P)).then_inc(small_in, 16)
                        sp.dma_start(mod["gabo"][:, 0, :], io["bo"].partition_broadcast(P)).then_inc(small_in, 16)
                        sp.dma_start(cos_t[:], io["cos"]).then_inc(small_in, 16)
                        sp.dma_start(sin_t[:], io["sin"]).then_inc(small_in, 16)
                        sp.dma_start(group_mask[:], io["mask"]).then_inc(small_in, 16)
                        for n in parts[0][NSTAGE:]:
                            load(n)
                    elif part == 1:
                        for n in parts[1] + parts[2]:
                            load(n)
                    elif part == 3:
                        sp.wait_ge(mod_ready, copies_before["gb"] + 4)
                        for bb in range(B):
                            sp.dma_start(scr["gb"][:, bb, :], x2[bb][:]).then_inc(gb_out, 16)

                def step(j, b):
                    if real(j, b, -2):
                        jn, bn = lag(j, b, -2)
                        wait_tile(sp, xhat_done, j, b, 0)
                        sp.dma_start(xin[bn], x_t[bn, jn]).then_inc(x_in[bn], 16)
                    if real(j, b, 3):
                        jl, bl = lag(j, b, 3)
                        wait_tile(sp, x2_done, j, b, 3)
                        sp.sem_inc(waited_sp, 1)
                        sp.dma_start(scr["x2"][bl, jl], x2[bl][:]).then_inc(x2_out[bl], 16)
                        wait_tile(sp, h2_done, j, b, 3)
                        sp.dma_start(scr["h2"][bl, jl], h2[bl]).then_inc(h2_out[bl], 16)
                    if real(j, b, 1):
                        jl, bl = lag(j, b, 1)
                        wait_tile(sp, x2_done, j, b, 3)
                        sp.dma_start(xres[bl][:], x_t[bl, jl]).then_inc(xres_in[bl], 16)
                    if real(j, b, 3):
                        jl, bl = lag(j, b, 3)
                        wait_tile(sp, h2T_lo, j, b, 3)
                        sp.dma_start(scr["h2T"][bl, jl], raw(h2T[:]).rearrange("p s c t -> p (s c t)"))\
                          .then_inc(h2T_out, 16)

                def begin_ffn(part):
                    if part == 0:
                        sp.wait_ge(g_mm, NT)
                        sp.wait_ge(h2T_out, 16 * B * SUB)
                        shared.load_gu(sp, 0)
                        shared.load_tokens(sp, 0)
                    elif part == 1:
                        shared.load_gu(sp, 1)
                        shared.load_down(sp, 0)
                    else:
                        shared.load_gu(sp, 2)
                        shared.load_down(sp, 1)

                run_steps(sp, step, prepare, begin_ffn)
                sp.wait_ge(gb_out, 32)
                sp.wait_ge(h2T_out, 16 * NT)
                for s in (x2_out, h2_out):
                    for i in range(2):
                        sp.wait_ge(s[i], 16 * TPB)

            @block.gpsimd
            def _(pool):
                pool.memset(ident[:], 0.0).then_inc(const_ready, 1)
                pool.memset(minus_half[:], -0.5).then_inc(const_ready, 1)
                for i in range(2):
                    pool.memset(v_buf[i][:, :, P:SW], 1.0).then_inc(const_ready, 1)
                    pool.memset(state[i][1][:], 0.0).then_inc(const_ready, 1)
                pool.wait_ge(const_ready, 6)
                pool.affine_select(out=ident[:], in_=ident[:], compare_op=ALU.not_equal, fill=1.0, base=0,
                                   pattern=[[-1, P]], channel_multiplier=1).then_inc(const_ready, 1)

                def block_diagonal(j, b, c):
                    jl, bl = lag(j, b, 1)
                    wait_tile(pool, state_done, j, b, 1, 2, c + 1)
                    wait_tile(pool, n_mm, j, b, 2)
                    pool.tensor_tensor(blocks[c][:], state[bl][c][:], group_mask[:].unsqueeze(1).broadcast_to((P, NG, SW)),
                                       ALU.mult).then_inc(blocks_done, 1)

                def sine(j, b, n):
                    wait_tile(pool, (q_out if n == "q" else k_out), j, b)
                    wait_tile(pool, rope_done[n], j, b, 1)
                    pool.sem_inc(waited_pool, 1)
                    pool.tensor_tensor(t2[:, qk[n]].rearrange("p (h e) -> p h e", e=DK),
                                       y[:, qk[n]].rearrange("p (h e) -> p h e", e=DK),
                                       sin_t[:, j, :].unsqueeze(1).broadcast_to((P, H, DK)),
                                       ALU.mult).then_inc(rope_sin[n], 1)

                def step(j, b):
                    if real(j, b, 0):
                        sine(j, b, "k")
                    if real(j, b, 1):
                        block_diagonal(j, b, 0)
                    if real(j, b, 2):
                        jl, bl = lag(j, b, 2)
                        pool.wait_ge(xres_in[bl], 16 * (jl + 1))
                        pool.tensor_tensor(xres[bl][:], xres[bl][:], mod["gabo"][:, bl, :], ALU.add)\
                            .then_inc(xg_done, 1)
                    if real(j, b, 1):
                        block_diagonal(j, b, 1)
                    if real(j, b, -2):
                        jn, bn = lag(j, b, -2)
                        wait_tile(pool, mv1_done, j, b, -2)
                        pool.sem_inc(waited_pool, 1)
                        pool.tensor_scalar(rs1[bn][:, 0:1], mv1[bn][:, 1:2], LN_EPS, None, ALU.add).then_inc(rs1_a, 1)
                        wait_tile(pool, rs1_a, j, b, -2)
                        pool.tensor_tensor(rs1[bn][:, 1:2], rs1[bn][:, 0:1], minus_half[:], ALU.pow)\
                            .then_inc(rs1_done, 1)
                    if real(j, b, 0):
                        sine(j, b, "q")
                    if real(j, b, -2):
                        jn, bn = lag(j, b, -2)
                        wait_tile(pool, xhat_done, j, b, -2)
                        pool.wait_ge(mod_ready, copies_before["ca"] + 4)
                        wait_tile(pool, hT_mm, j, b, 0)
                        pool.tensor_tensor(h_buf[bn], xhat[:], mod["ca1"][:, bn, :], ALU.mult).then_inc(h_a, 1)
                        wait_tile(pool, h_a, j, b, -2)
                        pool.tensor_tensor(h_buf[bn], h_buf[bn], mod["sa"][:, bn, :], ALU.add)\
                            .then_inc(h_done, 1)
                    if real(j, b, 2):
                        jl, bl = lag(j, b, 2)
                        wait_tile(pool, mv2_done, j, b, 2)
                        pool.sem_inc(waited_pool, 1)
                        pool.tensor_scalar(rs2[bl][:, 0:1], mv2[bl][:, 1:2], LN_EPS, None, ALU.add).then_inc(rs2_a, 1)
                        wait_tile(pool, rs2_a, j, b, 2)
                        pool.tensor_tensor(rs2[bl][:, 1:2], rs2[bl][:, 0:1], minus_half[:], ALU.pow)\
                            .then_inc(rs2_done, 1)
                    if real(j, b, 2):
                        jl, bl = lag(j, b, 2)
                        wait_tile(pool, xhat2_done, j, b, 2)
                        pool.wait_ge(mod_ready, copies_before["gb"])
                        if real(j, b, 4):
                            pool.wait_ge(h2_out[bl], 16 * jl)
                            wait_tile(pool, h2T_mm, j, b, 4)
                        pool.tensor_tensor(h2[bl], xhat2[:], mod["cb1"][:, bl, :], ALU.mult).then_inc(h2_a, 1)
                        wait_tile(pool, h2_a, j, b, 2)
                        pool.tensor_tensor(h2[bl], h2[bl], mod["sb"][:, bl, :], ALU.add).then_inc(h2_done, 1)

                run_steps(pool, step)

            @block.scalar
            def _(act):
                def prepare(part):
                    if part == 0:
                        act.wait_ge(c_in, 16)
                        nc.scalar.activation(cS[:], cT[:], ACT.Silu).then_inc(csilu_act, 1)
                    for n in parts[part] if part < 2 else []:
                        if n not in MODS:
                            slot_in(act, n)
                            nc.scalar.copy(w_hi[n][:], stage[slot[n]].rearrange("p (c n) -> p c n", c=KC))\
                                .then_inc(hi_done, 1)
                    if part == 0:
                        act.wait_ge(small_in, 144)
                        nc.scalar.copy(wr_hi[:], proj[:, 0:KC * RW].rearrange("p (c n) -> p c n", c=KC))\
                            .then_inc(csilu_act, 1)

                def exponential(j, b, n):
                    wait_tile(act, rope_done[n], j, b)
                    nc.scalar.activation(t1[:, qk[n]], y[:, qk[n]], ACT.Relu, scale=-1.0).then_inc(relu_done[n], 1)
                    wait_tile(act, relu_done[n], j, b)
                    nc.scalar.activation(t1[:, qk[n]], t1[:, qk[n]], ACT.Exp, scale=-1.0).then_inc(exp_done[n], 1)

                def step(j, b):
                    if real(j, b, 3):
                        jl, bl = lag(j, b, 3)
                        wait_tile(act, h2T_mm, j, b, 3)
                        if real(j, b, 4):
                            act.wait_ge(h2T_out, 16 * (2 * j + b - 3))
                            wait_tile(act, r_mm, j, b, 4)
                        nc.scalar.copy(h2T[:, 0], bank[2][:].rearrange("p (c t) -> p c t", c=KC)).then_inc(h2T_hi, 1)
                    if real(j, b, 0):
                        exponential(j, b, "k")
                    if real(j, b, 2):
                        wait_tile(act, oT_mm, j, b, 2)
                        wait_tile(act, o_mm, j, b, 3)
                        nc.scalar.copy(oT[:, 0], bank[3][:].rearrange("p (c t) -> p c t", c=KC)).then_inc(oT_hi, 1)
                    if real(j, b, 1):
                        wait_tile(act, qT_mm, j, b, 1)
                        wait_tile(act, n_mm, j, b, 2)
                        nc.scalar.copy(qT[:], bank[3][:].rearrange("p (g t) -> p g t", g=NG)).then_inc(qT_done, 1)
                    if real(j, b, 0):
                        exponential(j, b, "q")
                    if real(j, b, -1):
                        jn, bn = lag(j, b, -1)
                        wait_tile(act, hT_mm, j, b, -1)
                        wait_tile(act, g_mm, j, b, 1)
                        nc.scalar.copy(hT[bn][:, 0], bank[0][:].rearrange("p (c t) -> p c t", c=KC)).then_inc(hT_hi, 1)
                    if real(j, b, 0):
                        wait_tile(act, g_out, j, b)
                        nc.scalar.activation(th[b][:], th[b][:], ACT.Tanh, scale=0.5).then_inc(tanh_done, 1)

                def begin_ffn(part):
                    if part < 2:
                        shared.gu_high(act, part, part)
                    else:
                        shared.down_high(act, 0, 0)

                run_steps(act, step, prepare, begin_ffn)

            @block.vector
            def _(dve):
                tmp_count = [0]

                def tmp(ins):
                    tmp_count[0] += 1
                    ins.then_inc(mod_tmp, 1)
                    dve.wait_ge(mod_tmp, tmp_count[0])

                def prepare(part):
                    if part == 2:
                        return
                    part = min(part, 2)
                    if part == 0:
                        dve.wait_ge(csilu_act, 1)
                        nc.vector.tensor_copy(c_silu[:], cS[:].unsqueeze(3).broadcast_to((P, KC, B, P // B)))\
                            .then_inc(csilu_ready, 1)
                    for n in parts[part]:
                        if n in MODS:
                            modulation(n)
                        else:
                            dve.wait_ge(hi_done, split_no[n] + 1)
                            nc.vector.tensor_tensor(w_lo[n][:], stage[slot[n]].rearrange("p (c n) -> p c n", c=KC),
                                                    raw(w_hi[n][:]), ALU.subtract).then_inc(lo_done, 1)
                    if part == 0:
                        dve.wait_ge(csilu_act, 2)
                        nc.vector.tensor_tensor(wr_lo[:], proj[:, 0:KC * RW].rearrange("p (c n) -> p c n", c=KC),
                                                raw(wr_hi[:]), ALU.subtract).then_inc(csilu_ready, 1)
                        dve.wait_ge(csilu_ready, 2)
                        dve.wait_ge(const_ready, 6)
                    dve.wait_ge(mod_ready, 4 * sum(n in MODS for x in parts[:part + 1] for n in x))

                def modulation(n):
                    m = mod_no[n]
                    dve.wait_ge(mod_mm, m + 1)
                    if m:
                        dve.wait_ge(mod_ready, 4 * m)
                    src = bank[2][:] if n == "gb" else mod_bank[m % 4]
                    if n in ("ga", "gb"):
                        tmp(nc.vector.tensor_scalar(mod_a, src, 0.0, 2.0, ALU.is_ge, ALU.mult))
                        tmp(nc.vector.tensor_scalar(mod_a, mod_a, -1.0, None, ALU.add))
                        tmp(nc.vector.tensor_tensor(mod_b, src, mod_a, ALU.mult))
                        tmp(nc.vector.scalar_tensor_tensor(mod_a, mod_b, 0.25, mod_a, ALU.max, ALU.mult))
                        src = mod_a
                    elif n in ("ca", "cb"):
                        tmp(nc.vector.tensor_scalar(mod_a, src, 1.0, None, ALU.add))
                        src = mod_a
                    dst = {"sa": mod["sa"], "ca": mod["ca1"], "ga": mod["ga"], "sb": mod["sb"], "cb": mod["cb1"]}
                    for bb in range(B):
                        for top_half in range(2):
                            rows = slice(64 * top_half, 64 * top_half + 64)
                            target = x2[bb][rows, :] if n == "gb" else dst[n][rows, bb, :]
                            nc.vector.tensor_copy(target, src[64 * bb:64 * bb + 64, :]).then_inc(mod_ready, 1)
                    if n == "ga":
                        dve.wait_ge(mod_ready, copies_before["ga"] + 4)
                        for bb in (1, 0):
                            tmp(nc.vector.tensor_tensor(mod["gabo"][:, bb, :], mod["ga"][:, bb, :],
                                                        mod["gabo"][:, 0, :], ALU.mult))

                def cosine(j, b, n):
                    wait_tile(dve, (q_out if n == "q" else k_out), j, b)
                    nc.vector.tensor_tensor(t1[:, qk[n]].rearrange("p (h e) -> p h e", e=DK),
                                            y[:, qk[n]].rearrange("p (h e) -> p h e", e=DK),
                                            cos_t[:, j, :].unsqueeze(1).broadcast_to((P, H, DK)),
                                            ALU.mult).then_inc(rope_cos[n], 1)

                def rotated(j, b, n):
                    wait_tile(dve, rope_cos[n], j, b)
                    wait_tile(dve, rope_sin[n], j, b)
                    pairs = lambda a: a[:, qk[n]].rearrange("p (i two) -> p i two", two=2)
                    nc.vector.tensor_tensor(pairs(y), pairs(t1), pairs(t2)[:, :, ::-1], ALU.add)\
                        .then_inc(rope_done[n], 1)

                def running_state(j, b, c):
                    jl, bl = lag(j, b, 1)
                    wait_tile(dve, s_mm, j, b, 1, 2, c + 1)
                    wait_tile(dve, state_done, j, b, 1, 2, c)
                    wait_tile(dve, blocks_done, j, b, 3, 2, c + 1)
                    nc.vector.tensor_tensor(state[bl][c][:].rearrange("p (s g) e -> p s (g e)", s=2), psS[:, :, 0:2 * SW],
                                            state[bl][1 - c][:].rearrange("p (s g) e -> p s (g e)", s=2),
                                            ALU.add).then_inc(state_done, 1)

                def features(j, b, n):
                    wait_tile(dve, exp_done[n], j, b)
                    wait_tile(dve, rope_done[n], j, b)
                    if n == "k":
                        wait_tile(dve, s_mm, j, b, 2, 2)
                    else:
                        wait_tile(dve, qT_mm, j, b, 2)
                    nc.vector.scalar_tensor_tensor(feat[b][:, qk[n]], y[:, qk[n]], 1.0, t1[:, qk[n]], ALU.add,
                                                   ALU.max).then_inc(feat_done[n], 1)

                def step(j, b):
                    if real(j, b, 0):
                        wait_tile(dve, k_mm, j, b)
                        wait_tile(dve, feat_done["k"], j, b, 1)
                        nc.vector.tensor_tensor(y[:, D:2 * D], bank[0][:], bias_k[:], ALU.add).then_inc(k_out, 1)
                    if real(j, b, 0):
                        cosine(j, b, "k")
                    if real(j, b, 1):
                        running_state(j, b, 0)
                    if real(j, b, 3):
                        jl, bl = lag(j, b, 3)
                        wait_tile(dve, h2T_hi, j, b, 3)
                        nc.vector.tensor_tensor(h2T[:, 1], bank[2][:].rearrange("p (c t) -> p c t", c=KC),
                                                raw(h2T[:, 0]), ALU.subtract).then_inc(h2T_lo, 1)
                    if real(j, b, 0):
                        rotated(j, b, "k")
                    if real(j, b, 0):
                        features(j, b, "k")
                    if real(j, b, 0):
                        wait_tile(dve, v_mm, j, b)
                        wait_tile(dve, s_mm, j, b, 2, 2)
                        nc.vector.tensor_tensor(v_buf[b][:, :, 0:P], bank[1][:].rearrange("p (g e) -> p g e", g=NG),
                                                bias_v[:].rearrange("p (g e) -> p g e", g=NG), ALU.add)\
                            .then_inc(v_out, 1)
                    if real(j, b, 1):
                        running_state(j, b, 1)
                    if real(j, b, 2):
                        wait_tile(dve, oT_hi, j, b, 2)
                        nc.vector.tensor_tensor(oT[:, 1], bank[3][:].rearrange("p (c t) -> p c t", c=KC),
                                                raw(oT[:, 0]), ALU.subtract).then_inc(oT_lo, 1)
                    if real(j, b, 3):
                        jl, bl = lag(j, b, 3)
                        wait_tile(dve, r_mm, j, b, 3)
                        nc.vector.tensor_copy(logits[:, bl * TPB + jl, :], psN[:, 1, 300:300 + RW]).then_inc(logits_done, 1)
                    if real(j, b, -2):
                        jn, bn = lag(j, b, -2)
                        dve.wait_ge(x_in[bn], 16 * (jn + 1))
                        nc.vector.bn_stats(st1[:], xin[bn]).then_inc(st1_done, 1)
                        wait_tile(dve, st1_done, j, b, -2)
                        dve.sem_inc(waited_dve, 1)
                        nc.vector.bn_aggr(mv1[bn][:], st1[:]).then_inc(mv1_done, 1)
                    if real(j, b, 0):
                        wait_tile(dve, q_mm, j, b)
                        wait_tile(dve, feat_done["q"], j, b, 1)
                        nc.vector.tensor_tensor(y[:, 0:D], bank[0][:], bias_q[:], ALU.add).then_inc(q_out, 1)
                    if real(j, b, 0):
                        cosine(j, b, "q")
                    if real(j, b, -2):
                        jn, bn = lag(j, b, -2)
                        wait_tile(dve, rs1_done, j, b, -2)
                        wait_tile(dve, h_a, j, b, -1)
                        nc.vector.tensor_scalar(xhat[:], xin[bn], mv1[bn][:, 0:1], rs1[bn][:, 1:2],
                                                ALU.subtract, ALU.mult).then_inc(xhat_done, 1)
                    if real(j, b, 0):
                        rotated(j, b, "q")
                    if real(j, b, 2):
                        jl, bl = lag(j, b, 2)
                        wait_tile(dve, o_mm, j, b, 2)
                        wait_tile(dve, h2_a, j, b, 3)
                        nc.vector.tensor_tensor(proj[:], bank[2][:], mod["ga"][:, bl, :], ALU.mult).then_inc(proj_done, 1)
                        wait_tile(dve, proj_done, j, b, 2)
                        wait_tile(dve, xg_done, j, b, 2)
                        if real(j, b, 4):
                            dve.wait_ge(x2_out[bl], 16 * jl)
                        else:
                            dve.wait_ge(gb_out, 32)
                        nc.vector.tensor_tensor(x2[bl][:], proj[:], xres[bl][:], ALU.add).then_inc(x2_done, 1)
                        wait_tile(dve, x2_done, j, b, 2)
                        nc.vector.bn_stats(st2[:], x2[bl][:]).then_inc(st2_done, 1)
                        wait_tile(dve, st2_done, j, b, 2)
                        wait_tile(dve, xhat2_done, j, b, 4)
                        dve.sem_inc(waited_dve, 1)
                        nc.vector.bn_aggr(mv2[bl][:], st2[:]).then_inc(mv2_done, 1)
                    if real(j, b, 0):
                        features(j, b, "q")
                    if real(j, b, -1):
                        jn, bn = lag(j, b, -1)
                        wait_tile(dve, hT_hi, j, b, -1)
                        nc.vector.tensor_tensor(hT[bn][:, 1], bank[0][:].rearrange("p (c t) -> p c t", c=KC),
                                                raw(hT[bn][:, 0]), ALU.subtract).then_inc(hT_lo, 1)
                    if real(j, b, 2):
                        jl, bl = lag(j, b, 2)
                        wait_tile(dve, rs2_done, j, b, 2)
                        nc.vector.tensor_scalar(xhat2[:], x2[bl][:], mv2[bl][:, 0:1], rs2[bl][:, 1:2],
                                                ALU.subtract, ALU.mult).then_inc(xhat2_done, 1)
                    if real(j, b, 0):
                        wait_tile(dve, g_mm, j, b)
                        nc.vector.tensor_tensor(th[b][:], bank[1][:], bias_g[:], ALU.add).then_inc(g_out, 1)
                    if real(j, b, 1):
                        jl, bl = lag(j, b, 1)
                        wait_tile(dve, n_mm, j, b, 1)
                        wait_tile(dve, o_done, j, b, 2)
                        num = psN[:, :, 0:2 * SW].rearrange("p s (g e) -> p s g e", e=SW)
                        nc.vector.tensor_scalar(rden[:].rearrange("p (s g h) -> p s g h", s=2, g=2), num[:, :, :, P:SW],
                                                2.0, 2 * DEN_EPS, ALU.mult, ALU.add).then_inc(den_a, 1)
                        wait_tile(dve, den_a, j, b, 1)
                        nc.vector.reciprocal(rden2[:], rden[:]).then_inc(den_done, 1)
                        wait_tile(dve, tanh_done, j, b, 1)
                        for s in range(2):
                            nc.vector.scalar_tensor_tensor(
                                o1_buf[:, s * 256:(s + 1) * 256].rearrange("p (g e) -> p g e", g=2),
                                th[bl][:, s * 256:(s + 1) * 256].rearrange("p (g e) -> p g e", g=2), 1.0,
                                num[:, s, :, 0:P], ALU.add, ALU.mult).then_inc(o_half, 1)
                        wait_tile(dve, o_half, j, b, 1, 2)
                        wait_tile(dve, den_done, j, b, 1)
                        wait_tile(dve, oT_mm, j, b, 2)
                        nc.vector.tensor_tensor(o_buf.rearrange("p (h e) -> p h e", e=DK),
                                                o1_buf.rearrange("p (h e) -> p h e", e=DK),
                                                rden2[:].unsqueeze(2).broadcast_to((P, H, DK)), ALU.mult)\
                            .then_inc(o_done, 1)

                def begin_ffn(part):
                    if part < 2:
                        shared.gu_low(dve, part, part)
                    else:
                        shared.down_low(dve, 0, 0)

                run_steps(dve, step, prepare, begin_ffn)

            @block.tensor
            def _(pe):
                def transpose_tile(out, src):
                    v = src.rearrange("t (q c) -> t c q", c=KC)
                    for c in range(KC):
                        last = nc.tensor.transpose(out[:, c * P:(c + 1) * P], v[:, c, :], ident[:])
                    return last

                def prepare(part):
                    if part == 0:
                        pe.wait_ge(csilu_ready, 1)
                    for n in [jobs[:7], jobs[7:-1], jobs[-1:], []][part]:
                        if n in MODS:
                            m = mod_no[n]
                            slot_in(pe, n)
                            if m == 4:
                                pe.wait_ge(mod_ready, 4)
                            for c in range(KC):
                                last = nc.tensor.matmul(bank[2][:] if n == "gb" else mod_bank[m % 4],
                                                        c_silu[:, c].rearrange("p b m -> p (b m)"),
                                                        stage[slot[n]][:, c * D:(c + 1) * D],
                                                        start=c == 0, stop=c == KC - 1)
                            last.then_inc(mod_mm, 1)
                    if part == 0:
                        pe.wait_ge(const_ready, 7)
                        pe.wait_ge(lo_done, 4)
                    elif part == 1:
                        pe.wait_ge(lo_done, 5)

                def project(n, out, hb):
                    return product(nc, out, [((hb[:, 0, c], hb[:, 1, c]), (w_hi[n][:, c], w_lo[n][:, c]))
                                         for c in range(KC)])

                def chunk_state(j, b, c):
                    jl, bl = lag(j, b, 1)
                    wait_tile(pe, feat_done["k"], j, b, 1)
                    wait_tile(pe, v_out, j, b, 1)
                    if not real(j, b, 2):
                        pe.wait_ge(mod_ready, copies_before["gb"])
                    wait_tile(pe, state_done, j, b, 1, 2, c)
                    rows = slice(c * CS, (c + 1) * CS)
                    for g in range(NG):
                        last = nc.tensor.matmul(psS[:, g // 2, (g % 2) * SW:(g % 2 + 1) * SW],
                                                feat[bl][rows, D + g * P:D + (g + 1) * P],
                                                v_buf[bl][rows, g, :], start=True, stop=True)
                    last.then_inc(s_mm, 1)

                def step(j, b):
                    if real(j, b, 0):
                        wait_tile(pe, hT_lo, j, b)
                        project("k", bank[0][:], hT[b]).then_inc(k_mm, 1)
                    if real(j, b, 1):
                        chunk_state(j, b, 0)
                    if real(j, b, 3):
                        jl, bl = lag(j, b, 3)
                        wait_tile(pe, h2_done, j, b, 3)
                        wait_tile(pe, proj_done, j, b, 3)
                        transpose_tile(bank[2][:], h2[bl]).then_inc(h2T_mm, 1)
                    if real(j, b, 0):
                        wait_tile(pe, g_out, j, b, 1)
                        project("v", bank[1][:], hT[b]).then_inc(v_mm, 1)
                    if real(j, b, 1):
                        chunk_state(j, b, 1)
                    if real(j, b, 2):
                        wait_tile(pe, o_done, j, b, 2)
                        wait_tile(pe, qT_done, j, b, 2)
                        transpose_tile(bank[3][:], o_buf).then_inc(oT_mm, 1)
                    if real(j, b, 3):
                        wait_tile(pe, h2T_lo, j, b, 3)
                        wait_tile(pe, logits_done, j, b, 4)
                        wait_tile(pe, o_done, j, b, 2)
                        product(nc, psN[:, 1, 300:300 + RW],
                                [((h2T[:, 0, c], h2T[:, 1, c]), (wr_hi[:, c], wr_lo[:, c])) for c in range(KC)])\
                            .then_inc(r_mm, 1)
                    if real(j, b, 0):
                        wait_tile(pe, k_out, j, b)
                        project("q", bank[0][:], hT[b]).then_inc(q_mm, 1)
                    if real(j, b, 1):
                        jl, bl = lag(j, b, 1)
                        wait_tile(pe, feat_done["q"], j, b, 1)
                        wait_tile(pe, oT_lo, j, b, 2)
                        for g in range(NG):
                            last = nc.tensor.transpose(bank[3][:, g * P:(g + 1) * P], feat[bl][:, g * P:(g + 1) * P],
                                                       ident[:])
                        last.then_inc(qT_mm, 1)
                    if real(j, b, 2):
                        wait_tile(pe, oT_lo, j, b, 2)
                        wait_tile(pe, h2T_lo, j, b, 3)
                        if not real(j, b, 3):
                            pe.wait_ge(mod_ready, copies_before["gb"] + 4)
                        project("o", bank[2][:], oT).then_inc(o_mm, 1)
                    if real(j, b, -1):
                        jn, bn = lag(j, b, -1)
                        wait_tile(pe, h_done, j, b, -1)
                        wait_tile(pe, q_out, j, b)
                        transpose_tile(bank[0][:], h_buf[bn]).then_inc(hT_mm, 1)
                    if real(j, b, 0):
                        wait_tile(pe, v_out, j, b)
                        project("g", bank[1][:], hT[b]).then_inc(g_mm, 1)
                    if real(j, b, 1):
                        jl, bl = lag(j, b, 1)
                        wait_tile(pe, qT_done, j, b, 1)
                        wait_tile(pe, o_done, j, b, 2)
                        wait_tile(pe, logits_done, j, b, 3)
                        for c in range(2):
                            wait_tile(pe, blocks_done, j, b, 1, 2, c + 1)
                            for g in range(NG):
                                last = nc.tensor.matmul(psN[c * CS:(c + 1) * CS, g // 2, (g % 2) * SW:(g % 2 + 1) * SW],
                                                        qT[:, g, c * CS:(c + 1) * CS], blocks[c][:, g, :],
                                                        start=True, stop=True)
                        last.then_inc(n_mm, 1)

                def begin_ffn(part):
                    if part == 1:
                        pe.wait_ge(shared.wgu_lo, 1)
                        pe.wait_ge(shared.hT_in, 16)
                        pe.wait_ge(q_out, NT)
                        shared.multiply(0, 0)
                        pe.wait_ge(g_out, NT)
                        shared.multiply(1, 0)

                run_steps(pe, step, prepare, begin_ffn)


FCH = FS // P
GROUP = 3
NGROUPS = -(-FCH // GROUP)
SUB = 4
UNITS = NT // SUB
XPU = 4
FIRST_X = 2
LAST_X = FIRST_X + E // XPU
TABLE_COLS = 8 + E + 2 * NT + P
FX = -(-F // P)
RAW_SLOTS = 4
S1 = CAP // 8


def chunks_of(g):
    return GROUP if g < NGROUPS - 1 else FCH - GROUP * (NGROUPS - 1)


def chunk_no(u, c, last):
    if last:
        return GROUP * UNITS * (NGROUPS - 1) + chunks_of(NGROUPS - 1) * (u - UNITS * (NGROUPS - 1)) + c
    return GROUP * u + c


ROUTING0 = {
    "pe": [("gate", 1), ("up", 1), ("gate", 2), ("up", 2), ("down", 0),
           ("route", "positions"), ("down", 1), ("down", 2), ("down", 3)],
    "act": [("gate", 0), ("up", 0), ("first_gu", 2), ("route", "exp"), ("first_down", 1), ("gate", 1), ("up", 1),
            ("first_down", 2), ("gate", 2), ("up", 2)],
    "dve": [("mult", 0), ("gu_lo", 0), ("first_gu", 2), ("route", "softmax"), ("first_down", 1), ("mult", 1),
            ("gu_lo", 1), ("first_down", 2), ("mult", 2), ("gu_lo", 2), ("route", "one_hot"), ("route", "picks"),
            ("down", 0), ("down", 1), ("down", 2), ("down", 3), ("route", "digits")],
    "pool": [],
    "sp": [("hT", 0)],
}
ROUTING1 = {
    "pe": [("gate", 0), ("up", 0), ("gate", 1), ("up", 1), ("route", "tokens"), ("gate", 2), ("up", 2), ("down", 0),
           ("down", 1), ("down", 2), ("down", 3)],
    "act": [("gate", 0), ("up", 0), ("gate", 1), ("up", 1), ("gate", 2), ("up", 2),
            ("split_g", 4), ("split_u", 4)],
    "dve": [("route", "high"), ("mult", 0), ("gu_lo", 0), ("route", "low"), ("mult", 1), ("gu_lo", 1), ("route", "slots"),
            ("mult", 2), ("gu_lo", 2), ("down", 0), ("down", 1), ("down", 2), ("down", 3), ("split_g", 4),
            ("split_u", 4)],
    "pool": [("gather", 0), ("gather", 1)],
    "sp": [("route", "out"), ("first_x", 0), ("route", "columns"), ("first_x", 1), ("first_x", 2), ("hT", 0)],
}
WITH_X = {
    "pe": [("rows", 0), ("gate", 0), ("gu", 0), ("up", 0), ("mid", 0), ("gate", 1), ("exp_down", 0), ("gu", 1),
           ("up", 1), ("mid", 1), ("gate", 2), ("rows", 1), ("exp_down", 1), ("gu", 2), ("up", 2), ("mid", 2),
           ("exp_down", 2), ("down", 0), ("gu", 3), ("down", 1), ("down", 2), ("mid", 3), ("down", 3), ("exp_down", 3)],
    "act": [("rows", 0), ("split_d", 0), ("gate", 0), ("low", 0), ("silu", 0), ("split_g", 1), ("split_u", 1), ("up", 0), ("mid", 0),
            ("gate", 1), ("exp_down", 0), ("split_d", 1), ("low", 1), ("silu", 1), ("split_g", 2), ("split_u", 2),
            ("up", 1), ("mid", 1), ("gate", 2), ("rows", 1), ("exp_down", 1), ("split_d", 2), ("low", 2),
            ("silu", 2), ("split_g", 3), ("mid", 2), ("up", 2), ("split_u", 3), ("exp_down", 2), ("split_d", 3),
            ("low", 3), ("silu", 3), ("split_g", 4), ("split_u", 4), ("mid", 3), ("exp_down", 3)],
    "dve": [("rows", 0), ("split_d", 0), ("sum", 0), ("xmul", 0), ("mult", 0), ("split_g", 1), ("mid", 0), ("split_u", 1), ("gu_lo", 0),
            ("exp_down", 0), ("split_d", 1), ("sum", 1), ("xmul", 1), ("mult", 1), ("split_g", 2), ("mid", 1),
            ("split_u", 2), ("gu_lo", 1), ("rows", 1), ("exp_down", 1), ("split_d", 2), ("sum", 2), ("xmul", 2),
            ("mult", 2), ("mid", 2), ("gu_lo", 2), ("split_g", 3), ("split_u", 3), ("exp_down", 2), ("down", 0),
            ("split_d", 3), ("sum", 3), ("xmul", 3), ("down", 1), ("split_g", 4), ("down", 2), ("mid", 3),
            ("split_u", 4), ("down", 3), ("exp_down", 3)],
    "pool": [("ye_out", 0), ("ye_out", 1), ("gather", 0), ("gather", 1), ("ye_out", 2), ("ye_out", 3)],
    "sp": [("weights", 1), ("weights", 2), ("weights", 3), ("hT", 0), ("weights", 4)],
}
COMBINE4 = {
    "pe": [("gate", 0), ("up", 0), ("gate", 1), ("up", 1), ("gate", 2), ("up", 2), ("down", 0), ("down", 1),
           ("down", 2), ("down", 3)],
    "act": [("gate", 0), ("up", 0), ("gate", 1), ("up", 1), ("gate", 2), ("up", 2)],
    "dve": [("mult", 0), ("gu_lo", 0), ("combine", 0), ("mult", 1), ("gu_lo", 1), ("combine", 1), ("mult", 2),
            ("gu_lo", 2), ("combine", 2), ("down", 0), ("down", 1), ("down", 2), ("down", 3), ("combine", 3)],
    "pool": [("fetch", 2), ("fetch", 3), ("fetch", 4), ("fetch", 5)],
    "sp": [("hT", 0)],
}
COMBINE2 = {
    "pe": [("gate", 0), ("up", 0), ("gate", 1), ("up", 1), ("down", 0), ("down", 1), ("down", 2), ("down", 3)],
    "act": [("gate", 0), ("up", 0), ("gate", 1), ("up", 1)],
    "dve": [("mult", 0), ("gu_lo", 0), ("combine", 0), ("mult", 1), ("gu_lo", 1), ("combine", 1), ("down", 0),
            ("down", 1), ("down", 2), ("down", 3), ("times_gb", 0), ("times_gb", 1), ("times_gb", 2), ("times_gb", 3)],
    "pool": [("fetch", 2), ("fetch", 3), ("add_x2", 0), ("add_x2", 1), ("add_x2", 2), ("add_x2", 3)],
    "sp": [("x2", 0), ("hT", 0)],
}
LAST = {
    **COMBINE2,
    "dve": COMBINE2["dve"][:6] + [(what, r) for r in range(SUB) for what in ("down", "times_gb", "add_x2")],
    "pool": [],
    "sp": [("store", 1), ("x2", 0), ("last", 0), ("last", 1), ("last", 2), ("last", 3)],
}


def last_experts(order):
    return {e: [x for x in items if x[0] != "gather" and x[1] != 4] for e, items in order.items()}


def insert(items, at, after):
    out = []
    for x in items:
        new = at.get(x, [])
        out += [x] + new if after else new + [x]
    return out


def free_time(act):
    return "mid" if ("mid", 0) in act else "up"


def with_next_group(order, chunks):
    gu = [("new_gu", c) for c in range(chunks)]
    sp = order["sp"]
    if ("weights", 1) in sp:
        sp = insert(sp, {("weights", c + 1): [gu[c]] for c in range(chunks)}, False)
    else:
        sp = gu + sp
    return {**order, "act": insert(order["act"], {(free_time(order["act"]), c): [gu[c]] for c in range(chunks)}, True),
            "dve": insert(order["dve"], {("gu_lo", c): [gu[c]] for c in range(chunks)}, True),
            "sp": insert(sp, {("hT", 0): [("next_down", 0)]}, True)}


def with_new_down(order, chunks):
    new = [("new_down", c) for c in range(chunks)]
    later = lambda name: {(name, c - 1): [new[c]] for c in range(1, chunks)}
    sp = order["sp"]
    sp = insert(sp, {("weights", c): [new[c]] for c in range(1, chunks)}, True) \
        if ("weights", 1) in sp else new[1:] + sp
    return {**order, "act": insert(insert(order["act"], {("up", 0): [new[0]]}, False), later(free_time(order["act"])), True),
            "dve": insert(insert(order["dve"], {("mult", 0): [new[0]]}, False), later("gu_lo"), True), "sp": sp}


def run_units(eng, name, unit):
    def run(g, s, kind, order):
        unit(g, s, kind, order[name])

    run(0, 0, "routing0", ROUTING0)
    run(0, 1, "routing1", ROUTING1)
    run(0, 2, "experts", WITH_X)
    run(0, 3, "experts", with_next_group(WITH_X, chunks_of(1)))
    run(1, 0, "experts", with_new_down(WITH_X, chunks_of(1)))
    with eng.Fori(1, 3) as s:
        run(1, s, "experts", WITH_X)
    run(1, 3, "experts", with_next_group(WITH_X, chunks_of(2)))
    run(2, 0, "experts", with_new_down(WITH_X, chunks_of(2)))
    run(2, 1, "experts", last_experts(WITH_X))
    run(2, 2, "combine4", {**COMBINE4, "pool": [("fetch", 0), ("fetch", 1)] + COMBINE4["pool"]})
    run(2, 3, "combine4", with_next_group(COMBINE4, chunks_of(3)))
    run(3, 0, "combine2", with_new_down(COMBINE2, chunks_of(3)))
    with eng.Fori(1, 3) as s:
        run(3, s, "combine2", {**COMBINE2, "sp": [("store", 1)] + COMBINE2["sp"]})
    run(3, 3, "combine2", LAST)


def ffn(nc, io, scr, out):
    with ExitStack() as ctx:
        def sb(name, shape, dt=F32):
            return ctx.enter_context(nc.sbuf_tensor(name, shape, dt))

        def sem(name):
            return ctx.enter_context(nc.semaphore(name))

        logits, ident = io["logits"], io["ident"]
        acc = sb("acc", [P, NT, D])
        gb = sb("gb", [P, B, D])
        shared, psum = io["shared"], io["psum"]
        ws, pair, down_w = shared.ws, shared.pair, shared.down_w
        hT_in, gate_mm, up_mm, wgu_lo, wdn_lo = shared.hT_in, shared.gate_mm, shared.up_mm, shared.wgu_lo, shared.wdn_lo
        sil = sb("sil", [P, SUB * P])
        gu, guT = shared.gu, shared.guT
        sig4 = sb("sig4", [P, SUB])
        wx_raw = sb("wx_raw", [P, RAW_SLOTS, FX * D])
        wx = [sb(f"wx_{n}", [P, 2, FX * D], F32R) for n in ("gate", "up", "down")]
        rows = [sb(f"token_rows{i}", [P, D]) for i in range(2)]
        xs = [sb(f"xs{i}", [P, 2, KC, P], F32R) for i in range(2)]
        low_g, low_u = sb("low_g", [CAP, F]), sb("low_u", [CAP, F])
        xg, xu = sb("xg", [CAP, F]), sb("xu", [CAP, F])
        xgu = sb("xgu", [CAP, FX * P])
        xguT = sb("xguT", [P, FX, P], F32R)
        low_y = sb("low_y", [CAP, D])
        ye = sb("ye", [CAP, D])
        sig = sb("sig", [P, NT])
        w_top = sb("w_top", [P, NT, TOPK])
        slot_top = sb("slot_top", [P, NT, TOPK], I32)
        w_now = sb("w_now", [P, TOPK])
        slot_now = [sb(f"slot_now{i}", [P, TOPK], I32) for i in range(2)]
        tok_of_slot = sb("tok_of_slot", [P, E // 2], I32)
        tok_now = sb("tok_now", [P, 2], I32)
        free = wx_raw[:].rearrange("p s n -> p (s n)")
        used = [0]

        def take(n):
            used[0] += n
            return free[:, used[0] - n:used[0]]

        def by_tile(ap, n=E):
            return ap.rearrange("p (t e) -> p t e", e=n)

        PE_ = NT * E
        prob = by_tile(take(PE_))
        one_hot_flat, picked_flat = take(TOPK * PE_), take(TOPK * PE_)
        one_hot = one_hot_flat.rearrange("p (t k e) -> p t k e", k=TOPK, e=E)
        picked = picked_flat.rearrange("p (t k e) -> p t k e", k=TOPK, e=E)
        digit1 = one_hot_flat.bitcast(F16).rearrange("p (t n) -> p t n", t=NT)
        digit0 = picked_flat.bitcast(F16).rearrange("p (t n) -> p t n", t=NT)
        posm = by_tile(take(PE_))
        mask = take(PE_ // 2).bitcast(BF16)
        before = take(P // 2).bitcast(BF16)
        ones = take(P // 2).bitcast(BF16)
        top = take(NT * 8).rearrange("p (t k) -> p t k", k=8)
        c1 = prob
        pos_i, c0 = by_tile(rows[0][:].bitcast(I32)), by_tile(rows[1][:])
        top_i = sb("top_i", [P, NT, 8], U32)
        idx_f = sb("idx_f", [P, NT, TOPK])
        small = sb("small", [P, 4, NT])
        tables = sb("tables", [P, TABLE_COLS])
        iota8, iota_e = tables[:, 0:8], tables[:, 8:8 + E]
        token_id = tables[:, 8 + E:8 + E + NT]
        own_half = tables[:, 8 + E + NT:8 + E + 2 * NT]
        pos_k = sb("pos_k", [P, NT, TOPK])
        valid = sb("valid", [P, NT, TOPK])
        inv = sb("inv", [P, 2, 8, NT])
        inv_f = sb("inv_f", [P, 2, 8])
        inv_i = sb("inv_i", [P, 2, 8], I32)

        bankA, bankB = shared.bankA, shared.bankB
        psXG, psXU, psT, psY = (psum[:, i] for i in (2, 3, 6, 7))
        down_bank = [bankB[0], bankB[1], bankA[0], bankA[1]]

        x2u_in, gb_in, table_in = sem("x2u_in"), sem("gb_in"), sem("table_in")
        sil_done, gu_done = sem("sil_done"), sem("gu_done")
        gu_hi, gu_lo = sem("gu_hi"), sem("gu_lo")
        dn_mm, dn_evac, sig4_done = sem("dn_mm"), sem("dn_evac"), sem("sig4_done")
        wx_in = [sem(f"wx_in{i}") for i in range(RAW_SLOTS)]
        wxg_hi, wxd_hi = sem("wxg_hi"), sem("wxd_hi")
        wxg_lo, wxd_lo = sem("wxg_lo"), sem("wxd_lo")
        tok_copied, rows_in = sem("tok_copied"), [sem(f"rows_in{i}") for i in range(2)]
        rows_mm, rows_hi, rows_lo = sem("rows_mm"), sem("rows_hi"), sem("rows_lo")
        xgu_mm, xlow, xsum, xadd = sem("xgu_mm"), sem("xlow"), sem("xsum"), sem("xadd")
        xsil, xgu_done = sem("xsil"), sem("xgu_done")
        mid_mm, mid_hi, mid_lo = sem("mid_mm"), sem("mid_hi"), sem("mid_lo")
        xd_mm, y_low, ye_add, ye_out = sem("xd_mm"), sem("y_low"), sem("ye_add"), sem("ye_out")
        slot_copied, w_copied = sem("slot_copied"), sem("w_copied")
        y_in = [[sem(f"y_in{i}{k}") for k in range(TOPK)] for i in range(2)]
        cm_step, gb_mul, x2_add, last_add = sem("cm_step"), sem("gb_mul"), sem("x2_add"), sem("last_add")
        r_chain, r_exp, r_pe, r_consts = sem("r_chain"), sem("r_exp"), sem("r_pe"), sem("r_consts")
        r_dve, tok_moved, out_done = sem("r_dve"), sem("tok_moved"), sem("out_done")

        waited_pool, waited_pe = io["waited_pool"], io["waited_pe"]

        ye_rows = scr["ye"].rearrange("e c d -> (e c) d")
        h2_rows = scr["h2"].rearrange("b j p d -> (b j p) d")
        x2_tiles = scr["x2"].rearrange("b j p d -> p (b j) d")
        out_tiles = out.rearrange("b (j p) d -> p (b j) d", p=P)
        y_buf = [[free[:, (4 * i + k) * D:(4 * i + k + 1) * D] for k in range(TOPK)] for i in range(2)]
        x2u = free[:, 8 * D:12 * D].rearrange("p (i d) -> p i d", d=D)

        def raw_value(m, x):
            per_unit = 64
            return per_unit * x + sum(32 if k % 3 == 2 else 16 for k in range(m % RAW_SLOTS, m + 1, RAW_SLOTS))

        def tile_no(kind, s, r):
            return 4 * (s - 2) + r if kind == "combine4" else 2 * UNITS + 2 * s + r

        def tile_uses(kind, s, r):
            return 2 * (s - 2) + r // 2 + 1 if kind == "combine4" else UNITS + s + r // 2 + 1

        with nc.Block() as block:
            @block.sync
            def _(sp):
                sp.dma_start(tables[:], io["tables"]).then_inc(table_in, 16)

                shared.load_down(sp, 2)
                sp.dma_start(gb[:], scr["gb"]).then_inc(gb_in, 16)

                def load_matrix(x, m):
                    e, slot = x * XPU + m // 3, m % RAW_SLOTS
                    old_e, old = x * XPU + (m - RAW_SLOTS) // 3, (m - RAW_SLOTS) % 3
                    if not (isinstance(old_e, int) and old_e < 0):
                        if old == 2:
                            sp.wait_ge(wxd_lo, 2 + old_e + 1)
                        else:
                            sp.wait_ge(wxg_lo, 2 + 2 * old_e + old + 1)
                    if m % 3 < 2:
                        w = io["wg_x"] if m % 3 == 0 else io["wu_x"]
                        sp.dma_start(wx_raw[:, slot, 0:KC * F], w[e].rearrange("(p c) f -> p (c f)", c=KC))\
                          .then_inc(wx_in[slot], 16)
                    else:
                        w, full = io["wd_x"][e], F // P
                        sp.dma_start(wx_raw[:, slot, 0:full * D].rearrange("p (c n) -> p c n", n=D),
                                     w[0:full * P].rearrange("(c p) n -> p c n", p=P)).then_inc(wx_in[slot], 16)
                        sp.dma_start(wx_raw[0:F - full * P, slot, full * D:FX * D], w[full * P:F])\
                          .then_inc(wx_in[slot], 16)

                def unit(g, s, kind, order):
                    u = UNITS * g + s
                    x = u - FIRST_X
                    for what, r in order:
                        if (what, r) == ("route", "out"):
                            sp.wait_ge(r_dve, 5)
                            sp.dma_start(scr["slots"].rearrange("(h p c) -> p h c", h=2, p=P), inv_i[:])\
                              .then_inc(tok_moved, 16)
                        elif what == "route":
                            sp.wait_ge(tok_moved, 16)
                            with nc.allow_non_contiguous_dma("2048 slot numbers, once"):
                                sp.dma_start(tok_of_slot[:], scr["slots"].rearrange("(n p) -> p n", p=P))\
                                  .then_inc(tok_moved, 16)
                        elif what == "first_x":
                            sp.wait_ge(r_pe, 2)
                            load_matrix(x, 3 * XPU + r)
                        elif what == "weights":
                            for m in range(3 * r, 3 * r + 3):
                                load_matrix(x, m)
                        elif what == "hT":
                            sp.wait_ge(up_mm, chunk_no(u, chunks_of(g), g == NGROUPS - 1))
                            nxt = (s + 1) % UNITS if isinstance(s, int) else s + 1
                            shared.load_tokens(sp, nxt)
                        elif what == "new_gu":
                            shared.load_gu(sp, GROUP * (g + 1) + r)
                        elif what == "next_down":
                            shared.load_down(sp, GROUP * (g + 1))
                        elif what == "new_down":
                            shared.load_down(sp, GROUP * g + r)
                        elif what == "x2":
                            if not (isinstance(s, int) and s == 0):
                                sp.wait_ge(x2_add, SUB * s)
                            else:
                                sp.wait_ge(wxg_lo, 2 + 2 * E)
                                sp.wait_ge(wxd_lo, 2 + E)
                            sp.dma_start(x2u, x2_tiles[:, bass.ds(s * SUB, SUB), :]).then_inc(x2u_in, 16)
                        elif what == "store":
                            sp.wait_ge(x2_add, SUB * s)
                            sp.dma_start(out_tiles[:, bass.ds((s - r) * SUB, SUB), :],
                                         acc[:, bass.ds((s - r) * SUB, SUB), :]).then_inc(out_done, 16)
                        elif what == "last":
                            i = s * SUB + r
                            sp.wait_ge(last_add, r + 1)
                            sp.dma_start(out_tiles[:, i:i + 1, :], acc[:, i:i + 1, :]).then_inc(out_done, 16)

                run_units(sp, "sp", unit)
                sp.wait_ge(out_done, 16 * (UNITS - 1 + SUB))

            @block.gpsimd
            def _(pool):
                pool.memset(xgu[:, F:FX * P], 0.0).then_inc(r_consts, 1)
                pool.memset(ones, 1.0).then_inc(r_consts, 1)

                def unit(g, s, kind, order):
                    u = UNITS * g + s
                    for what, r in order:
                        if what == "gather":
                            x = u - FIRST_X + 1
                            if r == 0:
                                pool.wait_ge(rows_mm, 1 + 2 * x)
                                pool.wait_ge(tok_moved, 32)
                                pool.tensor_copy(tok_now[:], tok_of_slot[:, bass.ds(x * 2, 2)]).then_inc(tok_copied, 1)
                                pool.wait_ge(tok_copied, x + 1)
                                pool.sem_inc(waited_pool, 1)
                            pool.indirect_dma_start(rows[r][:], None, h2_rows,
                                                    bass.IndirectOffsetOnAxis(tok_now[:, r:r + 1], 0))\
                                .then_inc(rows_in[r], 16)
                        elif what == "ye_out":
                            e = (u - FIRST_X) * XPU + r
                            pool.wait_ge(ye_add, 1 + e + 1)
                            pool.sem_inc(waited_pool, 1)
                            pool.dma_start(scr["ye"][e], ye[:]).then_inc(ye_out, 16)
                        elif what == "add_x2":
                            i = s * SUB + r
                            pool.wait_ge(x2u_in, 16 * (s + 1))
                            pool.wait_ge(gb_mul, i + 1)
                            pool.tensor_tensor(acc[:, i], acc[:, i], x2u[:, r], ALU.add).then_inc(x2_add, 1)
                        elif what == "fetch":
                            i = tile_no(kind, s, r)
                            if r == 0:
                                pool.wait_ge(wxg_lo, 2 + 2 * E)
                                pool.wait_ge(wxd_lo, 2 + E)
                            if not (isinstance(i, int) and i < 2):
                                pool.wait_ge(cm_step, TOPK * (i - 1))
                            pool.tensor_copy(slot_now[r % 2][:], slot_top[:, i, :]).then_inc(slot_copied, 1)
                            pool.wait_ge(ye_out, 16 * E)
                            pool.wait_ge(slot_copied, i + 1)
                            pool.sem_inc(waited_pool, 1)
                            for k in range(TOPK):
                                pool.indirect_dma_start(y_buf[r % 2][k], None, ye_rows,
                                                        bass.IndirectOffsetOnAxis(slot_now[r % 2][:, k:k + 1], 0))\
                                    .then_inc(y_in[r % 2][k], 16)

                run_units(pool, "pool", unit)

            @block.scalar
            def _(act):
                def unit(g, s, kind, order):
                    u, x = UNITS * g + s, UNITS * g + s - FIRST_X
                    e0 = x * XPU
                    for what, r in order:
                        if isinstance(r, int):
                            q, e = chunk_no(u, r, g == NGROUPS - 1), e0 + r
                        if what == "gate":
                            act.wait_ge(gate_mm, q + 1)
                            if not (isinstance(q, int) and q == 0):
                                act.wait_ge(gu_done, q)
                            nc.scalar.activation(sil[:], pair[r][0][:], ACT.Silu).then_inc(sil_done, 1)
                        elif what == "up":
                            act.wait_ge(gu_done, q + 1)
                            if not (isinstance(u, int) and u == 0):
                                act.wait_ge(dn_mm, SUB * u)
                            nc.scalar.copy(guT[r][:, 0], gu).then_inc(gu_hi, 1)
                        elif what == "first_gu":
                            shared.gu_high(act, r, r)
                        elif what == "first_down":
                            shared.down_high(act, r, r)
                        elif what == "new_gu":
                            act.wait_ge(up_mm, q + 1)
                            shared.gu_high(act, GROUP * (g + 1) + r, r)
                        elif what == "new_down":
                            act.wait_ge(dn_mm, SUB * u)
                            shared.down_high(act, GROUP * g + r, r)
                        elif what == "route" and r == "exp":
                            act.wait_ge(r_dve, 1)
                            nc.scalar.activation(prob, prob, ACT.Exp).then_inc(r_exp, 1)
                            nc.scalar.activation(sig[:], logits[:, :, E], ACT.Sigmoid).then_inc(r_exp, 1)
                        elif what in ("split_g", "split_u"):
                            i = 0 if what == "split_g" else 1
                            slot = (3 * r + i) % RAW_SLOTS
                            act.wait_ge(xgu_mm, 1 + e)
                            act.wait_ge(wx_in[slot], raw_value(3 * r + i, x))
                            nc.scalar.copy(wx[i][:, 0, 0:KC * F], wx_raw[:, slot, 0:KC * F]).then_inc(wxg_hi, 1)
                        elif what == "split_d":
                            act.wait_ge(xd_mm, 1 + e)
                            slot = (3 * r + 2) % RAW_SLOTS
                            act.wait_ge(wx_in[slot], raw_value(3 * r + 2, x))
                            nc.scalar.copy(wx[2][:, 0], wx_raw[:, slot]).then_inc(wxd_hi, 1)
                        elif what == "rows":
                            act.wait_ge(rows_mm, 1 + 2 * x + r + 1)
                            act.wait_ge(xgu_mm, 1 + e0)
                            nc.scalar.copy(xs[r][:].rearrange("p h c m -> p c h m")[:, :, :, 0:CAP],
                                           psT[:].rearrange("p (c h m) -> p c h m", c=KC, h=2)).then_inc(rows_hi, 1)
                        elif what == "low":
                            act.wait_ge(xgu_mm, 1 + e + 1)
                            act.wait_ge(xadd, 1 + e)
                            nc.scalar.copy(low_g[:], psXG[CAP:P, 0:F]).then_inc(xlow, 1)
                            nc.scalar.copy(low_u[:], psXU[CAP:P, 0:F]).then_inc(xlow, 1)
                        elif what == "silu":
                            act.wait_ge(xsum, e + 1)
                            nc.scalar.activation(xg[:], xg[:], ACT.Silu).then_inc(xsil, 1)
                        elif what == "mid":
                            act.wait_ge(mid_mm, 1 + e + 1)
                            act.wait_ge(xd_mm, 1 + e)
                            nc.scalar.copy(xguT[:, :, 0:CAP], psT[:, 0:FX * CAP].rearrange("p (c m) -> p c m", c=FX))\
                                .then_inc(mid_hi, 1)
                        elif what == "exp_down":
                            act.wait_ge(xd_mm, 1 + e + 1)
                            act.wait_ge(ye_add, 1 + e)
                            nc.scalar.copy(low_y[:], psY[CAP:P, :]).then_inc(y_low, 1)

                run_units(act, "act", unit)

            @block.vector
            def _(dve):
                for s_, v_ in ((wxg_lo, 2), (wxd_lo, 2), (rows_lo, 1), (xadd, 1), (xgu_done, 1), (mid_lo, 1), (ye_add, 1)):
                    dve.sem_inc(s_, v_)
                links = [0]

                def link(ins):
                    links[0] += 1
                    ins.then_inc(r_chain, 1)
                    dve.wait_ge(r_chain, links[0])

                def route(r):
                    v = nc.vector
                    if r == "softmax":
                        dve.wait_ge(table_in, 16)
                        link(v.memset(free[:, used[0]:RAW_SLOTS * FX * D], 0.0))
                        link(v.reduce_max(small[:, 0], logits[:, :, 0:E], mybir.AxisListType.X))
                        v.tensor_tensor(prob, logits[:, :, 0:E], small[:, 0].unsqueeze(2).broadcast_to((P, NT, E)),
                                        ALU.subtract).then_inc(r_dve, 1)
                        dve.wait_ge(r_exp, 1)
                        link(v.reduce_sum(small[:, 1], prob, mybir.AxisListType.X))
                        link(v.reciprocal(small[:, 2], small[:, 1]))
                        link(v.tensor_tensor(prob, prob, small[:, 2].unsqueeze(2).broadcast_to((P, NT, E)), ALU.mult))
                        for t in range(NT):
                            last = v.max(top[:, t], prob[:, t])
                        link(last)
                        for t in range(NT):
                            last = v.max_index(top_i[:, t], top[:, t], prob[:, t])
                        link(last)
                    elif r == "one_hot":
                        link(v.tensor_copy(idx_f[:], top_i[:, :, 0:TOPK]))
                        link(v.tensor_tensor(one_hot, idx_f[:].unsqueeze(3).broadcast_to((P, NT, TOPK, E)),
                                             iota_e.unsqueeze(1).unsqueeze(1).broadcast_to((P, NT, TOPK, E)), ALU.is_equal))
                        link(v.tensor_copy(before, tables[:, TABLE_COLS - P:TABLE_COLS]))
                        with nc.allow_low_precision("zeros and ones"):
                            v.tensor_reduce(by_tile(mask), one_hot.rearrange("p t k e -> p t e k"),
                                            axis=mybir.AxisListType.X, op=ALU.add).then_inc(r_dve, 1)
                    elif r == "picks":
                        dve.wait_ge(r_pe, 1)
                        dve.wait_ge(r_dve, 2)
                        pos = by_tile(psXG[:])
                        link(v.tensor_tensor(picked, one_hot, pos.unsqueeze(2).broadcast_to((P, NT, TOPK, E)), ALU.mult))
                        link(v.tensor_reduce(pos_k[:], picked, axis=mybir.AxisListType.X, op=ALU.add))
                        link(v.tensor_scalar(valid[:], pos_k[:], float(CAP), None, ALU.is_lt))
                        link(v.tensor_scalar(pos_k[:], pos_k[:], float(CAP - 1), None, ALU.min))
                        link(v.scalar_tensor_tensor(pos_k[:], idx_f[:], float(CAP), pos_k[:], ALU.mult, ALU.add))
                        link(v.tensor_copy(slot_top[:], pos_k[:]))
                        link(v.reduce_sum(small[:, 3], top[:, :, 0:TOPK], mybir.AxisListType.X))
                        link(v.reciprocal(small[:, 1], small[:, 3]))
                        link(v.tensor_tensor(valid[:], valid[:], top[:, :, 0:TOPK], ALU.mult))
                        link(v.tensor_tensor(w_top[:], valid[:], small[:, 1].unsqueeze(2).broadcast_to((P, NT, TOPK)),
                                             ALU.mult))
                    elif r == "digits":
                        pos = by_tile(psXG[:])
                        link(v.scalar_tensor_tensor(posm, pos, 1.0, by_tile(mask), ALU.add, ALU.mult))
                        link(v.tensor_scalar(posm, posm, -1.0, None, ALU.add))
                        link(v.tensor_copy(pos_i, posm))
                        link(v.tensor_scalar(c1.bitcast(I32), pos_i, 3, None, ALU.arith_shift_right))
                        link(v.tensor_scalar(pos_i, pos_i, 7, None, ALU.bitwise_and))
                        link(v.tensor_copy(posm, c1.bitcast(I32)))
                        link(v.tensor_copy(c0, pos_i))
                    elif r == "high":
                        for c in range(S1):
                            last = v.tensor_scalar(digit1.rearrange("p t (e c) -> p t e c", c=S1)[:, :, :, c], posm, float(c),
                                                   None, ALU.is_equal)
                        last.then_inc(r_dve, 1)
                    elif r == "low":
                        for c in range(S1):
                            last = v.scalar_tensor_tensor(digit0.rearrange("p t (e c) -> p t e c", c=S1)[:, :, :, c], c0,
                                                          float(c), token_id.unsqueeze(2).broadcast_to((P, NT, E)),
                                                          ALU.is_equal, ALU.mult)
                        last.then_inc(r_dve, 1)
                    else:
                        dve.wait_ge(r_pe, 2)
                        for h in range(2):
                            src = (psXG if h == 0 else psXU)[:, 0:P].rearrange("p (e c) -> p c e", c=S1)
                            link(v.tensor_tensor(inv[:, h], src, own_half.unsqueeze(1).broadcast_to((P, S1, NT)), ALU.mult))
                        link(v.tensor_reduce(inv_f[:], inv[:], axis=mybir.AxisListType.X, op=ALU.add))
                        v.tensor_copy(inv_i[:], inv_f[:]).then_inc(r_dve, 1)

                def unit(g, s, kind, order):
                    u, x = UNITS * g + s, UNITS * g + s - FIRST_X
                    e0 = x * XPU
                    for what, r in order:
                        if isinstance(r, int):
                            q, e = chunk_no(u, r, g == NGROUPS - 1), e0 + r
                        if what == "mult":
                            dve.wait_ge(up_mm, q + 1)
                            dve.wait_ge(sil_done, q + 1)
                            if not (isinstance(q, int) and q == 0):
                                dve.wait_ge(gu_hi, q)
                                dve.wait_ge(gu_lo, q)
                            nc.vector.tensor_tensor(gu, sil[:], pair[r][1][:], ALU.mult).then_inc(gu_done, 1)
                        elif what == "gu_lo":
                            dve.wait_ge(gu_hi, q + 1)
                            nc.vector.tensor_tensor(guT[r][:, 1], gu, raw(guT[r][:, 0]), ALU.subtract).then_inc(gu_lo, 1)
                        elif what == "first_gu":
                            shared.gu_low(dve, r, r)
                        elif what == "first_down":
                            shared.down_low(dve, r, r)
                        elif what == "new_gu":
                            shared.gu_low(dve, GROUP * (g + 1) + r, r)
                        elif what == "new_down":
                            shared.down_low(dve, GROUP * g + r, r)
                        elif what == "down":
                            i = s * SUB + r
                            if r == 0:
                                dve.wait_ge(r_exp, 2)
                                if not (isinstance(u, int) and u == 0):
                                    dve.wait_ge(dn_evac, SUB * u)
                                nc.vector.tensor_copy(sig4[:], sig[:, bass.ds(s * SUB, SUB)]).then_inc(sig4_done, 1)
                                dve.wait_ge(sig4_done, u + 1)
                                if kind == "combine2":
                                    dve.wait_ge(cm_step, TOPK * (tile_no(kind, s, 1) + 1))
                            dve.wait_ge(dn_mm, SUB * u + r + 1)
                            if g == 0:
                                nc.vector.tensor_scalar(acc[:, i], down_bank[r][:], sig4[:, r:r + 1], None, ALU.mult)\
                                    .then_inc(dn_evac, 1)
                            else:
                                nc.vector.scalar_tensor_tensor(acc[:, i], down_bank[r][:], sig4[:, r:r + 1], acc[:, i],
                                                               ALU.mult, ALU.add).then_inc(dn_evac, 1)
                        elif what == "times_gb":
                            i = s * SUB + r
                            if r == 0:
                                dve.wait_ge(gb_in, 16)
                            dve.wait_ge(dn_evac, SUB * u + r + 1)
                            nc.vector.tensor_tensor(acc[:, i], acc[:, i], gb[:, s // 2, :], ALU.mult).then_inc(gb_mul, 1)
                        elif what == "add_x2":
                            i = s * SUB + r
                            if r == 0:
                                dve.wait_ge(x2u_in, 16 * UNITS)
                            dve.wait_ge(gb_mul, i + 1)
                            nc.vector.tensor_tensor(acc[:, i], acc[:, i], x2u[:, r], ALU.add).then_inc(last_add, 1)
                        elif what == "route":
                            route(r)
                        elif what in ("split_g", "split_u"):
                            i = 0 if what == "split_g" else 1
                            dve.wait_ge(wxg_hi, 2 * e + i + 1)
                            nc.vector.tensor_tensor(wx[i][:, 1, 0:KC * F], wx_raw[:, (3 * r + i) % RAW_SLOTS, 0:KC * F],
                                                    raw(wx[i][:, 0, 0:KC * F]), ALU.subtract).then_inc(wxg_lo, 1)
                        elif what == "split_d":
                            dve.wait_ge(wxd_hi, e + 1)
                            nc.vector.tensor_tensor(wx[2][:, 1], wx_raw[:, (3 * r + 2) % RAW_SLOTS], raw(wx[2][:, 0]),
                                                    ALU.subtract).then_inc(wxd_lo, 1)
                        elif what == "rows":
                            dve.wait_ge(rows_hi, 2 * x + r + 1)
                            v = xs[r][:].rearrange("p h c m -> p c h m")
                            nc.vector.tensor_tensor(v[:, :, :, CAP:P], psT[:].rearrange("p (c h m) -> p c h m", c=KC, h=2),
                                                    raw(v[:, :, :, 0:CAP]), ALU.subtract).then_inc(rows_lo, 1)
                        elif what == "sum":
                            dve.wait_ge(xlow, 2 * e + 2)
                            dve.wait_ge(xgu_done, 1 + e)
                            nc.vector.tensor_tensor(xg[:], psXG[0:CAP, 0:F], low_g[:], ALU.add).then_inc(xsum, 1)
                            nc.vector.tensor_tensor(xu[:], psXU[0:CAP, 0:F], low_u[:], ALU.add).then_inc(xadd, 1)
                        elif what == "xmul":
                            dve.wait_ge(xsil, e + 1)
                            dve.wait_ge(xadd, 1 + e + 1)
                            dve.wait_ge(mid_mm, 1 + e)
                            nc.vector.tensor_tensor(xgu[:, 0:F], xg[:], xu[:], ALU.mult).then_inc(xgu_done, 1)
                        elif what == "mid":
                            dve.wait_ge(mid_hi, e + 1)
                            nc.vector.tensor_tensor(xguT[:, :, CAP:P], psT[:, 0:FX * CAP].rearrange("p (c m) -> p c m", c=FX),
                                                    raw(xguT[:, :, 0:CAP]), ALU.subtract).then_inc(mid_lo, 1)
                        elif what == "exp_down":
                            dve.wait_ge(y_low, e + 1)
                            if not (isinstance(e, int) and e == 0):
                                dve.wait_ge(ye_out, 16 * e)
                            nc.vector.tensor_tensor(ye[:], psY[0:CAP, :], low_y[:], ALU.add).then_inc(ye_add, 1)
                        elif what == "combine":
                            i = tile_no(kind, s, r)
                            nc.vector.tensor_copy(w_now[:], w_top[:, i, :]).then_inc(w_copied, 1)
                            dve.wait_ge(w_copied, i + 1)
                            dve.wait_ge(dn_evac, SUB * u)
                            for k in range(TOPK):
                                if not (isinstance(i, int) and i + k == 0):
                                    dve.wait_ge(cm_step, TOPK * i + k)
                                dve.wait_ge(y_in[r % 2][k], 16 * tile_uses(kind, s, r))
                                nc.vector.scalar_tensor_tensor(acc[:, i], y_buf[r % 2][k], w_now[:, k:k + 1], acc[:, i],
                                                               ALU.mult, ALU.add).then_inc(cm_step, 1)

                run_units(dve, "dve", unit)

            @block.tensor
            def _(pe):
                for s_ in (rows_mm, xgu_mm, mid_mm, xd_mm):
                    pe.sem_inc(s_, 1)

                def halves(ap, cols):
                    return ap[:, 0, cols], ap[:, 1, cols]

                def unit(g, s, kind, order):
                    u, x = UNITS * g + s, UNITS * g + s - FIRST_X
                    e0, nch = x * XPU, chunks_of(g)
                    first = isinstance(u, int) and u == 0
                    for what, r in order:
                        if isinstance(r, int):
                            q, e = chunk_no(u, r, g == NGROUPS - 1), e0 + r
                        if what in ("gate", "up"):
                            which = 0 if what == "gate" else 1
                            if what == "gate":
                                pe.wait_ge(wgu_lo, GROUP * g + r + 1)
                                if r == 0:
                                    pe.wait_ge(hT_in, 16 * (u + 1))
                            if r == 0 and not first:
                                pe.wait_ge(dn_evac, SUB * u - 1 + which)
                            if r == 2:
                                pe.wait_ge(gu_done, q - 1)
                            shared.multiply(which, r)
                        elif what == "down":
                            if r == 0:
                                pe.wait_ge(wdn_lo, GROUP * g + nch)
                                pe.wait_ge(gu_lo, chunk_no(u, nch, g == NGROUPS - 1))
                            product(nc, down_bank[r], [(halves(guT[c], slice(r * P, (r + 1) * P)), halves(ws[c][:], down_w))
                                                      for c in range(nch)]).then_inc(dn_mm, 1)
                        elif what == "route" and r == "positions":
                            pe.wait_ge(r_dve, 2)
                            pe.wait_ge(r_consts, 2)
                            nc.tensor.matmul(psXG[:], before, mask, start=True, stop=False)
                            for t in range(NT - 1):
                                left = NT - 1 - t
                                last = nc.tensor.matmul(psXG[:, (t + 1) * E:NT * E], ones,
                                                        mask[:, t * E:(t + 1) * E].unsqueeze(1).broadcast_to((P, left, E)),
                                                        start=False, stop=t == NT - 2)
                            last.then_inc(r_pe, 1)
                        elif what == "route":
                            pe.wait_ge(r_dve, 4)
                            for h, ps in ((0, psXG), (1, psXU)):
                                for t in range(NT):
                                    last = nc.tensor.matmul(ps[:, 0:P], digit1[:, t, h * P:(h + 1) * P],
                                                            digit0[:, t, h * P:(h + 1) * P], start=t == 0, stop=t == NT - 1)
                            last.then_inc(r_pe, 1)
                        elif what == "rows":
                            pe.wait_ge(rows_in[r], 16 * (x + 1))
                            pe.wait_ge(mid_lo, 1 + e0 + 2 * r)
                            v = rows[r][:].rearrange("t (q c) -> t c q", c=KC)
                            for c in range(KC):
                                last = nc.tensor.transpose(psT[:, c * P:(c + 1) * P], v[:, c, :], ident[:])
                            last.then_inc(rows_mm, 1)
                        elif what == "gu":
                            pe.wait_ge(rows_lo, 1 + 2 * x + r // 2 + 1)
                            pe.wait_ge(wxg_lo, 2 + 2 * (e + 1))
                            pe.wait_ge(xadd, 1 + e)
                            for c in range(KC):
                                for ps, w in ((psXG, wx[0]), (psXU, wx[1])):
                                    for part in range(2):
                                        last = nc.tensor.matmul(ps[:, 0:F], xs[r // 2][:, r % 2, c, :],
                                                                w[:, part, c * F:(c + 1) * F],
                                                                start=c == 0 and part == 0, stop=c == KC - 1 and part == 1)
                            last.then_inc(xgu_mm, 1)
                        elif what == "mid":
                            pe.wait_ge(xgu_done, 1 + e + 1)
                            if r in (0, 2):
                                pe.wait_ge(rows_lo, 1 + 2 * x + r // 2 + 1)
                            else:
                                pe.wait_ge(mid_lo, 1 + e)
                            pe.sem_inc(waited_pe, 1)
                            for c in range(FX):
                                last = nc.tensor.transpose(psT[:, c * CAP:(c + 1) * CAP], xgu[:, c * P:(c + 1) * P],
                                                           ident[0:CAP, 0:CAP])
                            last.then_inc(mid_mm, 1)
                        elif what == "exp_down":
                            pe.wait_ge(mid_lo, 1 + e + 1)
                            pe.wait_ge(wxd_lo, 2 + e + 1)
                            pe.wait_ge(ye_add, 1 + e)
                            for c in range(FX):
                                k = min(P, F - c * P)
                                for part in range(2):
                                    last = nc.tensor.matmul(psY[:], xguT[0:k, c, :], wx[2][0:k, part, c * D:(c + 1) * D],
                                                            start=c == 0 and part == 0, stop=c == FX - 1 and part == 1)
                            last.then_inc(xd_mm, 1)

                run_units(pe, "pe", unit)


def adaln_block(nc, ins, out):
    scr = {
        "ye": nc.dram_tensor("ye_scratch", (E, CAP, D), F32).ap(),
        "slots": nc.dram_tensor("slots_scratch", (E * CAP,), I32).ap(),
        "gb": nc.dram_tensor("gb_scratch", (P, B, D), F32).ap(),
        "x2": nc.dram_tensor("x2_scratch", (B, TPB, P, D), F32).ap(),
        "h2": nc.dram_tensor("h2_scratch", (B, TPB, P, D), F32).ap(),
        "h2T": nc.dram_tensor("h2T_scratch", (B, TPB, P, 2 * D), F32).ap(),
    }
    with ExitStack() as ctx:
        both = {**ins, "logits": ctx.enter_context(nc.sbuf_tensor("logits", [P, NT, RW], F32)),
                "ident": ctx.enter_context(nc.sbuf_tensor("ident", [P, P], F32))}
        for e in ("pool", "dve", "sp", "pe"):
            both[f"waited_{e}"] = ctx.enter_context(nc.semaphore(f"waited_{e}"))
        both["area"] = ctx.enter_context(nc.sbuf_tensor("area", [P, 8 * KC * D], F32R))
        both["rows"] = ctx.enter_context(nc.sbuf_tensor("rows", [P, 4 * D], F32))
        both["psum"] = ctx.enter_context(nc.psum_tensor("psum", [P, 8, D], F32))
        both["shared"] = SharedFFN(nc, ins, scr, both["area"], both["rows"], both["psum"],
                                   lambda name: ctx.enter_context(nc.semaphore(name)))
        attention(nc, both, scr)
        ffn(nc, both, scr, out)


_OUTS = [((B, T, D), "float32")]


def _layout(inputs):
    import numpy as np
    a = {k: np.asarray(v) for k, v in inputs.items()}
    pos = np.arange(T, dtype=np.float32)
    inv = (1.0 / 10000.0 ** (np.arange(0, DK, 2, dtype=np.float32) / DK)).astype(np.float32)
    ang = (pos[:, None] * inv[None, :]).astype(np.float32)
    cos = np.repeat(np.cos(ang), 2, axis=1).astype(np.float32)
    sin = np.repeat(np.sin(ang), 2, axis=1).astype(np.float32)
    sin[:, 1::2] *= -1
    per_tile = lambda t: np.ascontiguousarray(t.reshape(TPB, P, DK).transpose(1, 0, 2))
    rows, cols = np.arange(P)[:, None] // DK, np.concatenate([np.arange(P) // DK, np.arange(HG)])[None]
    d = {
        "x": a["L0_attn_x"],
        "c": np.ascontiguousarray(a["L0_c"].reshape(B, P, KC).transpose(1, 2, 0)),
        "wmod": a["L0_wmod"],
        "cos": per_tile(cos), "sin": per_tile(sin), "mask": (rows == cols).astype(np.float32),
        "wr": np.concatenate([a["L0_ffn_Wr"], a["L0_ffn_Wse"], np.zeros((D, 1), np.float32)], axis=1),
    }
    gate_up = lambda w: w.reshape(P, KC, FCH, P).transpose(2, 0, 1, 3).reshape(FCH, P, D)
    d["ws"] = np.ascontiguousarray(np.concatenate(
        [gate_up(a["L0_ffn_Wsg"]), gate_up(a["L0_ffn_Wsu"]), a["L0_ffn_Wsd"].reshape(FCH, P, D)], axis=2))
    d["wg_x"], d["wu_x"], d["wd_x"] = a["L0_ffn_Wg"], a["L0_ffn_Wu"], a["L0_ffn_Wd"]
    const = lambda row: np.broadcast_to(np.asarray(row, np.float32), (P, len(row)))
    p = np.arange(P)[:, None]
    d["tables"] = np.ascontiguousarray(np.concatenate(
        [const(range(8)), const(range(E)), p + P * np.arange(NT)[None], p // 8 == np.arange(NT)[None],
         p < np.arange(P)[None]], axis=1).astype(np.float32))
    for n in "kvqgo":
        d[f"w{n}"] = np.ascontiguousarray(a[f"L0_attn_W{n}"].T)
        d[f"b{n}"] = a[f"L0_attn_b{n}"]
    return d


def kernel(**inputs):
    import numpy as _np
    import concourse.bacc as _bacc
    from concourse.bass_utils import run_bass_kernel_spmd as _run

    nc = _bacc.Bacc("TRN2", target_bir_lowering=False, num_devices=1)
    arrays, ins = {}, {}
    for name, a in _layout(inputs).items():
        arrays[f"in_{name}"] = a
        ins[name] = nc.dram_tensor(f"in_{name}", a.shape, mybir.dt.from_np(a.dtype), kind="ExternalInput").ap()
    shape, dtype = _OUTS[0]
    out = nc.dram_tensor("out_0", shape, mybir.dt.from_np(_np.dtype(dtype)), kind="ExternalOutput").ap()
    adaln_block(nc, ins, out)
    r = _run(nc, [arrays], core_ids=[0])
    return r.results[0]["out_0"]
```
